# Optimizing a Trainium2 kernel written in Bass

```python
import numpy as np
import jax
import jax.numpy as jnp

def _softmax(x, axis=-1):
    return jax.nn.softmax(x, axis=axis)

def _gelu(x):
    return jax.nn.gelu(x, approximate=True)

def _silu(x):
    return jax.nn.silu(x)

def _sigmoid(x):
    return jax.nn.sigmoid(x)

def _layernorm(x, axis=-1, eps=1e-05):
    m = jnp.mean(x, axis=axis, keepdims=True)
    v = jnp.var(x, axis=axis, keepdims=True)
    return (x - m) / jnp.sqrt(v + eps)

def _scatter_add(tgt, idx, src, axis=0):
    return tgt.at[idx].add(src)

def _segment_sum(src, seg, n):
    return jax.ops.segment_sum(src, seg, n)
kernel_name = 'mk_seq_preln_d1_jaxref_r8_508f17'

def setup_inputs(seed: int=0):
    np.random.seed(seed)
    _w = jnp.asarray

    def _L0_attn_setup():
        import jax, jax.numpy as jnp
        import numpy as np
        B, T, C, H = (2, 256, 128, 16)
        D = C // H

        def _alibi_slopes(n_heads):
            return 2.0 ** (-(8.0 / n_heads) * jnp.arange(1, n_heads + 1, dtype=jnp.float32))
        key = jax.random.key(seed)
        k1, k2, k3 = jax.random.split(key, 3)
        return {'x': jax.random.normal(k1, (B, T, C), dtype=jnp.float32), 'w_attn': jax.random.normal(k2, (C, 3 * C), dtype=jnp.float32) * 0.02, 'b_attn': jnp.zeros((3 * C,), dtype=jnp.float32), 'w_proj': jax.random.normal(k3, (C, C), dtype=jnp.float32) * 0.02, 'b_proj': jnp.zeros((C,), dtype=jnp.float32)}
    _L0_attn_in = _L0_attn_setup()

    def _L0_ffn_setup():
        import jax, jax.numpy as jnp
        import numpy as np
        DIM = 128
        DEPTH = 6
        HEADS = 16
        DIM_HEAD = 64
        WINDOW = 32
        INNER = HEADS * DIM_HEAD
        DIM_INNER = int(DIM * 4 * 2 / 3)
        QK_SCALE = 8.0

        def shift_tokens(t):
            a, s = jnp.split(t, 2, -1)
            s = jnp.pad(s, ((0, 0), (1, 0), (0, 0)))[:, :-1]
            return jnp.concatenate([a, s], -1)

        def l2norm(t):
            return t / jnp.maximum(jnp.linalg.norm(t, axis=-1, keepdims=True), 1e-12)

        def rotate_half(x):
            x1, x2 = jnp.split(x, 2, -1)
            return jnp.concatenate([-x2, x1], -1)

        def rotary_tables(n):
            half = jnp.arange(0, DIM_HEAD, 2, dtype=jnp.float32)
            inv_freq = 1.0 / 10000.0 ** (half / DIM_HEAD)
            t = jnp.arange(n, dtype=jnp.float32)
            freqs = t[:, None] * inv_freq[None, :]
            freqs = jnp.concatenate([freqs, freqs], -1)
            base_scale = (half + 0.4 * DIM_HEAD) / (1.4 * DIM_HEAD)
            power = (t - n // 2) / (WINDOW // 2)
            scale = base_scale[None, :] ** power[:, None]
            scale = jnp.concatenate([scale, scale], -1)
            return (freqs, scale)

        def local_attention(q, k, v):
            b, h, n, d = q.shape
            w = WINDOW
            nw = n // w
            bq = q.reshape(b, h, nw, w, d)
            bk = k.reshape(b, h, nw, w, d)
            bv = v.reshape(b, h, nw, w, d)

            def look(t):
                p = jnp.pad(t, ((0, 0), (0, 0), (1, 0), (0, 0), (0, 0)))
                return jnp.concatenate([p[:, :, :nw], p[:, :, 1:]], axis=3)
            bk2, bv2 = (look(bk), look(bv))
            seq = jnp.arange(n).reshape(nw, w)
            seq_p = jnp.pad(seq, ((1, 0), (0, 0)), constant_values=-1)
            jt = jnp.concatenate([seq_p[:nw], seq_p[1:]], axis=1)
            it = seq[:, :, None]
            jb = jt[:, None, :]
            mask = (it < jb) | (it > jb + w) | (jb == -1)
            sim = jnp.einsum('bhwie,bhwje->bhwij', bq, bk2) * QK_SCALE
            sim = jnp.where(mask, -jnp.finfo(sim.dtype).max, sim)
            attn = jax.nn.softmax(sim, -1)
            out = jnp.einsum('bhwij,bhwje->bhwie', attn, bv2)
            return out.reshape(b, h, n, d)

        def attn_layer(x, Wqkv, qs, ksc, Wo):
            b, n, _ = x.shape
            qkv = x @ Wqkv
            q, k, v = jnp.split(qkv, 3, -1)
            sh = lambda t: t.reshape(b, n, HEADS, DIM_HEAD).transpose(0, 2, 1, 3)
            q, k, v = (sh(q), sh(k), sh(v))
            q = l2norm(q) * qs
            k = l2norm(k) * ksc
            freqs, scale = rotary_tables(n)
            cos, sin = (jnp.cos(freqs), jnp.sin(freqs))
            q = q * cos * scale + rotate_half(q) * sin * scale
            inv = 1.0 / scale
            k = k * cos * inv + rotate_half(k) * sin * inv
            out = local_attention(q, k, v)
            out = out.transpose(0, 2, 1, 3).reshape(b, n, INNER)
            return out @ Wo

        def ffn_layer(x, g, bln, W1, b1, W2, b2):
            mu = x.mean(-1, keepdims=True)
            var = ((x - mu) ** 2).mean(-1, keepdims=True)
            xn = (x - mu) / jnp.sqrt(var + 1e-05) * g + bln
            hg = xn @ W1 + b1
            a, gate = jnp.split(hg, 2, -1)
            return a * jax.nn.gelu(gate, approximate=False) @ W2 + b2
        key = jax.random.key(seed)
        ks = jax.random.split(key, 8)
        B, N = (2, 256)
        init = lambda k, shape: jax.random.normal(k, shape, jnp.float32) * 0.02
        return {'x': jax.random.normal(ks[0], (B, N, DIM), jnp.float32), 'Wqkv': init(ks[1], (DEPTH, DIM, 3 * INNER)), 'q_scale': jnp.ones((DEPTH, DIM_HEAD), jnp.float32), 'k_scale': jnp.ones((DEPTH, DIM_HEAD), jnp.float32), 'Wo': init(ks[2], (DEPTH, INNER, DIM)), 'ln_g': jnp.ones((DEPTH, DIM), jnp.float32), 'ln_b': jnp.zeros((DEPTH, DIM), jnp.float32), 'W1': init(ks[3], (DEPTH, DIM, 2 * DIM_INNER)), 'b1': jnp.zeros((DEPTH, 2 * DIM_INNER), jnp.float32), 'W2': init(ks[4], (DEPTH, DIM_INNER, DIM)), 'b2': jnp.zeros((DEPTH, DIM), jnp.float32)}
    _L0_ffn_in = _L0_ffn_setup()
    _d = {'L0_attn_x': _L0_attn_in['x'], 'L0_attn_w_attn': _L0_attn_in['w_attn'], 'L0_attn_b_attn': _L0_attn_in['b_attn'], 'L0_attn_w_proj': _L0_attn_in['w_proj'], 'L0_attn_b_proj': _L0_attn_in['b_proj'], 'L0_ffn_Wqkv': _L0_ffn_in['Wqkv'], 'L0_ffn_q_scale': _L0_ffn_in['q_scale'], 'L0_ffn_k_scale': _L0_ffn_in['k_scale'], 'L0_ffn_Wo': _L0_ffn_in['Wo'], 'L0_ffn_ln_g': _L0_ffn_in['ln_g'], 'L0_ffn_ln_b': _L0_ffn_in['ln_b'], 'L0_ffn_W1': _L0_ffn_in['W1'], 'L0_ffn_b1': _L0_ffn_in['b1'], 'L0_ffn_W2': _L0_ffn_in['W2'], 'L0_ffn_b2': _L0_ffn_in['b2']}
    _x0 = _d['L0_attn_x']
    _d['L0_attn_x'] = jax.random.normal(jax.random.fold_in(jax.random.key(seed), 1), (8, 256, 128), dtype=_x0.dtype)
    del _x0
    return _d

def reference(L0_attn_x, L0_attn_w_attn, L0_attn_b_attn, L0_attn_w_proj, L0_attn_b_proj, L0_ffn_Wqkv, L0_ffn_q_scale, L0_ffn_k_scale, L0_ffn_Wo, L0_ffn_ln_g, L0_ffn_ln_b, L0_ffn_W1, L0_ffn_b1, L0_ffn_W2, L0_ffn_b2):

    def _L0_attn_ref(x, w_attn, b_attn, w_proj, b_proj):
        import jax, jax.numpy as jnp
        import numpy as np
        B, T, C, H = (2, 256, 128, 16)
        D = C // H

        def _alibi_slopes(n_heads):
            return 2.0 ** (-(8.0 / n_heads) * jnp.arange(1, n_heads + 1, dtype=jnp.float32))
        b, t, c = x.shape
        qkv = (x @ w_attn + b_attn).reshape(b, t, 3, H, D).transpose(2, 0, 3, 1, 4)
        q, k, v = (qkv[0], qkv[1], qkv[2])
        scores = jnp.einsum('bhtd,bhsd->bhts', q, k) / jnp.sqrt(jnp.float32(D))
        slopes = _alibi_slopes(H)
        pos = jnp.arange(t, dtype=scores.dtype)
        scores = scores + slopes[None, :, None, None] * pos[None, None, None, :]
        causal = jnp.tril(jnp.ones((t, t), dtype=bool))
        scores = jnp.where(causal[None, None], scores, -jnp.inf)
        attn = jax.nn.softmax(scores, axis=-1)
        y = jnp.einsum('bhts,bhsd->bhtd', attn, v)
        y = y.transpose(0, 2, 1, 3).reshape(b, t, c)
        return y @ w_proj + b_proj

    def _L0_ffn_ref(x, Wqkv, q_scale, k_scale, Wo, ln_g, ln_b, W1, b1, W2, b2):
        import jax, jax.numpy as jnp
        import numpy as np
        DIM = 128
        DEPTH = 6
        HEADS = 16
        DIM_HEAD = 64
        WINDOW = 32
        INNER = HEADS * DIM_HEAD
        DIM_INNER = int(DIM * 4 * 2 / 3)
        QK_SCALE = 8.0

        def shift_tokens(t):
            a, s = jnp.split(t, 2, -1)
            s = jnp.pad(s, ((0, 0), (1, 0), (0, 0)))[:, :-1]
            return jnp.concatenate([a, s], -1)

        def l2norm(t):
            return t / jnp.maximum(jnp.linalg.norm(t, axis=-1, keepdims=True), 1e-12)

        def rotate_half(x):
            x1, x2 = jnp.split(x, 2, -1)
            return jnp.concatenate([-x2, x1], -1)

        def rotary_tables(n):
            half = jnp.arange(0, DIM_HEAD, 2, dtype=jnp.float32)
            inv_freq = 1.0 / 10000.0 ** (half / DIM_HEAD)
            t = jnp.arange(n, dtype=jnp.float32)
            freqs = t[:, None] * inv_freq[None, :]
            freqs = jnp.concatenate([freqs, freqs], -1)
            base_scale = (half + 0.4 * DIM_HEAD) / (1.4 * DIM_HEAD)
            power = (t - n // 2) / (WINDOW // 2)
            scale = base_scale[None, :] ** power[:, None]
            scale = jnp.concatenate([scale, scale], -1)
            return (freqs, scale)

        def local_attention(q, k, v):
            b, h, n, d = q.shape
            w = WINDOW
            nw = n // w
            bq = q.reshape(b, h, nw, w, d)
            bk = k.reshape(b, h, nw, w, d)
            bv = v.reshape(b, h, nw, w, d)

            def look(t):
                p = jnp.pad(t, ((0, 0), (0, 0), (1, 0), (0, 0), (0, 0)))
                return jnp.concatenate([p[:, :, :nw], p[:, :, 1:]], axis=3)
            bk2, bv2 = (look(bk), look(bv))
            seq = jnp.arange(n).reshape(nw, w)
            seq_p = jnp.pad(seq, ((1, 0), (0, 0)), constant_values=-1)
            jt = jnp.concatenate([seq_p[:nw], seq_p[1:]], axis=1)
            it = seq[:, :, None]
            jb = jt[:, None, :]
            mask = (it < jb) | (it > jb + w) | (jb == -1)
            sim = jnp.einsum('bhwie,bhwje->bhwij', bq, bk2) * QK_SCALE
            sim = jnp.where(mask, -jnp.finfo(sim.dtype).max, sim)
            attn = jax.nn.softmax(sim, -1)
            out = jnp.einsum('bhwij,bhwje->bhwie', attn, bv2)
            return out.reshape(b, h, n, d)

        def attn_layer(x, Wqkv, qs, ksc, Wo):
            b, n, _ = x.shape
            qkv = x @ Wqkv
            q, k, v = jnp.split(qkv, 3, -1)
            sh = lambda t: t.reshape(b, n, HEADS, DIM_HEAD).transpose(0, 2, 1, 3)
            q, k, v = (sh(q), sh(k), sh(v))
            q = l2norm(q) * qs
            k = l2norm(k) * ksc
            freqs, scale = rotary_tables(n)
            cos, sin = (jnp.cos(freqs), jnp.sin(freqs))
            q = q * cos * scale + rotate_half(q) * sin * scale
            inv = 1.0 / scale
            k = k * cos * inv + rotate_half(k) * sin * inv
            out = local_attention(q, k, v)
            out = out.transpose(0, 2, 1, 3).reshape(b, n, INNER)
            return out @ Wo

        def ffn_layer(x, g, bln, W1, b1, W2, b2):
            mu = x.mean(-1, keepdims=True)
            var = ((x - mu) ** 2).mean(-1, keepdims=True)
            xn = (x - mu) / jnp.sqrt(var + 1e-05) * g + bln
            hg = xn @ W1 + b1
            a, gate = jnp.split(hg, 2, -1)
            return a * jax.nn.gelu(gate, approximate=False) @ W2 + b2
        for i in range(DEPTH):
            x = attn_layer(shift_tokens(x), Wqkv[i], q_scale[i], k_scale[i], Wo[i]) + x
            x = ffn_layer(shift_tokens(x), ln_g[i], ln_b[i], W1[i], b1[i], W2[i], b2[i]) + x
        return x
    x = L0_attn_x
    x = x + _L0_attn_ref(_layernorm(x, axis=-1), L0_attn_w_attn, L0_attn_b_attn, L0_attn_w_proj, L0_attn_b_proj)
    x = x + _L0_ffn_ref(_layernorm(x, axis=-1), L0_ffn_Wqkv, L0_ffn_q_scale, L0_ffn_k_scale, L0_ffn_Wo, L0_ffn_ln_g, L0_ffn_ln_b, L0_ffn_W1, L0_ffn_b1, L0_ffn_W2, L0_ffn_b2)
    return x

_drawn_inputs = setup_inputs


def setup_inputs(seed=0):
    import zlib

    import numpy as np

    out = dict(_drawn_inputs(seed))
    spreads = {'L0_attn_b_attn': (0.0, 0.378),
     'L0_attn_b_proj': (0.0, 0.1),
     'L0_ffn_q_scale': (1.0, 0.6),
     'L0_ffn_k_scale': (1.0, 0.6),
     'L0_ffn_ln_g': (1.0, 0.6),
     'L0_ffn_ln_b': (0.0, 0.8),
     'L0_ffn_b1': (0.0, 0.8),
     'L0_ffn_b2': (0.0, 0.1)}
    factors = {'L0_attn_w_attn': 3.74, 'L0_ffn_W1': 3.644, 'L0_ffn_W2': 3.563}
    for name, (base, spread) in spreads.items():
        noise = np.random.default_rng([zlib.crc32(name.encode()), seed]).standard_normal(out[name].shape)
        drawn = base * np.exp(spread * noise) if base else spread * noise
        out[name] = jnp.asarray(drawn.astype(out[name].dtype))
    for name, factor in factors.items():
        out[name] = (out[name] * factor).astype(out[name].dtype)
    return out
```

```python
from contextlib import ExitStack

import concourse.bass as bass
from concourse import mybir

F32 = mybir.dt.float32
BF16 = mybir.dt.bfloat16
ALU = mybir.AluOpType
ACT = mybir.ActivationFunctionType
AX_X = mybir.AxisListType.X

P = 128
C = 128
B = 8
T = 256
TT = T // P
LN_EPS = 1e-5
NEG = -1e30

H0 = 16
D0 = C // H0
HG = 4
KEYS = P + T

L = 6
H = 16
D = 64
PAIRS = H // 2
INNER = H * D
WIN = 32
NW = T // WIN
QK_SCALE = 8.0
DI = int(C * 4 * 2 / 3)
PIECES = [(0, 128), (128, 128), (256, DI - 256)]
UNITS = L * B


class Signal:

    def __init__(self, sem, per=1):
        self.sem, self.per = sem, per

    def at(self, u, i=0):
        return self.per * u + (i + 1)

    def before(self, u, i=0):
        return self.per * u + i


def build(nc, x, w_attn, b_attn_cols, b_v_rows, w_proj, b_proj_rows, wqkv, q_scale_rows, k_scale_rows, wo,
          ln_cols, w1, b1_cols, w2, b2_cols, rope, ident, win_mask, causal, alibi, ones3, head_pick, out):
    with ExitStack() as ctx:
        def sb(name, shape, dt=F32):
            return ctx.enter_context(nc.sbuf_tensor(name, shape, dt))

        def signal(name, per=1):
            return Signal(ctx.enter_context(nc.semaphore(name)), per)

        ps = ctx.enter_context(nc.psum_tensor("ps", [P, 8, 512], F32))

        x1 = sb("x1", [P, B * TT, C])
        xT = sb("xT", [P, B * T])
        ident_s = sb("ident_s", [P, P])
        ident_b = sb("ident_b", [P, P], BF16)
        mean_w = sb("mean_w", [P, P])
        rope_s = sb("rope_s", [P, 4, TT, D])
        rope_l = sb("rope_l", [P, L * 4 * TT * D])
        scale_s = sb("scale_s", [P, 2, L, D])
        ln_s = sb("ln_s", [P, 2, L])
        b1_s = sb("b1_s", [P, L * 6])
        b2_s = sb("b2_s", [P, L])
        cur = sb("cur", [P, 2, 9])
        minus_half = sb("minus_half", [P, H])
        wmask_s = sb("wmask_s", [P, 2, 2 * WIN])
        wmask = sb("wmask", [P, 2, PAIRS, 2 * WIN], BF16)
        wqkv_s = sb("wqkv_s", [P, 3 * INNER])
        wo_s = sb("wo_s", [P, PAIRS, C])
        w1_s = sb("w1_s", [P, 2 * DI])
        w2_s = sb("w2_s", [P, 3, C])

        consts_in = signal("consts_in")
        x_in = signal("x_in")
        qkvw_in = signal("qkvw_in", 16)
        ffw_in = signal("ffw_in", 64)
        setup_done = signal("setup_done")
        pool_setup = signal("pool_setup")
        x0_ready = signal("x0_ready")

        def in_register(eng, value):
            return value if isinstance(value, int) else eng.snap(value)

        with ExitStack() as ctx0:
            def sb0(name, shape, dt=F32):
                return ctx0.enter_context(nc.sbuf_tensor(name, shape, dt))

            wa = sb0("wa", [P, 3 * C])
            wp = sb0("wp", [P, C])
            bqk = sb0("bqk", [P, 2])
            bqm = sb0("bqm", [P, HG])
            pick = sb0("pick", [P, HG])
            bv = sb0("bv", [P, C])
            bp = sb0("bp", [P, C])
            causal_s = sb0("causal_s", [P, KEYS])
            causal_b = sb0("causal_b", [P, KEYS], BF16)
            alibi_s = sb0("alibi_s", [P, HG, KEYS])
            alibi_b = sb0("alibi_b", [P, HG, KEYS], BF16)
            ones3_s = sb0("ones3_s", [P, P])
            ones3_b = sb0("ones3_b", [P, P], BF16)
            stats = sb0("stats", [P, TT, 6])
            mv = sb0("mv", [P, TT, 2])
            var0 = sb0("var0", [P, TT])
            rstd0 = sb0("rstd0", [P, TT])
            xn = sb0("xn", [P, TT, C])
            xnT = sb0("xnT", [P, T])
            kT0 = sb0("kT0", [P, T])
            qm = sb0("qm", [P, HG, T])
            vm = sb0("vm", [P, TT, HG, HG, HG, D0])
            nmax = sb0("nmax", [P, H0, TT])
            rsum = sb0("rsum", [P, TT, H0])
            rinv = sb0("rinv", [P, TT, H0])
            rexp = sb0("rexp", [P, TT, H0, D0])
            p0 = sb0("p0", [P, 2, KEYS])
            pT0 = sb0("pT0", [P, 2, KEYS])
            rT = sb0("rT", [P, T])
            oT0 = sb0("oT0", [P, T])
            ybuf = sb0("ybuf", [P, TT, C])

            const_loads = [
                (wa[:, :], w_attn), (wp[:, :], w_proj), (bqk[:, :], b_attn_cols), (pick[:, :], head_pick),
                (bv[:, :], b_v_rows), (bp[:, :], b_proj_rows), (causal_s[:, :], causal), (alibi_s[:, :, :], alibi),
                (ones3_s[:, :], ones3), (ident_s[:, :], ident), (rope_s[:, :, :, :], rope),
                (scale_s[:, 0, :, :], q_scale_rows), (scale_s[:, 1, :, :], k_scale_rows), (ln_s[:, :, :], ln_cols),
                (b1_s[:, :], b1_cols), (b2_s[:, :], b2_cols), (wmask_s[:, :, :], win_mask),
            ]

            dve_set = signal("dve_set")
            stats_d = signal("stats_d", 2)
            aggr_d = signal("aggr_d", 2)
            var_d = signal("var_d", 2)
            rstd_g = signal("rstd_g", 2)
            xn_d = signal("xn_d", 2)
            xnT_p = signal("xnT_p", 2)
            xnT_a = signal("xnT_a")
            qk_p = signal("qk_p")
            kq_a = signal("kq_a")
            v_p = signal("v_p")
            v_d = signal("v_d")
            s_p = signal("s_p", H0)
            max_d = signal("max_d", H0)
            exp_a = signal("exp_a", H0)
            pT_p = signal("pT_p", H0)
            pT_d = signal("pT_d", H0)
            pv_p = signal("pv_p", H0)
            rinv_d = signal("rinv_d")
            rexp_d = signal("rexp_d")
            rT_p = signal("rT_p")
            rT_a = signal("rT_a")
            oT_d = signal("oT_d")
            y_p = signal("y_p")
            yb_d = signal("yb_d")
            x1_d = signal("x1_d")

            BANK_T, BANK_V, BANK_S, BANK_PT, BANK_O, BANK_QK = 0, 1, 2, 4, 6, 7
            qm_rows = [slice(32 * r, 32 * r + 32) for r in range(HG)]

            with nc.Block() as block:
                @block.sync
                def _(sp):
                    sp.dma_start(x1[:, :, :], x.rearrange("b (t p) c -> p (b t) c", p=P)).then_inc(x_in.sem, 16)
                    for dst, src in const_loads:
                        sp.dma_start(dst, src).then_inc(consts_in.sem, 16)
                    sp.dma_start(wqkv_s[:, :], wqkv[0, :, :]).then_inc(qkvw_in.sem, 16)
                    sp.dma_start(wo_s[:, :, :], wo[0, :, :, :]).then_inc(ffw_in.sem, 16)
                    sp.dma_start(w1_s[:, :], w1[0, :, :]).then_inc(ffw_in.sem, 16)
                    sp.dma_start(w2_s[:, :, :], w2[0, :, :, :]).then_inc(ffw_in.sem, 16)

                @block.gpsimd
                def _(pool):
                    nc.gpsimd.memset(vm[:, :, :, :, :, :], 0.0)
                    nc.gpsimd.memset(minus_half[:, :], -0.5).then_inc(pool_setup.sem, 1)
                    pool.wait_ge(pool_setup.sem, 1)
                    with pool.Fori(0, B) as b:
                        for n in range(2):
                            pool.wait_ge(var_d.sem, var_d.at(b, n))
                            nc.gpsimd.tensor_tensor(rstd0[:, :], var0[:, :], minus_half[:, 0:TT], ALU.pow).then_inc(rstd_g.sem, 1)

                @block.vector
                def _(dve):
                    V = nc.vector
                    V.memset(mean_w[:, :], 1.0 / C)
                    dve.wait_ge(consts_in.sem, 16 * len(const_loads))
                    V.tensor_copy(ident_b[:, :], ident_s[:, :])
                    V.tensor_copy(causal_b[:, :], causal_s[:, :])
                    V.tensor_copy(alibi_b[:, :, :], alibi_s[:, :, :])
                    V.tensor_copy(ones3_b[:, :], ones3_s[:, :])
                    V.tensor_scalar(bqm[:, :], pick[:, :], bqk[:, 0:1], None, ALU.mult)
                    for m in range(2):
                        V.tensor_copy(wmask[:, m, :, :], wmask_s[:, m, None, :].broadcast_to([P, PAIRS, 2 * WIN]))
                    for layer in range(L):
                        for k in range(4):
                            dst = rope_l[:, (layer * 4 + k) * TT * D:(layer * 4 + k + 1) * TT * D]
                            dst = dst.rearrange("p (t s e) -> p t s e", t=TT, s=2)
                            src = rope_s[:, k, :, :].rearrange("p t (s e) -> p t s e", s=2)
                            sc = scale_s[:, k // 2, layer, :].rearrange("p (s e) -> p s e", s=2)
                            for half in range(2):
                                other = half if k % 2 == 0 else 1 - half
                                last = V.tensor_tensor(dst[:, :, half, :], src[:, :, half, :],
                                                       sc[:, other, None, :].broadcast_to([P, TT, D // 2]), ALU.mult)
                    last.then_inc(setup_done.sem, 1)
                    dve.wait_ge(x_in.sem, 16)
                    dve.wait_ge(pool_setup.sem, 1)

                    def layernorm(b, n):
                        for t in range(TT):
                            last = V.bn_stats(stats[:, t, :], x1[:, bass.ds(b * TT + t, 1), :].rearrange("p o c -> p (o c)"))
                        last.then_inc(stats_d.sem, 1)
                        dve.wait_ge(stats_d.sem, stats_d.at(b, n))
                        V.memset(var0[:, :], LN_EPS)
                        for t in range(TT):
                            last = V.bn_aggr(mv[:, t, :], stats[:, t, :])
                        last.then_inc(aggr_d.sem, 1)
                        value = in_register(dve, aggr_d.at(b, n))
                        dve.wait_ge(setup_done.sem, 1)
                        dve.wait_ge(aggr_d.sem, value)
                        V.tensor_tensor(var0[:, :], mv[:, :, 1], var0[:, :], ALU.add).then_inc(var_d.sem, 1)
                        dve.wait_ge(rstd_g.sem, rstd_g.at(b, n))
                        for t in range(TT):
                            last = V.tensor_scalar(xn[:, t, :], x1[:, bass.ds(b * TT + t, 1), :].rearrange("p o c -> p (o c)"),
                                                   mv[:, t, 0:1], rstd0[:, t:t + 1], ALU.subtract, ALU.mult)
                        last.then_inc(xn_d.sem, 1)

                    def evac_pT(b, h):
                        dve.wait_ge(pT_p.sem, pT_p.at(b, h))
                        if h >= 2:
                            dve.wait_ge(pv_p.sem, pv_p.at(b, h - 2))
                        V.tensor_copy(pT0[:, h % 2, :], ps[:, BANK_PT + h % 2, 0:KEYS]).then_inc(pT_d.sem, 1)

                    with dve.Fori(0, B) as b:
                        layernorm(b, 0)
                        dve.wait_ge(v_p.sem, v_p.at(b))
                        for j in range(HG):
                            for t in range(TT):
                                src = ps[:, BANK_V, t * C:(t + 1) * C].rearrange("p (r j d) -> p r j d", r=HG, j=HG)
                                bias = bv[:, :].rearrange("p (r j d) -> p r j d", r=HG, j=HG)
                                last = V.tensor_tensor(vm[:, t, j, :, j, :], src[:, :, j, :], bias[:, :, j, :], ALU.add)
                        last.then_inc(v_d.sem, 1)
                        for h in range(H0):
                            dve.wait_ge(s_p.sem, s_p.at(b, h))
                            s = ps[:, BANK_S + h % 2, :]
                            V.tensor_reduce(nmax[:, h, 0:1], s[:, 0:P], AX_X, ALU.max, negate=True)
                            V.tensor_reduce(nmax[:, h, 1:2], s[:, P:KEYS], AX_X, ALU.max, negate=True).then_inc(max_d.sem, 1)
                            if h >= 1:
                                evac_pT(b, h - 1)
                        evac_pT(b, H0 - 1)
                        V.reciprocal(rinv[:, :, :], rsum[:, :, :]).then_inc(rinv_d.sem, 1)
                        dve.wait_ge(rinv_d.sem, rinv_d.at(b))
                        V.tensor_copy(rexp[:, :, :, :], rinv[:, :, :, None].broadcast_to([P, TT, H0, D0])).then_inc(rexp_d.sem, 1)
                        dve.wait_ge(rT_a.sem, rT_a.at(b))
                        dve.wait_ge(pv_p.sem, pv_p.at(b, H0 - 1))
                        V.tensor_tensor(oT0[:, :], ps[:, BANK_O, 0:T], rT[:, :], ALU.mult).then_inc(oT_d.sem, 1)
                        dve.wait_ge(y_p.sem, y_p.at(b))
                        V.tensor_tensor(ybuf[:, :, :], ps[:, BANK_T, 0:T].rearrange("p (t c) -> p t c", t=TT),
                                        bp[:, None, :].broadcast_to([P, TT, C]), ALU.add).then_inc(yb_d.sem, 1)
                        dve.wait_ge(yb_d.sem, yb_d.at(b))
                        xb = x1[:, bass.ds(b * TT, TT), :]
                        V.tensor_tensor(xb, ybuf[:, :, :], xb, ALU.add).then_inc(x1_d.sem, 1)
                        value = in_register(dve, x1_d.at(b))
                        dve.wait_ge(setup_done.sem, 1)
                        dve.wait_ge(x1_d.sem, value)
                        layernorm(b, 1)
                        dve.wait_ge(xnT_p.sem, xnT_p.at(b, 1))

                @block.scalar
                def _(act):
                    S = nc.scalar
                    act.wait_ge(setup_done.sem, 1)
                    with act.Fori(0, B) as b:
                        act.wait_ge(xnT_p.sem, xnT_p.at(b, 0))
                        S.activation(xnT[:, :], ps[:, BANK_T, 0:T], ACT.Copy).then_inc(xnT_a.sem, 1)
                        act.wait_ge(qk_p.sem, qk_p.at(b))
                        S.activation(kT0[:, :], ps[:, BANK_QK, T:2 * T], ACT.Identity, bias=bqk[:, 1:2])
                        for j in range(HG):
                            last = S.activation(qm[:, j, :], ps[:, BANK_QK, 0:T], ACT.Identity,
                                                bias=bqm[:, j:j + 1], scale=pick[:, j:j + 1])
                        last.then_inc(kq_a.sem, 1)
                        for h in range(H0):
                            act.wait_ge(max_d.sem, max_d.at(b, h))
                            if h >= 2:
                                act.wait_ge(pT_p.sem, pT_p.at(b, h - 2))
                            s = ps[:, BANK_S + h % 2, :]
                            S.activation(p0[:, h % 2, 0:P], s[:, 0:P], ACT.Exp, bias=nmax[:, h, 0:1],
                                         accum_out=rsum[:, 0, h:h + 1])
                            S.activation(p0[:, h % 2, P:KEYS], s[:, P:KEYS], ACT.Exp, bias=nmax[:, h, 1:2],
                                         accum_out=rsum[:, 1, h:h + 1]).then_inc(exp_a.sem, 1)
                        act.wait_ge(rT_p.sem, rT_p.at(b))
                        S.activation(rT[:, :], ps[:, BANK_V, 0:T], ACT.Copy).then_inc(rT_a.sem, 1)
                        act.wait_ge(xnT_p.sem, xnT_p.at(b, 1))
                        S.activation(xT[:, bass.ds(b * T, T)], ps[:, BANK_T, 0:T], ACT.Copy).then_inc(x0_ready.sem, 1)

                @block.tensor
                def _(pe):
                    M = nc.tensor
                    pe.wait_ge(setup_done.sem, 1)

                    def scores(b, h):
                        r, j = h // HG, h % HG
                        rows = qm_rows[r]
                        s = ps[:, BANK_S + h % 2, :]
                        if h >= 2:
                            pe.wait_ge(exp_a.sem, exp_a.at(b, h - 2))
                        M.matmul(s[:, 0:KEYS], ident_b[:, :], causal_b[:, :], start=True, stop=False)
                        M.matmul(s[:, 0:KEYS], ones3_b[rows, :], alibi_b[rows, j, :], start=False, stop=False)
                        M.matmul(s[:, 0:P], qm[rows, j, 0:P], kT0[rows, 0:P], start=False, stop=False)
                        M.matmul(s[:, P:KEYS], qm[rows, j, P:T], kT0[rows, :], start=False, stop=True).then_inc(s_p.sem, 1)

                    def transpose_p(b, h):
                        pe.wait_ge(exp_a.sem, exp_a.at(b, h))
                        if h >= 2:
                            pe.wait_ge(pT_d.sem, pT_d.at(b, h - 2))
                        for c in range(KEYS // P):
                            last = M.transpose(ps[:, BANK_PT + h % 2, c * P:(c + 1) * P], p0[:, h % 2, c * P:(c + 1) * P], ident_s[:, :])
                        last.then_inc(pT_p.sem, 1)

                    def values(b, h):
                        r, j = h // HG, h % HG
                        o = ps[32 * r:32 * r + 32, BANK_O, :]
                        pe.wait_ge(pT_d.sem, pT_d.at(b, h))
                        cols = [vm[:, t, j, r, :, :].rearrange("p j d -> p (j d)") for t in range(TT)]
                        M.matmul(o[:, 0:T], cols[0], pT0[:, h % 2, 0:T], start=j == 0, stop=False)
                        M.matmul(o[:, P:T], cols[1], pT0[:, h % 2, T:KEYS], start=False, stop=j == HG - 1).then_inc(pv_p.sem, 1)

                    with pe.Fori(0, B) as b:
                        pe.wait_ge(xn_d.sem, xn_d.at(b, 0))
                        for t in range(TT):
                            last = M.transpose(ps[:, BANK_T, t * P:(t + 1) * P], xn[:, t, :], ident_s[:, :])
                        last.then_inc(xnT_p.sem, 1)
                        pe.wait_ge(xnT_a.sem, xnT_a.at(b))
                        for k in range(2):
                            last = M.matmul(ps[:, BANK_QK, k * T:(k + 1) * T], wa[:, k * C:(k + 1) * C], xnT[:, :], start=True, stop=True)
                        last.then_inc(qk_p.sem, 1)
                        for t in range(TT):
                            last = M.matmul(ps[:, BANK_V, t * C:(t + 1) * C], xnT[:, t * P:(t + 1) * P], wa[:, 2 * C:3 * C], start=True, stop=True)
                        last.then_inc(v_p.sem, 1)
                        pe.wait_ge(kq_a.sem, kq_a.at(b))
                        pe.wait_ge(v_d.sem, v_d.at(b))
                        for i in range(H0 + 2):
                            if i < H0:
                                scores(b, i)
                            if 1 <= i <= H0:
                                transpose_p(b, i - 1)
                            if i >= 2:
                                values(b, i - 2)
                        pe.wait_ge(rexp_d.sem, rexp_d.at(b))
                        for t in range(TT):
                            last = M.transpose(ps[:, BANK_V, t * P:(t + 1) * P], rexp[:, t, :, :].rearrange("p h d -> p (h d)"), ident_s[:, :])
                        last.then_inc(rT_p.sem, 1)
                        pe.wait_ge(oT_d.sem, oT_d.at(b))
                        for t in range(TT):
                            last = M.matmul(ps[:, BANK_T, t * C:(t + 1) * C], oT0[:, t * P:(t + 1) * P], wp[:, :], start=True, stop=True)
                        last.then_inc(y_p.sem, 1)
                        pe.wait_ge(xn_d.sem, xn_d.at(b, 1))
                        for t in range(TT):
                            last = M.transpose(ps[:, BANK_T, t * P:(t + 1) * P], xn[:, t, :], ident_s[:, :])
                        last.then_inc(xnT_p.sem, 1)
                        pe.wait_ge(x0_ready.sem, x0_ready.at(b))

        xs = sb("xs", [P, 2, T])
        raw = sb("raw", [P, 2, INNER])
        sq = sb("sq", [P, INNER])
        rot1 = sb("rot1", [P, 2, INNER])
        rot2 = sb("rot2", [P, 2, INNER])
        ssum = sb("ssum", [P, 2, H])
        rnorm = sb("rnorm", [P, 2, H])
        qT = sb("qT", [P, 2, PAIRS, T])
        kT = sb("kT", [P, 2, PAIRS, WIN + T])
        vn = sb("vn", [P, TT, 2, PAIRS * D])
        vk = sb("vk", [P, 2, NW, PAIRS * D])
        smax = sb("smax", [P, 2, H])
        prob = sb("prob", [P, 2, H * 2 * WIN])
        lsum = sb("lsum", [P, 2, H])
        linv = sb("linv", [P, 2, H])
        pT = sb("pT", [P, PAIRS, P])
        on = sb("on", [P, INNER])
        oT = sb("oT", [P, PAIRS, T])
        xf = sb("xf", [P, T])
        xc = sb("xc", [P, T])
        xq = sb("xq", [P, T])
        vtok = sb("vtok", [P, TT])
        rtok = sb("rtok", [P, TT])
        rwide = sb("rwide", [P, TT, P])
        xg = sb("xg", [P, T])
        gate = sb("gate", [P, T])
        hid = sb("hid", [P, 3, T])
        xlast = sb("xlast", [P, T])
        outb = sb("outb", [P, TT, C])

        PJ, SO, TP, FB = 0, (2, 4), 6, 7

        zeroed = signal("zeroed")
        xs_d = signal("xs_d")
        proj_p = signal("proj_p", 6)
        raw_a = signal("raw_a", 6)
        sq_a = signal("sq_a", 4)
        ss_d = signal("ss_d", 4)
        cl_d = signal("cl_d", 4)
        rn_g = signal("rn_g", 4)
        nrm_d = signal("nrm_d", 4)
        cos_d = signal("cos_d", 4)
        sin_g = signal("sin_g", 4)
        rope_d = signal("rope_d", 4)
        qkT_p = signal("qkT_p", 8)
        qkT_a = signal("qkT_a", 8)
        VK_DMAS = (14, 16)
        vk_in = [[signal(f"vk_in{par}{t}", 16 * VK_DMAS[t]) for t in range(TT)] for par in range(2)]
        sc_p = signal("sc_p", 2)
        mx_d = signal("mx_d", 2)
        sub_d = signal("sub_d", 2)
        ex_a = signal("ex_a", 2)
        ls_d = signal("ls_d", 2)
        li_d = signal("li_d", 2)
        ptp = signal("ptp", 2)
        pta = signal("pta", 2)
        av_p = signal("av_p", 2)
        on_d = signal("on_d", 2)
        otp = signal("otp", 2)
        ota = signal("ota", 2)
        wo_p = signal("wo_p")
        x2_d = signal("x2_d")
        xf_d = signal("xf_d")
        cur_d = signal("cur_d")
        mean_p = signal("mean_p")
        xc_d = signal("xc_d")
        xq_a = signal("xq_a")
        var_p = signal("var_p")
        vr_d = signal("vr_d")
        rr_g = signal("rr_g")
        rx_d = signal("rx_d")
        rt_p = signal("rt_p")
        xg_d = signal("xg_d")
        xh_d = signal("xh_d")
        w1_p = signal("w1_p", 3)
        gelu_a = signal("gelu_a", 3)
        hid_d = signal("hid_d", 3)
        w2_p = signal("w2_p")
        fin_d = signal("fin_d")
        xl_d = signal("xl_d")
        xl_p = signal("xl_p")
        res_d = signal("res_d")
        out_done = signal("out_done", 16)

        def index(u):
            return u[0] * 2 + u[1]

        def schedule(eng, project, feed, body):
            project((0, 0))
            body((0, 0), False, True)
            with eng.Fori(0, (UNITS - 2) // 2) as m:
                body((m, 1), True, True)
                body((m, 2), True, True)
            body((0, UNITS - 1), True, False)
            feed((0, UNITS - 1))

        with nc.Block() as block:
            @block.sync
            def _(sp):
                def copy_v(u):
                    n, par = index(u), u[1] % 2
                    for t in range(TT):
                        if t == 0 and not (isinstance(n, int) and n < 2):
                            value = in_register(sp, av_p.before(n - 1, 0))
                            sp.wait_ge(setup_done.sem, 1)
                            sp.wait_ge(av_p.sem, value)
                        value = in_register(sp, raw_a.at(n, 3 * t + 2))
                        sp.wait_ge(setup_done.sem, 1)
                        sp.wait_ge(raw_a.sem, value)
                        for hp in range(2):
                            for k in range(4):
                                w = 4 * t + k
                                src = vn[32 * k:32 * k + 32, t, hp, :]
                                lo = 64 * hp
                                sp.dma_start(vk[lo + 32:lo + 64, par, w, :], src).then_inc(vk_in[par][t].sem, 16)
                                if w + 1 < NW:
                                    tt = (w + 1) // 4
                                    sp.dma_start(vk[lo:lo + 32, par, w + 1, :], src).then_inc(vk_in[par][tt].sem, 16)

                def load_qkv(layer):
                    sp.wait_ge(proj_p.sem, proj_p.before(layer * B, 0))
                    sp.dma_start(wqkv_s[:, :], wqkv[bass.ds(layer, 1), :, :].rearrange("o p n -> p (o n)")).then_inc(qkvw_in.sem, 16)

                def load_ffw(layer):
                    sp.wait_ge(w2_p.sem, w2_p.before(layer * B, 0))
                    sp.dma_start(wo_s[:, :, :], wo[bass.ds(layer, 1), :, :, :].rearrange("o p k n -> p (o k) n")).then_inc(ffw_in.sem, 16)
                    sp.dma_start(w1_s[:, :], w1[bass.ds(layer, 1), :, :].rearrange("o p n -> p (o n)")).then_inc(ffw_in.sem, 16)
                    sp.dma_start(w2_s[:, :, :], w2[bass.ds(layer, 1), :, :, :].rearrange("o p k n -> p (o k) n")).then_inc(ffw_in.sem, 16)

                sp.wait_ge(zeroed.sem, 1)
                copy_v((0, 0))
                copy_v((0, 1))
                with sp.Fori(0, L - 1) as layer:
                    with sp.Fori(0, 3) as i:
                        m = layer * 4 + i
                        copy_v((m, 2))
                        copy_v((m, 3))
                    load_qkv(layer + 1)
                    copy_v((layer * 4, 8))
                    copy_v((layer * 4, 9))
                    load_ffw(layer + 1)
                with sp.Fori(0, 3) as i:
                    copy_v((i, UNITS - 6))
                    copy_v((i, UNITS - 5))
                with sp.Fori(0, B) as b:
                    sp.wait_ge(res_d.sem, res_d.at(b))
                    sp.dma_start(out[bass.ds(b, 1), :, :].rearrange("o (t p) c -> p (o t) c", p=P), outb[:, :, :]).then_inc(out_done.sem, 16)
                sp.wait_ge(out_done.sem, 16 * B)

            @block.gpsimd
            def _(pool):
                G = nc.gpsimd
                pool.wait_ge(x0_ready.sem, B)
                G.memset(xs[:, :, :], 0.0)
                G.memset(xf[:, :], 0.0)
                for par in range(2):
                    G.memset(kT[:, par, :, 0:WIN], 0.0)
                    last = G.memset(vk[:, par, 0, :], 0.0)
                last.then_inc(zeroed.sem, 1)

                def norms(u, t, kind):
                    n, i = index(u), 2 * t + kind
                    pool.wait_ge(cl_d.sem, cl_d.at(n, i))
                    G.tensor_tensor(rnorm[:, kind, :], ssum[:, kind, :], minus_half[:, :], ALU.pow).then_inc(rn_g.sem, 1)

                def feed_rstd(u):
                    n = index(u)
                    pool.wait_ge(vr_d.sem, vr_d.at(n))
                    G.tensor_tensor(rtok[:, :], vtok[:, :], minus_half[:, 0:TT], ALU.pow).then_inc(rr_g.sem, 1)

                def sin_term(u, t, kind):
                    n = index(u)
                    i = 2 * t + kind
                    pool.wait_ge(nrm_d.sem, nrm_d.at(n, i))
                    if t > 0 or not (isinstance(n, int) and n < 1):
                        pool.wait_ge(rope_d.sem, rope_d.before(n, i - 1))
                    base = (n // B) * (4 * TT * D) + (2 * kind + 1) * TT * D + t * D
                    tab = rope_l[:, bass.ds(base, D)].rearrange("p (s e) -> p s e", s=2)
                    src = raw[:, kind, :].rearrange("p (h s e) -> p h s e", h=H, s=2)
                    dst = rot2[:, kind, :].rearrange("p (h s e) -> p h s e", h=H, s=2)
                    for half in range(2):
                        last = G.tensor_tensor(dst[:, :, half, :], src[:, :, 1 - half, :],
                                               tab[:, half, None, :].broadcast_to([P, H, D // 2]), ALU.mult)
                    last.then_inc(sin_g.sem, 1)

                def project(u):
                    for t in range(TT):
                        norms(u, t, 0)
                        norms(u, t, 1)
                        sin_term(u, t, 0)
                        sin_term(u, t, 1)

                def body(u, feeds, projects):
                    v, f = (u[0], u[1] + 1), (u[0], u[1] - 1)
                    if projects:
                        norms(v, 0, 0)
                        norms(v, 0, 1)
                        sin_term(v, 0, 0)
                        sin_term(v, 0, 1)
                    if feeds:
                        feed_rstd(f)
                    if projects:
                        norms(v, 1, 0)
                        norms(v, 1, 1)
                        sin_term(v, 1, 0)
                        sin_term(v, 1, 1)

                schedule(pool, project, feed_rstd, body)

            @block.vector
            def _(dve):
                V = nc.vector
                dve.wait_ge(x0_ready.sem, B)
                dve.wait_ge(zeroed.sem, 1)
                dve.sem_inc(fin_d.sem, 1)

                def seq(u):
                    return bass.ds((index(u) % B) * T, T)

                def shift_in(u):
                    n, par = index(u), u[1] % 2
                    if not (isinstance(n, int) and n < 2):
                        dve.wait_ge(fin_d.sem, n - 1)
                        value = in_register(dve, proj_p.before(n - 1, 0))
                        dve.wait_ge(setup_done.sem, 1)
                        dve.wait_ge(proj_p.sem, value)
                    b = index(u) % B
                    V.tensor_copy(xs[0:64, par, :], xT[0:64, bass.ds(b * T, T)])
                    V.tensor_copy(xs[64:P, par, 1:T], xT[64:P, bass.ds(b * T, T - 1)]).then_inc(xs_d.sem, 1)

                def sums(u, t, kind):
                    n, i = index(u), 2 * t + kind
                    dve.wait_ge(sq_a.sem, sq_a.at(n, i))
                    V.tensor_reduce(ssum[:, kind, :], sq[:, :].rearrange("p (h e) -> p h e", h=H), AX_X, ALU.add).then_inc(ss_d.sem, 1)
                    dve.wait_ge(ss_d.sem, ss_d.at(n, i))
                    V.tensor_scalar(ssum[:, kind, :], ssum[:, kind, :], 1e-24, None, ALU.max).then_inc(cl_d.sem, 1)

                def normalise(u, t, kind):
                    n, i = index(u), 2 * t + kind
                    dve.wait_ge(rn_g.sem, rn_g.at(n, i))
                    v = raw[:, kind, :].rearrange("p (h e) -> p h e", h=H)
                    V.tensor_tensor(v, v, rnorm[:, kind, :, None].broadcast_to([P, H, D]), ALU.mult).then_inc(nrm_d.sem, 1)

                def cos_term(u, t, kind):
                    n, i = index(u), 2 * t + kind
                    dve.wait_ge(nrm_d.sem, nrm_d.at(n, i))
                    if t > 0 or not (isinstance(n, int) and n < 1):
                        dve.wait_ge(qkT_p.sem, qkT_p.before(n, 4 * t + 2 * kind - 2))
                    base = (n // B) * (4 * TT * D) + 2 * kind * TT * D + t * D
                    tab = rope_l[:, bass.ds(base, D)]
                    V.tensor_tensor(rot1[:, kind, :].rearrange("p (h e) -> p h e", h=H),
                                    raw[:, kind, :].rearrange("p (h e) -> p h e", h=H),
                                    tab[:, None, :].broadcast_to([P, H, D]), ALU.mult).then_inc(cos_d.sem, 1)

                def rotate(u, t, kind):
                    n, i = index(u), 2 * t + kind
                    dve.wait_ge(cos_d.sem, cos_d.at(n, i))
                    dve.wait_ge(sin_g.sem, sin_g.at(n, i))
                    V.tensor_tensor(rot1[:, kind, :], rot1[:, kind, :], rot2[:, kind, :], ALU.add).then_inc(rope_d.sem, 1)

                def tile_scores(t):
                    return ps[:, SO[t]:SO[t] + 2, :].rearrange("p s (a k) -> p s a k", a=PAIRS)

                def soft_max(u, t):
                    n = index(u)
                    dve.wait_ge(sc_p.sem, sc_p.at(n, t))
                    V.tensor_reduce(smax[:, t, :], tile_scores(t), AX_X, ALU.max).then_inc(mx_d.sem, 1)
                    dve.wait_ge(mx_d.sem, mx_d.at(n, t))
                    if not (isinstance(n, int) and n < 1):
                        dve.wait_ge(ptp.sem, ptp.at(n - 1, t))
                    m = smax[:, t, :].rearrange("p (s a) -> p s a", s=2)
                    V.tensor_tensor(prob[:, t, :].rearrange("p (a s k) -> p s a k", a=PAIRS, s=2), tile_scores(t),
                                    m[:, :, :, None].broadcast_to([P, 2, PAIRS, 2 * WIN]), ALU.subtract).then_inc(sub_d.sem, 1)

                def soft_sum(u, t):
                    n = index(u)
                    dve.wait_ge(ex_a.sem, ex_a.at(n, t))
                    V.tensor_reduce(lsum[:, t, :], prob[:, t, :].rearrange("p (h k) -> p h k", h=H), AX_X, ALU.add).then_inc(ls_d.sem, 1)
                    dve.wait_ge(ls_d.sem, ls_d.at(n, t))
                    V.reciprocal(linv[:, t, :], lsum[:, t, :]).then_inc(li_d.sem, 1)

                def normalise_o(u, t):
                    n = index(u)
                    dve.wait_ge(li_d.sem, li_d.at(n, t))
                    dve.wait_ge(av_p.sem, av_p.at(n, t))
                    if t > 0 or not (isinstance(n, int) and n < 1):
                        dve.wait_ge(otp.sem, otp.before(n, t))
                    li = linv[:, t, :].rearrange("p (a s) -> p s a", s=2)
                    V.tensor_tensor(on[:, :].rearrange("p (a s e) -> p s a e", a=PAIRS, s=2), tile_scores(t),
                                    li[:, :, :, None].broadcast_to([P, 2, PAIRS, D]), ALU.mult).then_inc(on_d.sem, 1)

                def feed_1(u):
                    n = index(u)
                    layer = n // B
                    dve.wait_ge(wo_p.sem, wo_p.at(n))
                    V.tensor_tensor(xT[:, seq(u)], ps[:, FB, 0:T], xT[:, seq(u)], ALU.add).then_inc(x2_d.sem, 1)
                    value = in_register(dve, x2_d.at(n))
                    dve.wait_ge(setup_done.sem, 1)
                    dve.wait_ge(x2_d.sem, value)
                    b = n % B
                    V.tensor_copy(xf[0:64, :], xT[0:64, bass.ds(b * T, T)])
                    V.tensor_copy(xf[64:P, 1:T], xT[64:P, bass.ds(b * T, T - 1)]).then_inc(xf_d.sem, 1)
                    V.tensor_copy(cur[:, 0, 0:2], ln_s[:, :, bass.ds(layer, 1)].rearrange("p a o -> p (a o)"))
                    V.tensor_copy(cur[:, 0, 2:8], b1_s[:, bass.ds(layer * 6, 6)])
                    V.tensor_copy(cur[:, 0, 8:9], b2_s[:, bass.ds(layer, 1)]).then_inc(cur_d.sem, 1)

                def feed_2(u):
                    n = index(u)
                    dve.wait_ge(mean_p.sem, mean_p.at(n))
                    V.tensor_tensor(xc[:, :], xf[:, :], ps[:, FB, 0:T], ALU.subtract).then_inc(xc_d.sem, 1)

                def feed_3(u):
                    n = index(u)
                    dve.wait_ge(var_p.sem, var_p.at(n))
                    V.tensor_scalar(vtok[:, :], ps[:, FB, T:T + TT], LN_EPS, None, ALU.add).then_inc(vr_d.sem, 1)

                def feed_spread(u):
                    n = index(u)
                    dve.wait_ge(rr_g.sem, rr_g.at(n))
                    V.tensor_copy(rwide[:, :, :], rtok[:, :, None].broadcast_to([P, TT, P])).then_inc(rx_d.sem, 1)

                def feed_norm(u):
                    n = index(u)
                    dve.wait_ge(rt_p.sem, rt_p.at(n))
                    V.tensor_tensor(xg[:, :], xc[:, :], ps[:, FB, 0:T], ALU.mult).then_inc(xg_d.sem, 1)
                    dve.wait_ge(xg_d.sem, xg_d.at(n))
                    V.tensor_scalar(xg[:, :], xg[:, :], cur[:, 0, 0:1], cur[:, 0, 1:2], ALU.mult, ALU.add).then_inc(xh_d.sem, 1)

                def feed_hidden(u, i):
                    n, rows = index(u), PIECES[i][1]
                    dve.wait_ge(gelu_a.sem, gelu_a.at(n, i))
                    V.scalar_tensor_tensor(hid[0:rows, i, :], ps[0:rows, FB, 0:T], cur[0:rows, 0, 2 + i:3 + i],
                                           gate[0:rows, :], ALU.add, ALU.mult).then_inc(hid_d.sem, 1)

                def feed_4(u):
                    n = index(u)
                    dve.wait_ge(w2_p.sem, w2_p.at(n))
                    V.scalar_tensor_tensor(xT[:, seq(u)], ps[:, FB, 0:T], cur[:, 0, 8:9], xT[:, seq(u)],
                                           ALU.add, ALU.add).then_inc(fin_d.sem, 1)

                def project(u):
                    shift_in(u)
                    for t in range(TT):
                        for kind in range(2):
                            sums(u, t, kind)
                        for kind in range(2):
                            normalise(u, t, kind)
                            cos_term(u, t, kind)
                        for kind in range(2):
                            rotate(u, t, kind)

                def feed(u):
                    feed_1(u)
                    feed_2(u)
                    feed_3(u)
                    feed_spread(u)
                    feed_norm(u)
                    for i in range(3):
                        feed_hidden(u, i)
                    feed_4(u)

                def body(u, feeds, projects):
                    v, f = (u[0], u[1] + 1), (u[0], u[1] - 1)
                    if projects:
                        shift_in(v)
                    soft_max(u, 0)
                    if projects:
                        sums(v, 0, 0)
                    if feeds:
                        feed_1(f)
                    if projects:
                        sums(v, 0, 1)
                    soft_sum(u, 0)
                    if projects:
                        normalise(v, 0, 0)
                        cos_term(v, 0, 0)
                    if feeds:
                        feed_2(f)
                    if projects:
                        normalise(v, 0, 1)
                        cos_term(v, 0, 1)
                        rotate(v, 0, 0)
                    soft_max(u, 1)
                    if projects:
                        rotate(v, 0, 1)
                    if feeds:
                        feed_3(f)
                    normalise_o(u, 0)
                    if feeds:
                        feed_spread(f)
                    if projects:
                        sums(v, 1, 0)
                        sums(v, 1, 1)
                    if feeds:
                        feed_norm(f)
                    soft_sum(u, 1)
                    if projects:
                        normalise(v, 1, 0)
                        cos_term(v, 1, 0)
                    if feeds:
                        feed_hidden(f, 0)
                    if projects:
                        normalise(v, 1, 1)
                        cos_term(v, 1, 1)
                    if feeds:
                        feed_hidden(f, 1)
                    if projects:
                        rotate(v, 1, 0)
                    normalise_o(u, 1)
                    if projects:
                        rotate(v, 1, 1)
                    if feeds:
                        feed_hidden(f, 2)
                        feed_4(f)

                schedule(dve, project, feed, body)

                with dve.Fori(0, B) as b:
                    dve.wait_ge(fin_d.sem, UNITS + 1)
                    V.tensor_copy(xlast[:, :], xT[:, bass.ds(b * T, T)]).then_inc(xl_d.sem, 1)
                    dve.wait_ge(xl_p.sem, xl_p.at(b))
                    V.tensor_tensor(outb[:, :, :], ps[:, PJ, 0:T].rearrange("p (t c) -> p t c", t=TT),
                                    x1[:, bass.ds(b * TT, TT), :], ALU.add).then_inc(res_d.sem, 1)
                    dve.wait_ge(out_done.sem, out_done.per * (b + 1))

            @block.scalar
            def _(act):
                S = nc.scalar
                act.wait_ge(x0_ready.sem, B)

                def copy_raw(u, t, kind):
                    n, i = index(u), 2 * t + kind
                    act.wait_ge(proj_p.sem, proj_p.at(n, 3 * t + kind))
                    if t > 0 or not (isinstance(n, int) and n < 1):
                        act.wait_ge(cos_d.sem, cos_d.before(n, i - 1))
                        act.wait_ge(sin_g.sem, sin_g.before(n, i - 1))
                    S.activation(raw[:, kind, :], ps[:, PJ:PJ + 2, :].rearrange("p a n -> p (a n)"), ACT.Copy).then_inc(raw_a.sem, 1)
                    act.wait_ge(raw_a.sem, raw_a.at(n, 3 * t + kind))
                    if i > 0 or not (isinstance(n, int) and n < 1):
                        act.wait_ge(ss_d.sem, ss_d.before(n, i))
                    S.activation(sq[:, :], raw[:, kind, :], ACT.Square).then_inc(sq_a.sem, 1)

                def copy_v(u, t):
                    n, par = index(u), u[1] % 2
                    act.wait_ge(proj_p.sem, proj_p.at(n, 3 * t + 2))
                    if not (isinstance(n, int) and n < 1):
                        before = (u[0], u[1] - 1)
                        m, c = before[0], before[1] // 2
                        for tt in range(TT):
                            sig = vk_in[1 - par][tt]
                            act.wait_ge(sig.sem, sig.at(m + c, sig.per - 1))
                    S.activation(vn[:, t, :, :].rearrange("p s n -> p (s n)"), ps[:, PJ:PJ + 2, :].rearrange("p a n -> p (a n)"),
                                 ACT.Copy).then_inc(raw_a.sem, 1)

                def copy_qkT(u, t, kind, half):
                    n, par = index(u), u[1] % 2
                    i = 4 * t + 2 * kind + half
                    act.wait_ge(qkT_p.sem, qkT_p.at(n, i))
                    src = ps[:, TP, :].rearrange("p (a n) -> p a n", a=4)
                    if kind == 0:
                        dst = qT[:, par, 4 * half:4 * half + 4, t * P:(t + 1) * P]
                    else:
                        dst = kT[:, par, 4 * half:4 * half + 4, WIN + t * P:WIN + (t + 1) * P]
                    S.activation(dst, src, ACT.Copy).then_inc(qkT_a.sem, 1)

                def exps(u, t):
                    n = index(u)
                    act.wait_ge(sub_d.sem, sub_d.at(n, t))
                    S.activation(prob[:, t, :], prob[:, t, :], ACT.Exp, scale=QK_SCALE).then_inc(ex_a.sem, 1)

                def copy_pT(u, t):
                    n = index(u)
                    act.wait_ge(ptp.sem, ptp.at(n, t))
                    if t > 0 or not (isinstance(n, int) and n < 1):
                        act.wait_ge(av_p.sem, av_p.before(n, t))
                    S.activation(pT[:, :, :].rearrange("p a q -> p (a q)"), ps[:, SO[t]:SO[t] + 2, :].rearrange("p a n -> p (a n)"),
                                 ACT.Copy).then_inc(pta.sem, 1)

                def copy_oT(u, t):
                    n = index(u)
                    act.wait_ge(otp.sem, otp.at(n, t))
                    if t == 0 and not (isinstance(n, int) and n < 1):
                        act.wait_ge(wo_p.sem, wo_p.at(n - 1))
                    S.activation(oT[:, :, t * P:(t + 1) * P], ps[:, SO[t]:SO[t] + 2, :].rearrange("p s (a q) -> p (s a) q", a=4),
                                 ACT.Copy).then_inc(ota.sem, 1)

                def square_x(u):
                    n = index(u)
                    act.wait_ge(xc_d.sem, xc_d.at(n))
                    S.activation(xq[:, :], xc[:, :], ACT.Square).then_inc(xq_a.sem, 1)

                def gelu(u, i):
                    n, rows = index(u), PIECES[i][1]
                    act.wait_ge(w1_p.sem, w1_p.at(n, i))
                    if i > 0:
                        act.wait_ge(hid_d.sem, hid_d.at(n, i - 1))
                    S.activation(gate[0:rows, :], ps[0:rows, FB, T:2 * T], ACT.Gelu, bias=cur[0:rows, 0, 5 + i:6 + i]).then_inc(gelu_a.sem, 1)

                def project(u):
                    for t in range(TT):
                        copy_raw(u, t, 0)
                        copy_raw(u, t, 1)
                        copy_v(u, t)
                        for kind in range(2):
                            for half in range(2):
                                copy_qkT(u, t, kind, half)

                def feed(u):
                    square_x(u)
                    for i in range(3):
                        gelu(u, i)

                def body(u, feeds, projects):
                    v, f = (u[0], u[1] + 1), (u[0], u[1] - 1)
                    if projects:
                        copy_raw(v, 0, 0)
                    exps(u, 0)
                    if projects:
                        copy_raw(v, 0, 1)
                    copy_pT(u, 0)
                    if feeds:
                        square_x(f)
                    if projects:
                        copy_qkT(v, 0, 0, 0)
                        copy_qkT(v, 0, 0, 1)
                        copy_v(v, 0)
                    exps(u, 1)
                    copy_oT(u, 0)
                    if projects:
                        copy_qkT(v, 0, 1, 0)
                        copy_qkT(v, 0, 1, 1)
                        copy_raw(v, 1, 0)
                    copy_pT(u, 1)
                    if projects:
                        copy_raw(v, 1, 1)
                    if feeds:
                        gelu(f, 0)
                        gelu(f, 1)
                        gelu(f, 2)
                    if projects:
                        copy_v(v, 1)
                        copy_qkT(v, 1, 0, 0)
                        copy_qkT(v, 1, 0, 1)
                    copy_oT(u, 1)
                    if projects:
                        copy_qkT(v, 1, 1, 0)
                        copy_qkT(v, 1, 1, 1)

                schedule(act, project, feed, body)

            @block.tensor
            def _(pe):
                M = nc.tensor
                pe.wait_ge(x0_ready.sem, B)
                pe.wait_ge(zeroed.sem, 1)

                def proj(u, t, kind):
                    n, par = index(u), u[1] % 2
                    i = 3 * t + kind
                    if i == 0:
                        pe.wait_ge(xs_d.sem, xs_d.at(n))
                        pe.wait_ge(qkvw_in.sem, 16 * (n // B) + 16)
                    pe.wait_ge(raw_a.sem, raw_a.before(n, i))
                    w = wqkv_s[:, kind * INNER:(kind + 1) * INNER]
                    for half in range(2):
                        if kind < 2:
                            rhs = w[:, half * 512:(half + 1) * 512]
                        else:
                            rhs = w.rearrange("p (a s e) -> p s a e", a=PAIRS, s=2)[:, half, :, :]
                        last = M.matmul(ps[:, PJ + half, :], xs[:, par, t * P:(t + 1) * P], rhs, start=True, stop=True)
                    last.then_inc(proj_p.sem, 1)

                def transpose_qk(u, t, kind, half):
                    n = index(u)
                    i = 4 * t + 2 * kind + half
                    pe.wait_ge(rope_d.sem, rope_d.at(n, 2 * t + kind))
                    pe.wait_ge(qkT_a.sem, qkT_a.before(n, i))
                    for a in range(4):
                        c = 4 * half + a
                        last = M.transpose(ps[:, TP, a * P:(a + 1) * P], rot1[:, kind, c * P:(c + 1) * P], ident_s[:, :])
                    last.then_inc(qkT_p.sem, 1)

                def scores(u, t, hp):
                    n, par = index(u), u[1] % 2
                    if hp == 0:
                        pe.wait_ge(qkT_a.sem, qkT_a.at(n, 4 * t + 3))
                        if not (isinstance(n, int) and n < 1):
                            pe.wait_ge(ota.sem, ota.at(n - 1, t))
                    bank = SO[t] + hp
                    M.matmul(ps[:, bank, :], ident_b[:, :], wmask[:, 0 if t == 0 else 1, :, :].rearrange("p a k -> p (a k)"),
                             start=True, stop=False)
                    rows = slice(64 * hp, 64 * hp + 64)
                    for a in range(PAIRS):
                        for k in range(4):
                            w = 4 * t + k
                            last = M.matmul(ps[32 * k:32 * k + 32, bank, a * 64:(a + 1) * 64],
                                            qT[rows, par, a, 32 * w:32 * w + 32], kT[rows, par, a, 32 * w:32 * w + 64],
                                            start=False, stop=a == PAIRS - 1)
                    if hp == 1:
                        last.then_inc(sc_p.sem, 1)

                def transpose_p(u, t):
                    n = index(u)
                    sig = vk_in[u[1] % 2][t]
                    pe.wait_ge(sig.sem, sig.at(u[0] + u[1] // 2, sig.per - 1))
                    pe.wait_ge(ex_a.sem, ex_a.at(n, t))
                    for a in range(PAIRS):
                        last = M.transpose(ps[:, SO[t] + a // 4, (a % 4) * P:(a % 4 + 1) * P], prob[:, t, a * P:(a + 1) * P], ident_s[:, :])
                    last.then_inc(ptp.sem, 1)

                def values(u, t, hp):
                    n, par = index(u), u[1] % 2
                    if hp == 0:
                        value = in_register(pe, pta.at(n, t))
                        pe.wait_ge(setup_done.sem, 1)
                        pe.wait_ge(pta.sem, value)
                    rows = slice(64 * hp, 64 * hp + 64)
                    for a in range(PAIRS):
                        for k in range(4):
                            last = M.matmul(ps[32 * k:32 * k + 32, SO[t] + hp, a * D:(a + 1) * D],
                                            pT[rows, a, 32 * k:32 * k + 32], vk[rows, par, 4 * t + k, a * D:(a + 1) * D],
                                            start=True, stop=True)
                    if hp == 1:
                        last.then_inc(av_p.sem, 1)

                def transpose_o(u, t):
                    n = index(u)
                    pe.wait_ge(on_d.sem, on_d.at(n, t))
                    for a in range(PAIRS):
                        last = M.transpose(ps[:, SO[t] + a // 4, (a % 4) * P:(a % 4 + 1) * P], on[:, a * P:(a + 1) * P], ident_s[:, :])
                    last.then_inc(otp.sem, 1)

                def feed_wo(u):
                    n = index(u)
                    pe.wait_ge(ffw_in.sem, 48 * (n // B) + 48)
                    pe.wait_ge(ota.sem, ota.at(n, 1))
                    pe.wait_ge(fin_d.sem, fin_d.at(n))
                    for a in range(PAIRS):
                        last = M.matmul(ps[:, FB, 0:T], wo_s[:, a, :], oT[:, a, :], start=a == 0, stop=a == PAIRS - 1)
                    last.then_inc(wo_p.sem, 1)

                def feed_mean(u):
                    n = index(u)
                    pe.wait_ge(xf_d.sem, xf_d.at(n))
                    M.matmul(ps[:, FB, 0:T], mean_w[:, :], xf[:, :], start=True, stop=True).then_inc(mean_p.sem, 1)

                def feed_var(u):
                    n = index(u)
                    pe.wait_ge(xq_a.sem, xq_a.at(n))
                    for t in range(TT):
                        last = M.matmul(ps[:, FB, T + t:T + t + 1], xq[:, t * P:(t + 1) * P], mean_w[:, 0:1], start=True, stop=True)
                    last.then_inc(var_p.sem, 1)

                def feed_rstd(u):
                    n = index(u)
                    pe.wait_ge(rx_d.sem, rx_d.at(n))
                    for t in range(TT):
                        last = M.transpose(ps[:, FB, t * P:(t + 1) * P], rwide[:, t, :], ident_s[:, :])
                    last.then_inc(rt_p.sem, 1)

                def feed_w1(u, i):
                    n = index(u)
                    at, rows = PIECES[i]
                    if i == 0:
                        pe.wait_ge(xh_d.sem, xh_d.at(n))
                    else:
                        pe.wait_ge(hid_d.sem, hid_d.at(n, i - 1))
                    for g in range(2):
                        last = M.matmul(ps[0:rows, FB, g * T:(g + 1) * T], w1_s[:, g * DI + at:g * DI + at + rows], xg[:, :],
                                        start=True, stop=True)
                    last.then_inc(w1_p.sem, 1)

                def feed_w2(u):
                    n = index(u)
                    pe.wait_ge(hid_d.sem, hid_d.at(n, 2))
                    for i, (_, rows) in enumerate(PIECES):
                        last = M.matmul(ps[:, FB, 0:T], w2_s[0:rows, i, :], hid[0:rows, i, :], start=i == 0, stop=i == 2)
                    last.then_inc(w2_p.sem, 1)

                def project(u):
                    for t in range(TT):
                        for kind in range(3):
                            proj(u, t, kind)
                        for kind in range(2):
                            for half in range(2):
                                transpose_qk(u, t, kind, half)

                def feed(u):
                    feed_wo(u)
                    feed_mean(u)
                    feed_var(u)
                    feed_rstd(u)
                    for i in range(3):
                        feed_w1(u, i)
                    feed_w2(u)

                def body(u, feeds, projects):
                    v, f = (u[0], u[1] + 1), (u[0], u[1] - 1)
                    scores(u, 0, 0)
                    scores(u, 0, 1)
                    if projects:
                        proj(v, 0, 0)
                    if feeds:
                        feed_wo(f)
                    transpose_p(u, 0)
                    if projects:
                        proj(v, 0, 1)
                    if feeds:
                        feed_mean(f)
                    scores(u, 1, 0)
                    values(u, 0, 0)
                    values(u, 0, 1)
                    scores(u, 1, 1)
                    if projects:
                        transpose_qk(v, 0, 0, 0)
                    if feeds:
                        feed_var(f)
                    if projects:
                        transpose_qk(v, 0, 0, 1)
                        proj(v, 0, 2)
                    transpose_o(u, 0)
                    if feeds:
                        feed_rstd(f)
                    if projects:
                        transpose_qk(v, 0, 1, 0)
                        transpose_qk(v, 0, 1, 1)
                        proj(v, 1, 0)
                    transpose_p(u, 1)
                    if projects:
                        proj(v, 1, 1)
                    if feeds:
                        feed_w1(f, 0)
                    values(u, 1, 0)
                    if feeds:
                        feed_w1(f, 1)
                    values(u, 1, 1)
                    if feeds:
                        feed_w1(f, 2)
                    if projects:
                        proj(v, 1, 2)
                        transpose_qk(v, 1, 0, 0)
                        transpose_qk(v, 1, 0, 1)
                    transpose_o(u, 1)
                    if projects:
                        transpose_qk(v, 1, 1, 0)
                    if feeds:
                        feed_w2(f)
                    if projects:
                        transpose_qk(v, 1, 1, 1)

                schedule(pe, project, feed, body)

                with pe.Fori(0, B) as b:
                    pe.wait_ge(xl_d.sem, xl_d.at(b))
                    for t in range(TT):
                        last = M.transpose(ps[:, PJ, t * P:(t + 1) * P], xlast[:, t * P:(t + 1) * P], ident_s[:, :])
                    last.then_inc(xl_p.sem, 1)


def _constants():
    import numpy as np

    f = np.float32
    half = np.arange(0, D, 2, dtype=f)
    inv_freq = f(1.0) / f(10000.0) ** (half / f(D))
    pos = np.arange(T, dtype=f)
    freqs = pos[:, None] * inv_freq[None, :]
    freqs = np.concatenate([freqs, freqs], -1)
    base = (half + f(0.4 * D)) / f(1.4 * D)
    power = (pos - T // 2) / f(WIN // 2)
    scale = base[None, :] ** power[:, None]
    scale = np.concatenate([scale, scale], -1).astype(f)
    cos, sin = np.cos(freqs).astype(f), np.sin(freqs).astype(f)
    sign = np.concatenate([-np.ones(D // 2, f), np.ones(D // 2, f)])
    inv = (f(1.0) / scale).astype(f)
    rope = np.stack([cos * scale, sin * scale * sign, cos * inv, sin * inv * sign]).astype(f)
    rope = rope.reshape(4, TT, P, D).transpose(2, 0, 1, 3)

    i = np.arange(P)[:, None] % WIN
    j = np.arange(2 * WIN)[None, :]
    seen = (j >= i) & (j <= i + WIN)
    first = seen & ((np.arange(P)[:, None] >= WIN) | (j >= WIN))
    win_mask = np.where(np.stack([first, seen], 1), f(0), f(NEG)).astype(f)

    q = np.arange(P)[:, None]
    k = np.arange(P)[None, :]
    tri = np.where(k <= q, f(0), f(NEG)).astype(f)
    causal = np.concatenate([tri, np.zeros((P, P), f), tri], 1)

    def bf16_part(a):
        bits = np.ascontiguousarray(a, f).view(np.uint32) & np.uint32(0xFFFF0000)
        return bits.view(f)

    slopes = (f(2.0) ** (-f(8.0 / H0) * np.arange(1, H0 + 1, dtype=f))).astype(f)
    keys = np.concatenate([np.arange(P), np.arange(T)]).astype(f)
    bias = (slopes[:, None] * keys[None, :]).astype(f)
    parts = []
    for _ in range(3):
        part = bf16_part(bias)
        parts.append(part)
        bias = bias - part
    alibi = np.zeros((P, HG, KEYS), f)
    ones3 = np.zeros((P, P), f)
    pick = np.zeros((P, HG), f)
    for h in range(H0):
        for n in range(3):
            alibi[32 * (h // HG) + n, h % HG] = parts[n][h]
            ones3[32 * (h // HG) + n] = 1
        pick[h * D0:(h + 1) * D0, h % HG] = f(1.0) / np.sqrt(f(D0))
    return {"rope": rope, "ident": np.eye(P, dtype=f), "win_mask": win_mask, "causal": causal,
            "alibi": alibi, "ones3": ones3, "head_pick": pick}


def kernel(**inputs):
    import numpy as np
    import concourse.bacc as bacc
    from concourse.bass_utils import run_bass_kernel_spmd

    a = {k: np.asarray(v) for k, v in inputs.items()}

    def rows(v, n=P):
        return np.ascontiguousarray(np.broadcast_to(v, (n,) + v.shape))

    b1 = np.zeros((L, 6, P), np.float32)
    w2 = np.zeros((L, 3, P, C), np.float32)
    for i, (at, n) in enumerate(PIECES):
        w2[:, i, :n] = a["L0_ffn_W2"][:, at:at + n]
        for g in range(2):
            b1[:, 3 * g + i, :n] = a["L0_ffn_b1"][:, g * DI + at:g * DI + at + n]
    arrays = {
        "x": a["L0_attn_x"],
        "w_attn": a["L0_attn_w_attn"],
        "b_attn_cols": a["L0_attn_b_attn"][:2 * C].reshape(2, C).T,
        "b_v_rows": rows(a["L0_attn_b_attn"][2 * C:]),
        "w_proj": a["L0_attn_w_proj"],
        "b_proj_rows": rows(a["L0_attn_b_proj"]),
        "wqkv": a["L0_ffn_Wqkv"],
        "q_scale_rows": rows(a["L0_ffn_q_scale"]),
        "k_scale_rows": rows(a["L0_ffn_k_scale"]),
        "wo": a["L0_ffn_Wo"].reshape(L, PAIRS, P, C).transpose(0, 2, 1, 3),
        "ln_cols": np.stack([a["L0_ffn_ln_g"].T, a["L0_ffn_ln_b"].T], 1),
        "w1": a["L0_ffn_W1"],
        "b1_cols": b1.transpose(2, 0, 1).reshape(P, L * 6),
        "w2": w2.transpose(0, 2, 1, 3),
        "b2_cols": a["L0_ffn_b2"].T,
        **_constants(),
    }
    nc = bacc.Bacc("TRN2", target_bir_lowering=False, num_devices=1)
    feeds, args = {}, {}
    for name, v in arrays.items():
        v = np.ascontiguousarray(v)
        feeds[name + "_dram"] = v
        args[name] = nc.dram_tensor(name + "_dram", v.shape, mybir.dt.from_np(v.dtype), kind="ExternalInput").ap()
    out = nc.dram_tensor("out_dram", (B, T, C), F32, kind="ExternalOutput").ap()
    build(nc, out=out, **args)
    r = run_bass_kernel_spmd(nc, [feeds], core_ids=[0])
    return r.results[0]["out_dram"]
```

```python
from contextlib import ExitStack

import concourse.bass as bass
from concourse import mybir

F32 = mybir.dt.float32
BF16 = mybir.dt.bfloat16
ALU = mybir.AluOpType
ACT = mybir.ActivationFunctionType
AX_X = mybir.AxisListType.X

P = 128
C = 128
B = 8
T = 256
TT = T // P
LN_EPS = 1e-5
NEG = -1e30

H0 = 16
D0 = C // H0
HG = 4
KEYS = P + T

L = 6
H = 16
D = 64
PAIRS = H // 2
INNER = H * D
WIN = 32
NW = T // WIN
QK_SCALE = 8.0
DI = int(C * 4 * 2 / 3)
PIECES = [(0, 128), (128, 128), (256, DI - 256)]
UNITS = L * B
LOOP_FROM = 2
LOOP_STEPS = UNITS - 4


class Signal:

    def __init__(self, sem, per=1, start=0):
        self.sem, self.per, self.start = sem, per, start

    def at(self, u, i=0):
        return self.per * u + (i + 1 + self.start)

    def before(self, u, i=0):
        return self.per * u + (i + self.start)


def build(nc, x, w_attn, b_attn_cols, b_v_rows, w_proj, b_proj_rows, wqkv, q_scale_rows, k_scale_rows, wo,
          ln_cols, w1, b1_cols, w2, b2_cols, rope, ident, win_mask, causal, alibi, ones3, head_pick, out):
    with ExitStack() as ctx:
        def sb(name, shape, dt=F32):
            return ctx.enter_context(nc.sbuf_tensor(name, shape, dt))

        def signal(name, per=1, start=0):
            return Signal(ctx.enter_context(nc.semaphore(name)), per, start)

        ps = ctx.enter_context(nc.psum_tensor("ps", [P, 8, 512], F32))

        x1 = sb("x1", [P, B * TT, C])
        xT = sb("xT", [P, B * T])
        ident_s = sb("ident_s", [P, P])
        ident_b = sb("ident_b", [P, P], BF16)
        mean_w = sb("mean_w", [P, P])
        rope_s = sb("rope_s", [P, 4, TT, D])
        rope_l = sb("rope_l", [P, L * 4 * TT * D])
        scale_s = sb("scale_s", [P, 2, L, D])
        ln_s = sb("ln_s", [P, 2, L])
        b1_s = sb("b1_s", [P, L * 6])
        b2_s = sb("b2_s", [P, L])
        cur = sb("cur", [P, 2, 9])
        minus_half = sb("minus_half", [P, H])
        wmask_s = sb("wmask_s", [P, 2, 2 * WIN])
        wmask = sb("wmask", [P, 2, PAIRS, 2 * WIN], BF16)
        wqkv_s = sb("wqkv_s", [P, 3 * INNER])
        wo_s = sb("wo_s", [P, PAIRS, C])
        w1_s = sb("w1_s", [P, 2 * DI])
        w2_s = sb("w2_s", [P, 3, C])

        consts_in = signal("consts_in")
        x_in = signal("x_in")
        qkvw_in = signal("qkvw_in", 16)
        ffw_in = signal("ffw_in", 64)
        setup_done = signal("setup_done")
        pool_setup = signal("pool_setup")
        x0_ready = signal("x0_ready")

        def in_register(eng, value):
            return value if isinstance(value, int) else eng.snap(value)

        with ExitStack() as ctx0:
            def sb0(name, shape, dt=F32):
                return ctx0.enter_context(nc.sbuf_tensor(name, shape, dt))

            wa = sb0("wa", [P, 3 * C])
            wp = sb0("wp", [P, C])
            bqk = sb0("bqk", [P, 2])
            bqm = sb0("bqm", [P, H0])
            pick = sb0("pick", [P, H0])
            bv = sb0("bv", [P, C])
            bp = sb0("bp", [P, C])
            causal_s = sb0("causal_s", [P, KEYS])
            causal_b = sb0("causal_b", [P, KEYS], BF16)
            alibi_s = sb0("alibi_s", [P, HG, KEYS])
            alibi_b = sb0("alibi_b", [P, HG, KEYS], BF16)
            ones3_s = sb0("ones3_s", [P, HG, P])
            ones3_b = sb0("ones3_b", [P, HG, P], BF16)
            stats = sb0("stats", [P, TT, 6])
            mv = sb0("mv", [P, TT, 2])
            var0 = sb0("var0", [P, TT])
            rstd0 = sb0("rstd0", [P, TT])
            xn = sb0("xn", [P, TT, C])
            xnT = sb0("xnT", [P, T])
            kT0 = sb0("kT0", [P, T])
            qm = sb0("qm", [P, H0, T])
            vm = sb0("vm", [P, TT, HG, HG, HG, D0])
            nmax = sb0("nmax", [P, H0, TT])
            rsum = sb0("rsum", [P, TT, H0])
            rinv = sb0("rinv", [P, TT, H0])
            rexp = sb0("rexp", [P, TT, H0, D0])
            p0 = sb0("p0", [P, 2, KEYS])
            pT0 = sb0("pT0", [P, 2, KEYS])
            rT = sb0("rT", [P, T])
            oT0 = sb0("oT0", [P, T])
            ybuf = sb0("ybuf", [P, TT, C])

            const_loads = [
                (wa[:, :], w_attn), (wp[:, :], w_proj), (bqk[:, :], b_attn_cols), (pick[:, :], head_pick),
                (bv[:, :], b_v_rows), (bp[:, :], b_proj_rows), (causal_s[:, :], causal), (alibi_s[:, :, :], alibi),
                (ones3_s[:, :, :], ones3), (ident_s[:, :], ident), (rope_s[:, :, :, :], rope),
                (scale_s[:, 0, :, :], q_scale_rows), (scale_s[:, 1, :, :], k_scale_rows), (ln_s[:, :, :], ln_cols),
                (b1_s[:, :], b1_cols), (b2_s[:, :], b2_cols), (wmask_s[:, :, :], win_mask),
            ]

            dve_set = signal("dve_set")
            stats_d = signal("stats_d", 2)
            aggr_d = signal("aggr_d", 2)
            var_d = signal("var_d", 2)
            rstd_g = signal("rstd_g", 2)
            xn_d = signal("xn_d", 2)
            xnT_p = signal("xnT_p", 2)
            xnT_a = signal("xnT_a")
            qk_p = signal("qk_p")
            k_a = signal("k_a")
            q_a = signal("q_a", H0)
            v_p = signal("v_p")
            v_d = signal("v_d")
            s_p = signal("s_p", H0)
            max_d = signal("max_d", H0)
            exp_a = signal("exp_a", H0)
            pT_p = signal("pT_p", H0)
            pT_d = signal("pT_d", H0)
            pv_p = signal("pv_p", H0)
            rinv_d = signal("rinv_d")
            rexp_d = signal("rexp_d")
            rT_p = signal("rT_p")
            rT_a = signal("rT_a")
            oT_d = signal("oT_d")
            y_p = signal("y_p")
            yb_d = signal("yb_d")
            x1_d = signal("x1_d")

            BANK_T, BANK_V, BANK_S, BANK_PT, BANK_O, BANK_QK = 0, 1, 2, 4, 6, 7

            with nc.Block() as block:
                @block.sync
                def _(sp):
                    sp.dma_start(x1[:, :, :], x.rearrange("b (t p) c -> p (b t) c", p=P)).then_inc(x_in.sem, 16)
                    for dst, src in const_loads:
                        sp.dma_start(dst, src).then_inc(consts_in.sem, 16)
                    sp.dma_start(wqkv_s[:, :], wqkv[0, :, :]).then_inc(qkvw_in.sem, 16)
                    sp.dma_start(wo_s[:, :, :], wo[0, :, :, :]).then_inc(ffw_in.sem, 16)
                    sp.dma_start(w1_s[:, :], w1[0, :, :]).then_inc(ffw_in.sem, 16)
                    sp.dma_start(w2_s[:, :, :], w2[0, :, :, :]).then_inc(ffw_in.sem, 16)

                @block.gpsimd
                def _(pool):
                    nc.gpsimd.memset(vm[:, :, :, :, :, :], 0.0)
                    nc.gpsimd.memset(minus_half[:, :], -0.5).then_inc(pool_setup.sem, 1)
                    pool.wait_ge(pool_setup.sem, 1)
                    with pool.Fori(0, B) as b:
                        for n in range(2):
                            pool.wait_ge(var_d.sem, var_d.at(b, n))
                            nc.gpsimd.tensor_tensor(rstd0[:, :], var0[:, :], minus_half[:, 0:TT], ALU.pow).then_inc(rstd_g.sem, 1)

                @block.vector
                def _(dve):
                    V = nc.vector
                    V.memset(mean_w[:, :], 1.0 / C)
                    dve.wait_ge(consts_in.sem, 16 * len(const_loads))
                    V.tensor_copy(ident_b[:, :], ident_s[:, :])
                    V.tensor_copy(causal_b[:, :], causal_s[:, :])
                    V.tensor_copy(alibi_b[:, :, :], alibi_s[:, :, :])
                    V.tensor_copy(ones3_b[:, :, :], ones3_s[:, :, :])
                    V.tensor_scalar(bqm[:, :], pick[:, :], bqk[:, 0:1], None, ALU.mult)
                    for m in range(2):
                        V.tensor_copy(wmask[:, m, :, :], wmask_s[:, m, None, :].broadcast_to([P, PAIRS, 2 * WIN]))
                    for layer in range(L):
                        for k in range(4):
                            dst = rope_l[:, (layer * 4 + k) * TT * D:(layer * 4 + k + 1) * TT * D]
                            dst = dst.rearrange("p (t s e) -> p t s e", t=TT, s=2)
                            src = rope_s[:, k, :, :].rearrange("p t (s e) -> p t s e", s=2)
                            sc = scale_s[:, k // 2, layer, :].rearrange("p (s e) -> p s e", s=2)
                            for half in range(2):
                                other = half if k % 2 == 0 else 1 - half
                                last = V.tensor_tensor(dst[:, :, half, :], src[:, :, half, :],
                                                       sc[:, other, None, :].broadcast_to([P, TT, D // 2]), ALU.mult)
                    last.then_inc(setup_done.sem, 1)
                    dve.wait_ge(x_in.sem, 16)
                    dve.wait_ge(pool_setup.sem, 1)

                    def layernorm(b, n):
                        for t in range(TT):
                            last = V.bn_stats(stats[:, t, :], x1[:, bass.ds(b * TT + t, 1), :].rearrange("p o c -> p (o c)"))
                        last.then_inc(stats_d.sem, 1)
                        dve.wait_ge(stats_d.sem, stats_d.at(b, n))
                        V.memset(var0[:, :], LN_EPS)
                        for t in range(TT):
                            last = V.bn_aggr(mv[:, t, :], stats[:, t, :])
                        last.then_inc(aggr_d.sem, 1)
                        value = in_register(dve, aggr_d.at(b, n))
                        dve.wait_ge(setup_done.sem, 1)
                        dve.wait_ge(aggr_d.sem, value)
                        V.tensor_tensor(var0[:, :], mv[:, :, 1], var0[:, :], ALU.add).then_inc(var_d.sem, 1)
                        dve.wait_ge(rstd_g.sem, rstd_g.at(b, n))
                        for t in range(TT):
                            last = V.tensor_scalar(xn[:, t, :], x1[:, bass.ds(b * TT + t, 1), :].rearrange("p o c -> p (o c)"),
                                                   mv[:, t, 0:1], rstd0[:, t:t + 1], ALU.subtract, ALU.mult)
                        last.then_inc(xn_d.sem, 1)

                    def evac_pT(b, h):
                        dve.wait_ge(pT_p.sem, pT_p.at(b, h))
                        if h >= 2:
                            dve.wait_ge(pv_p.sem, pv_p.at(b, h - 2))
                        V.tensor_copy(pT0[:, h % 2, :], ps[:, BANK_PT + h % 2, 0:KEYS]).then_inc(pT_d.sem, 1)

                    with dve.Fori(0, B) as b:
                        layernorm(b, 0)
                        dve.wait_ge(v_p.sem, v_p.at(b))
                        for j in range(HG):
                            for t in range(TT):
                                src = ps[:, BANK_V, t * C:(t + 1) * C].rearrange("p (r j d) -> p r j d", r=HG, j=HG)
                                bias = bv[:, :].rearrange("p (r j d) -> p r j d", r=HG, j=HG)
                                last = V.tensor_tensor(vm[:, t, j, :, j, :], src[:, :, j, :], bias[:, :, j, :], ALU.add)
                        last.then_inc(v_d.sem, 1)
                        for h in range(H0):
                            dve.wait_ge(s_p.sem, s_p.at(b, h))
                            s = ps[:, BANK_S + h % 2, :]
                            V.tensor_reduce(nmax[:, h, 0:1], s[:, 0:P], AX_X, ALU.max, negate=True)
                            V.tensor_reduce(nmax[:, h, 1:2], s[:, P:KEYS], AX_X, ALU.max, negate=True).then_inc(max_d.sem, 1)
                            if h >= 1:
                                evac_pT(b, h - 1)
                        evac_pT(b, H0 - 1)
                        V.reciprocal(rinv[:, :, :], rsum[:, :, :]).then_inc(rinv_d.sem, 1)
                        dve.wait_ge(rinv_d.sem, rinv_d.at(b))
                        V.tensor_copy(rexp[:, :, :, :], rinv[:, :, :, None].broadcast_to([P, TT, H0, D0])).then_inc(rexp_d.sem, 1)
                        dve.wait_ge(rT_a.sem, rT_a.at(b))
                        dve.wait_ge(pv_p.sem, pv_p.at(b, H0 - 1))
                        V.tensor_tensor(oT0[:, :], ps[:, BANK_O, 0:T], rT[:, :], ALU.mult).then_inc(oT_d.sem, 1)
                        dve.wait_ge(y_p.sem, y_p.at(b))
                        V.tensor_tensor(ybuf[:, :, :], ps[:, BANK_T, 0:T].rearrange("p (t c) -> p t c", t=TT),
                                        bp[:, None, :].broadcast_to([P, TT, C]), ALU.add).then_inc(yb_d.sem, 1)
                        dve.wait_ge(yb_d.sem, yb_d.at(b))
                        xb = x1[:, bass.ds(b * TT, TT), :]
                        V.tensor_tensor(xb, ybuf[:, :, :], xb, ALU.add).then_inc(x1_d.sem, 1)
                        value = in_register(dve, x1_d.at(b))
                        dve.wait_ge(setup_done.sem, 1)
                        dve.wait_ge(x1_d.sem, value)
                        layernorm(b, 1)
                        dve.wait_ge(xnT_p.sem, xnT_p.at(b, 1))

                @block.scalar
                def _(act):
                    S = nc.scalar
                    act.wait_ge(setup_done.sem, 1)

                    def head_q(h):
                        S.activation(qm[:, h, :], ps[:, BANK_QK, 0:T], ACT.Identity,
                                     bias=bqm[:, h:h + 1], scale=pick[:, h:h + 1]).then_inc(q_a.sem, 1)

                    with act.Fori(0, B) as b:
                        act.wait_ge(xnT_p.sem, xnT_p.at(b, 0))
                        S.activation(xnT[:, :], ps[:, BANK_T, 0:T], ACT.Copy).then_inc(xnT_a.sem, 1)
                        act.wait_ge(qk_p.sem, qk_p.at(b))
                        S.activation(kT0[:, :], ps[:, BANK_QK, T:2 * T], ACT.Identity, bias=bqk[:, 1:2]).then_inc(k_a.sem, 1)
                        for h in range(2):
                            head_q(h)
                        for h in range(H0):
                            act.wait_ge(max_d.sem, max_d.at(b, h))
                            if h >= 2:
                                act.wait_ge(pT_p.sem, pT_p.at(b, h - 2))
                            s = ps[:, BANK_S + h % 2, :]
                            S.activation(p0[:, h % 2, 0:P], s[:, 0:P], ACT.Exp, bias=nmax[:, h, 0:1],
                                         accum_out=rsum[:, 0, h:h + 1])
                            S.activation(p0[:, h % 2, P:KEYS], s[:, P:KEYS], ACT.Exp, bias=nmax[:, h, 1:2],
                                         accum_out=rsum[:, 1, h:h + 1]).then_inc(exp_a.sem, 1)
                            if h + 2 < H0:
                                head_q(h + 2)
                        act.wait_ge(rT_p.sem, rT_p.at(b))
                        S.activation(rT[:, :], ps[:, BANK_V, 0:T], ACT.Copy).then_inc(rT_a.sem, 1)
                        act.wait_ge(xnT_p.sem, xnT_p.at(b, 1))
                        S.activation(xT[:, bass.ds(b * T, T)], ps[:, BANK_T, 0:T], ACT.Copy).then_inc(x0_ready.sem, 1)

                @block.tensor
                def _(pe):
                    M = nc.tensor
                    pe.wait_ge(setup_done.sem, 1)

                    def scores(b, h):
                        r, j = h // HG, h % HG
                        s = ps[:, BANK_S + h % 2, :]
                        pe.wait_ge(q_a.sem, q_a.at(b, h))
                        if h >= 2:
                            pe.wait_ge(exp_a.sem, exp_a.at(b, h - 2))
                        M.matmul(s[:, 0:KEYS], ident_b[:, :], causal_b[:, :], start=True, stop=False)
                        M.matmul(s[:, 0:KEYS], ones3_b[:, r, :], alibi_b[:, j, :], start=False, stop=False)
                        M.matmul(s[:, 0:P], qm[:, h, 0:P], kT0[:, 0:P], start=False, stop=False)
                        M.matmul(s[:, P:KEYS], qm[:, h, P:T], kT0[:, :], start=False, stop=True).then_inc(s_p.sem, 1)

                    def transpose_p(b, h):
                        pe.wait_ge(exp_a.sem, exp_a.at(b, h))
                        if h >= 2:
                            pe.wait_ge(pT_d.sem, pT_d.at(b, h - 2))
                        for c in range(KEYS // P):
                            last = M.transpose(ps[:, BANK_PT + h % 2, c * P:(c + 1) * P], p0[:, h % 2, c * P:(c + 1) * P], ident_s[:, :])
                        last.then_inc(pT_p.sem, 1)

                    def values(b, h):
                        r, j = h // HG, h % HG
                        o = ps[32 * r:32 * r + 32, BANK_O, :]
                        pe.wait_ge(pT_d.sem, pT_d.at(b, h))
                        cols = [vm[:, t, j, r, :, :].rearrange("p j d -> p (j d)") for t in range(TT)]
                        M.matmul(o[:, 0:T], cols[0], pT0[:, h % 2, 0:T], start=j == 0, stop=False)
                        M.matmul(o[:, P:T], cols[1], pT0[:, h % 2, T:KEYS], start=False, stop=j == HG - 1).then_inc(pv_p.sem, 1)

                    with pe.Fori(0, B) as b:
                        pe.wait_ge(xn_d.sem, xn_d.at(b, 0))
                        for t in range(TT):
                            last = M.transpose(ps[:, BANK_T, t * P:(t + 1) * P], xn[:, t, :], ident_s[:, :])
                        last.then_inc(xnT_p.sem, 1)
                        pe.wait_ge(xnT_a.sem, xnT_a.at(b))
                        for k in range(2):
                            last = M.matmul(ps[:, BANK_QK, k * T:(k + 1) * T], wa[:, k * C:(k + 1) * C], xnT[:, :], start=True, stop=True)
                        last.then_inc(qk_p.sem, 1)
                        for t in range(TT):
                            last = M.matmul(ps[:, BANK_V, t * C:(t + 1) * C], xnT[:, t * P:(t + 1) * P], wa[:, 2 * C:3 * C], start=True, stop=True)
                        last.then_inc(v_p.sem, 1)
                        pe.wait_ge(k_a.sem, k_a.at(b))
                        pe.wait_ge(v_d.sem, v_d.at(b))
                        for i in range(H0 + 2):
                            if i < H0:
                                scores(b, i)
                            if 1 <= i <= H0:
                                transpose_p(b, i - 1)
                            if i >= 2:
                                values(b, i - 2)
                        pe.wait_ge(rexp_d.sem, rexp_d.at(b))
                        for t in range(TT):
                            last = M.transpose(ps[:, BANK_V, t * P:(t + 1) * P], rexp[:, t, :, :].rearrange("p h d -> p (h d)"), ident_s[:, :])
                        last.then_inc(rT_p.sem, 1)
                        pe.wait_ge(oT_d.sem, oT_d.at(b))
                        for t in range(TT):
                            last = M.matmul(ps[:, BANK_T, t * C:(t + 1) * C], oT0[:, t * P:(t + 1) * P], wp[:, :], start=True, stop=True)
                        last.then_inc(y_p.sem, 1)
                        pe.wait_ge(xn_d.sem, xn_d.at(b, 1))
                        for t in range(TT):
                            last = M.transpose(ps[:, BANK_T, t * P:(t + 1) * P], xn[:, t, :], ident_s[:, :])
                        last.then_inc(xnT_p.sem, 1)
                        pe.wait_ge(x0_ready.sem, x0_ready.at(b))

        xs = sb("xs", [P, 2, T])
        raw = sb("raw", [P, 2, INNER])
        sq = sb("sq", [P, INNER])
        rot1 = sb("rot1", [P, 2, INNER])
        rot2 = sb("rot2", [P, 2, INNER])
        ssum = sb("ssum", [P, 2, H])
        rnorm = sb("rnorm", [P, 2, H])
        qT = sb("qT", [P, 2, PAIRS, T])
        kT = sb("kT", [P, 2, PAIRS, WIN + T])
        vn = sb("vn", [P, TT, INNER])
        vk = sb("vk", [P, NW, PAIRS, 2, D])
        smax = sb("smax", [P, 2, H])
        prob = sb("prob", [P, 2, H * 2 * WIN])
        lsum = sb("lsum", [P, 2, H])
        linv = sb("linv", [P, 2, H])
        pT = sb("pT", [P, PAIRS, P])
        on = sb("on", [P, INNER])
        oT = sb("oT", [P, PAIRS, T])
        xf = sb("xf", [P, T])
        xc = sb("xc", [P, T])
        xq = sb("xq", [P, T])
        vtok = sb("vtok", [P, TT])
        rtok = sb("rtok", [P, TT])
        rwide = sb("rwide", [P, TT, P])
        xg = sb("xg", [P, T])
        gate = sb("gate", [P, T])
        hid = sb("hid", [P, 3, T])
        xlast = sb("xlast", [P, T])
        outb = sb("outb", [P, TT, C])

        PJ, SO, TP, FB = 0, (2, 4), 6, 7

        zeroed = signal("zeroed")
        xs_d = signal("xs_d")
        proj_p = signal("proj_p", 6)
        raw_a = signal("raw_a", 4)
        sq_a = signal("sq_a", 4)
        ss_d = signal("ss_d", 4)
        cl_d = signal("cl_d", 4)
        rn_g = signal("rn_g", 4)
        nrm_d = signal("nrm_d", 4)
        cos_d = signal("cos_d", 4)
        sin_g = signal("sin_g", 4)
        rope_d = signal("rope_d", 4)
        qkT_p = signal("qkT_p", 8)
        qkT_a = signal("qkT_a", 8)
        vn_a = signal("vn_a", 2)
        VK_DMAS = (14, 16)
        vk_in = [signal(f"vk_in{t}", 16 * VK_DMAS[t]) for t in range(TT)]
        sc_p = signal("sc_p", 2)
        mx_d = signal("mx_d", 2)
        sub_d = signal("sub_d", 2)
        ex_a = signal("ex_a", 2)
        ls_d = signal("ls_d", 2)
        li_d = signal("li_d", 2)
        ptp = signal("ptp", 2)
        pta = signal("pta", 2)
        av_p = signal("av_p", 2, start=2)
        on_d = signal("on_d", 2)
        otp = signal("otp", 2)
        ota = signal("ota", 2)
        wo_p = signal("wo_p")
        x2_d = signal("x2_d")
        xf_d = signal("xf_d")
        cur_d = signal("cur_d")
        mean_p = signal("mean_p")
        xc_d = signal("xc_d")
        xq_a = signal("xq_a")
        var_p = signal("var_p")
        vr_d = signal("vr_d")
        rr_g = signal("rr_g")
        rx_d = signal("rx_d")
        rt_p = signal("rt_p")
        xg_d = signal("xg_d")
        xh_d = signal("xh_d")
        w1_p = signal("w1_p", 3)
        gelu_a = signal("gelu_a", 3)
        hid_d = signal("hid_d", 3)
        w2_p = signal("w2_p")
        fin_d = signal("fin_d")
        xl_d = signal("xl_d")
        xl_p = signal("xl_p")
        res_d = signal("res_d")
        out_done = signal("out_done", 16)

        def index(u):
            return u[0] * 2 + u[1]

        def live(u):
            n = index(u)
            return not isinstance(n, int) or 0 <= n < UNITS

        def pipeline(eng, step):
            for u in range(-1, LOOP_FROM):
                step((0, u - 1), (0, u), (0, u + 1))
            with eng.Fori(0, LOOP_STEPS // 2) as m:
                for u in range(LOOP_FROM, LOOP_FROM + 2):
                    step((m, u - 1), (m, u), (m, u + 1))
            for u in range(LOOP_FROM + LOOP_STEPS, UNITS + 1):
                step((0, u - 1), (0, u), (0, u + 1))

        with nc.Block() as block:
            @block.sync
            def _(sp):
                def copy_v(u):
                    n = index(u)
                    for t in range(TT):
                        value = in_register(sp, vn_a.at(n, t))
                        sp.wait_ge(setup_done.sem, 1)
                        sp.wait_ge(av_p.sem, value)
                        sp.wait_ge(vn_a.sem, value)
                        for w in range(4 * t, 4 * t + 4):
                            for back in (1, 0):
                                if w - back < 0:
                                    continue
                                tile, k = (w - back) // 4, (w - back) % 4
                                src = vn[32 * k:32 * k + 32, tile, :].rearrange("p (a s e) -> p a s e", a=PAIRS, s=2)
                                for hp in range(2):
                                    lo = 64 * hp + 32 * (1 - back)
                                    sp.dma_start(vk[lo:lo + 32, w, :, hp, :], src[:, :, hp, :]).then_inc(vk_in[t].sem, 16)

                def load_qkv(layer):
                    sp.wait_ge(proj_p.sem, proj_p.before(layer * B, 0))
                    sp.dma_start(wqkv_s[:, :], wqkv[bass.ds(layer, 1), :, :].rearrange("o p n -> p (o n)")).then_inc(qkvw_in.sem, 16)

                def load_ffw(layer):
                    sp.wait_ge(w2_p.sem, w2_p.before(layer * B, 0))
                    sp.dma_start(wo_s[:, :, :], wo[bass.ds(layer, 1), :, :, :].rearrange("o p k n -> p (o k) n")).then_inc(ffw_in.sem, 16)
                    sp.dma_start(w1_s[:, :], w1[bass.ds(layer, 1), :, :].rearrange("o p n -> p (o n)")).then_inc(ffw_in.sem, 16)
                    sp.dma_start(w2_s[:, :, :], w2[bass.ds(layer, 1), :, :, :].rearrange("o p k n -> p (o k) n")).then_inc(ffw_in.sem, 16)

                sp.wait_ge(zeroed.sem, 1)
                copy_v((0, 0))
                copy_v((0, 1))
                with sp.Fori(0, L - 1) as layer:
                    with sp.Fori(0, 3) as i:
                        m = layer * 4 + i
                        copy_v((m, 2))
                        copy_v((m, 3))
                    load_qkv(layer + 1)
                    copy_v((layer * 4, 8))
                    copy_v((layer * 4, 9))
                    load_ffw(layer + 1)
                with sp.Fori(0, 3) as i:
                    copy_v((i, UNITS - 6))
                    copy_v((i, UNITS - 5))
                with sp.Fori(0, B) as b:
                    sp.wait_ge(res_d.sem, res_d.at(b))
                    sp.dma_start(out[bass.ds(b, 1), :, :].rearrange("o (t p) c -> p (o t) c", p=P), outb[:, :, :]).then_inc(out_done.sem, 16)
                sp.wait_ge(out_done.sem, 16 * B)

            @block.gpsimd
            def _(pool):
                G = nc.gpsimd
                pool.wait_ge(x0_ready.sem, B)
                G.memset(xs[:, :, :], 0.0)
                G.memset(xf[:, :], 0.0)
                G.memset(kT[:, :, :, :], 0.0)
                G.memset(vk[:, :, :, :, :], 0.0).then_inc(zeroed.sem, 1)

                def norms(u, t, kind):
                    if not live(u):
                        return
                    n, i = index(u), 2 * t + kind
                    pool.wait_ge(cl_d.sem, cl_d.at(n, i))
                    G.tensor_tensor(rnorm[:, kind, :], ssum[:, kind, :], minus_half[:, :], ALU.pow).then_inc(rn_g.sem, 1)

                def feed_rstd(u):
                    if not live(u):
                        return
                    n = index(u)
                    pool.wait_ge(vr_d.sem, vr_d.at(n))
                    G.tensor_tensor(rtok[:, :], vtok[:, :], minus_half[:, 0:TT], ALU.pow).then_inc(rr_g.sem, 1)

                def normalise(u, t, kind):
                    if not live(u):
                        return
                    n, i = index(u), 2 * t + kind
                    pool.wait_ge(rn_g.sem, rn_g.at(n, i))
                    v = raw[:, kind, :].rearrange("p (h e) -> p h e", h=H)
                    G.tensor_tensor(v, v, rnorm[:, kind, :, None].broadcast_to([P, H, D]), ALU.mult).then_inc(nrm_d.sem, 1)

                def sin_term(u, t, kind):
                    if not live(u):
                        return
                    n = index(u)
                    i = 2 * t + kind
                    pool.wait_ge(nrm_d.sem, nrm_d.at(n, i))
                    if t > 0 or not (isinstance(n, int) and n < 1):
                        pool.wait_ge(rope_d.sem, rope_d.before(n, i - 1))
                    base = (n // B) * (4 * TT * D) + (2 * kind + 1) * TT * D + t * D
                    tab = rope_l[:, bass.ds(base, D)].rearrange("p (s e) -> p s e", s=2)
                    src = raw[:, kind, :].rearrange("p (h s e) -> p h s e", h=H, s=2)
                    dst = rot2[:, kind, :].rearrange("p (h s e) -> p h s e", h=H, s=2)
                    for half in range(2):
                        last = G.tensor_tensor(dst[:, :, half, :], src[:, :, 1 - half, :],
                                               tab[:, half, None, :].broadcast_to([P, H, D // 2]), ALU.mult)
                    last.then_inc(sin_g.sem, 1)

                def step(before, u, after):
                    norms(after, 0, 0)
                    feed_rstd(before)
                    sin_term(after, 0, 0)
                    norms(after, 0, 1)
                    normalise(after, 0, 1)
                    sin_term(after, 0, 1)
                    norms(after, 1, 0)
                    sin_term(after, 1, 0)
                    norms(after, 1, 1)
                    normalise(after, 1, 1)
                    sin_term(after, 1, 1)

                pipeline(pool, step)

            @block.vector
            def _(dve):
                V = nc.vector
                dve.wait_ge(x0_ready.sem, B)
                dve.wait_ge(zeroed.sem, 1)
                dve.sem_inc(fin_d.sem, 1)

                def seq(u):
                    return bass.ds((index(u) % B) * T, T)

                def shift_in(u):
                    if not live(u):
                        return
                    n, par = index(u), u[1] % 2
                    if not (isinstance(n, int) and n < 2):
                        dve.wait_ge(fin_d.sem, n - 1)
                        value = in_register(dve, proj_p.before(n - 1, 0))
                        dve.wait_ge(setup_done.sem, 1)
                        dve.wait_ge(proj_p.sem, value)
                    b = index(u) % B
                    V.tensor_copy(xs[0:64, par, :], xT[0:64, bass.ds(b * T, T)])
                    V.tensor_copy(xs[64:P, par, 1:T], xT[64:P, bass.ds(b * T, T - 1)]).then_inc(xs_d.sem, 1)

                def sums(u, t, kind):
                    if not live(u):
                        return
                    n, i = index(u), 2 * t + kind
                    dve.wait_ge(sq_a.sem, sq_a.at(n, i))
                    V.tensor_reduce(ssum[:, kind, :], sq[:, :].rearrange("p (h e) -> p h e", h=H), AX_X, ALU.add).then_inc(ss_d.sem, 1)
                    dve.wait_ge(ss_d.sem, ss_d.at(n, i))
                    V.tensor_scalar(ssum[:, kind, :], ssum[:, kind, :], 1e-24, None, ALU.max).then_inc(cl_d.sem, 1)

                def normalise(u, t, kind):
                    if not live(u):
                        return
                    n, i = index(u), 2 * t + kind
                    dve.wait_ge(rn_g.sem, rn_g.at(n, i))
                    v = raw[:, kind, :].rearrange("p (h e) -> p h e", h=H)
                    V.tensor_tensor(v, v, rnorm[:, kind, :, None].broadcast_to([P, H, D]), ALU.mult).then_inc(nrm_d.sem, 1)

                def cos_term(u, t, kind):
                    if not live(u):
                        return
                    n, i = index(u), 2 * t + kind
                    dve.wait_ge(nrm_d.sem, nrm_d.at(n, i))
                    if t > 0 or not (isinstance(n, int) and n < 1):
                        dve.wait_ge(qkT_p.sem, qkT_p.before(n, 4 * t + 2 * kind - 2))
                    base = (n // B) * (4 * TT * D) + 2 * kind * TT * D + t * D
                    tab = rope_l[:, bass.ds(base, D)]
                    V.tensor_tensor(rot1[:, kind, :].rearrange("p (h e) -> p h e", h=H),
                                    raw[:, kind, :].rearrange("p (h e) -> p h e", h=H),
                                    tab[:, None, :].broadcast_to([P, H, D]), ALU.mult).then_inc(cos_d.sem, 1)

                def rotate(u, t, kind):
                    if not live(u):
                        return
                    n, i = index(u), 2 * t + kind
                    dve.wait_ge(cos_d.sem, cos_d.at(n, i))
                    dve.wait_ge(sin_g.sem, sin_g.at(n, i))
                    V.tensor_tensor(rot1[:, kind, :], rot1[:, kind, :], rot2[:, kind, :], ALU.add).then_inc(rope_d.sem, 1)

                def tile_scores(t):
                    return ps[:, SO[t]:SO[t] + 2, :].rearrange("p b (h k) -> p (b h) k", k=64)

                def soft_max(u, t):
                    if not live(u):
                        return
                    n = index(u)
                    dve.wait_ge(sc_p.sem, sc_p.at(n, t))
                    V.tensor_reduce(smax[:, t, :], tile_scores(t), AX_X, ALU.max).then_inc(mx_d.sem, 1)
                    dve.wait_ge(mx_d.sem, mx_d.at(n, t))
                    if not (isinstance(n, int) and n < 1):
                        dve.wait_ge(ptp.sem, ptp.at(n - 1, t))
                    V.tensor_tensor(prob[:, t, :].rearrange("p (h k) -> p h k", h=H), tile_scores(t),
                                    smax[:, t, :, None].broadcast_to([P, H, 2 * WIN]), ALU.subtract).then_inc(sub_d.sem, 1)

                def soft_sum(u, t):
                    if not live(u):
                        return
                    n = index(u)
                    dve.wait_ge(ex_a.sem, ex_a.at(n, t))
                    V.tensor_reduce(lsum[:, t, :], prob[:, t, :].rearrange("p (h k) -> p h k", h=H), AX_X, ALU.add).then_inc(ls_d.sem, 1)
                    dve.wait_ge(ls_d.sem, ls_d.at(n, t))
                    V.reciprocal(linv[:, t, :], lsum[:, t, :]).then_inc(li_d.sem, 1)

                def normalise_o(u, t):
                    if not live(u):
                        return
                    n = index(u)
                    dve.wait_ge(li_d.sem, li_d.at(n, t))
                    dve.wait_ge(av_p.sem, av_p.at(n, t))
                    if t > 0 or not (isinstance(n, int) and n < 1):
                        dve.wait_ge(otp.sem, otp.before(n, t))
                    V.tensor_tensor(on[:, :].rearrange("p (h e) -> p h e", h=H), tile_scores(t),
                                    linv[:, t, :, None].broadcast_to([P, H, D]), ALU.mult).then_inc(on_d.sem, 1)

                def feed_1(u):
                    if not live(u):
                        return
                    n = index(u)
                    layer = n // B
                    dve.wait_ge(wo_p.sem, wo_p.at(n))
                    V.tensor_tensor(xT[:, seq(u)], ps[:, FB, 0:T], xT[:, seq(u)], ALU.add).then_inc(x2_d.sem, 1)
                    value = in_register(dve, x2_d.at(n))
                    dve.wait_ge(setup_done.sem, 1)
                    dve.wait_ge(x2_d.sem, value)
                    b = n % B
                    V.tensor_copy(xf[0:64, :], xT[0:64, bass.ds(b * T, T)])
                    V.tensor_copy(xf[64:P, 1:T], xT[64:P, bass.ds(b * T, T - 1)]).then_inc(xf_d.sem, 1)
                    V.tensor_copy(cur[:, 0, 0:2], ln_s[:, :, bass.ds(layer, 1)].rearrange("p a o -> p (a o)"))
                    V.tensor_copy(cur[:, 0, 2:8], b1_s[:, bass.ds(layer * 6, 6)])
                    V.tensor_copy(cur[:, 0, 8:9], b2_s[:, bass.ds(layer, 1)]).then_inc(cur_d.sem, 1)

                def feed_2(u):
                    if not live(u):
                        return
                    n = index(u)
                    dve.wait_ge(mean_p.sem, mean_p.at(n))
                    V.tensor_tensor(xc[:, :], xf[:, :], ps[:, FB, 0:T], ALU.subtract).then_inc(xc_d.sem, 1)

                def feed_3(u):
                    if not live(u):
                        return
                    n = index(u)
                    dve.wait_ge(var_p.sem, var_p.at(n))
                    V.tensor_scalar(vtok[:, :], ps[:, FB, T:T + TT], LN_EPS, None, ALU.add).then_inc(vr_d.sem, 1)

                def feed_spread(u):
                    if not live(u):
                        return
                    n = index(u)
                    dve.wait_ge(rr_g.sem, rr_g.at(n))
                    V.tensor_copy(rwide[:, :, :], rtok[:, :, None].broadcast_to([P, TT, P])).then_inc(rx_d.sem, 1)

                def feed_norm(u):
                    if not live(u):
                        return
                    n = index(u)
                    dve.wait_ge(rt_p.sem, rt_p.at(n))
                    V.tensor_tensor(xg[:, :], xc[:, :], ps[:, FB, 0:T], ALU.mult).then_inc(xg_d.sem, 1)
                    dve.wait_ge(xg_d.sem, xg_d.at(n))
                    V.tensor_scalar(xg[:, :], xg[:, :], cur[:, 0, 0:1], cur[:, 0, 1:2], ALU.mult, ALU.add).then_inc(xh_d.sem, 1)

                def feed_hidden(u, i):
                    if not live(u):
                        return
                    n, rows = index(u), PIECES[i][1]
                    dve.wait_ge(gelu_a.sem, gelu_a.at(n, i))
                    V.scalar_tensor_tensor(hid[0:rows, i, :], ps[0:rows, FB, 0:T], cur[0:rows, 0, 2 + i:3 + i],
                                           gate[0:rows, :], ALU.add, ALU.mult).then_inc(hid_d.sem, 1)

                def feed_4(u):
                    if not live(u):
                        return
                    n = index(u)
                    dve.wait_ge(w2_p.sem, w2_p.at(n))
                    V.scalar_tensor_tensor(xT[:, seq(u)], ps[:, FB, 0:T], cur[:, 0, 8:9], xT[:, seq(u)],
                                           ALU.add, ALU.add).then_inc(fin_d.sem, 1)

                def step(before, u, after):
                    shift_in(after)
                    rotate(u, 1, 0)
                    cos_term(u, 1, 1)
                    soft_max(u, 0)
                    rotate(u, 1, 1)
                    sums(after, 0, 0)
                    feed_1(before)
                    soft_sum(u, 0)
                    feed_2(before)
                    normalise(after, 0, 0)
                    feed_3(before)
                    cos_term(after, 0, 0)
                    feed_spread(before)
                    sums(after, 0, 1)
                    rotate(after, 0, 0)
                    feed_norm(before)
                    soft_max(u, 1)
                    sums(after, 1, 0)
                    cos_term(after, 0, 1)
                    feed_hidden(before, 0)
                    normalise_o(u, 0)
                    rotate(after, 0, 1)
                    feed_hidden(before, 1)
                    normalise(after, 1, 0)
                    sums(after, 1, 1)
                    soft_sum(u, 1)
                    feed_hidden(before, 2)
                    normalise_o(u, 1)
                    feed_4(before)
                    cos_term(after, 1, 0)

                pipeline(dve, step)

                with dve.Fori(0, B) as b:
                    dve.wait_ge(fin_d.sem, UNITS + 1)
                    V.tensor_copy(xlast[:, :], xT[:, bass.ds(b * T, T)]).then_inc(xl_d.sem, 1)
                    dve.wait_ge(xl_p.sem, xl_p.at(b))
                    V.tensor_tensor(outb[:, :, :], ps[:, PJ, 0:T].rearrange("p (t c) -> p t c", t=TT),
                                    x1[:, bass.ds(b * TT, TT), :], ALU.add).then_inc(res_d.sem, 1)
                    dve.wait_ge(out_done.sem, out_done.per * (b + 1))

            @block.scalar
            def _(act):
                S = nc.scalar
                act.wait_ge(x0_ready.sem, B)

                def copy_raw(u, t, kind):
                    if not live(u):
                        return
                    n, i = index(u), 2 * t + kind
                    act.wait_ge(proj_p.sem, proj_p.at(n, 3 * t + kind))
                    if t > 0 or not (isinstance(n, int) and n < 1):
                        act.wait_ge(cos_d.sem, cos_d.before(n, i - 1))
                        act.wait_ge(sin_g.sem, sin_g.before(n, i - 1))
                    S.activation(raw[:, kind, :], ps[:, PJ:PJ + 2, :].rearrange("p a n -> p (a n)"), ACT.Copy).then_inc(raw_a.sem, 1)

                def square(u, t, kind):
                    if not live(u):
                        return
                    n, i = index(u), 2 * t + kind
                    act.wait_ge(raw_a.sem, raw_a.at(n, i))
                    if i > 0 or not (isinstance(n, int) and n < 1):
                        act.wait_ge(ss_d.sem, ss_d.before(n, i))
                    S.activation(sq[:, :], raw[:, kind, :], ACT.Square).then_inc(sq_a.sem, 1)

                def copy_v(u, t):
                    if not live(u):
                        return
                    n, par = index(u), u[1] % 2
                    act.wait_ge(proj_p.sem, proj_p.at(n, 3 * t + 2))
                    if not (isinstance(n, int) and n < 1):
                        act.wait_ge(vk_in[1].sem, vk_in[1].at(n - 1, vk_in[1].per - 1))
                    S.activation(vn[:, t, :], ps[:, PJ:PJ + 2, :].rearrange("p a n -> p (a n)"), ACT.Copy).then_inc(vn_a.sem, 1)

                def copy_qkT(u, t, kind, half):
                    if not live(u):
                        return
                    n, par = index(u), u[1] % 2
                    i = 4 * t + 2 * kind + half
                    act.wait_ge(qkT_p.sem, qkT_p.at(n, i))
                    src = ps[:, TP, :].rearrange("p (a n) -> p a n", a=4)
                    pairs = slice(4 * half, 4 * half + 4)
                    if kind == 0:
                        last = S.activation(qT[:, par, pairs, t * P:(t + 1) * P], src, ACT.Copy)
                    else:
                        if not (isinstance(n, int) and n < 1):
                            act.wait_ge(sc_p.sem, sc_p.at(n - 1, 1))
                        for hp in range(2):
                            rows = slice(64 * hp, 64 * hp + 64)
                            last = S.activation(kT[rows, hp, pairs, WIN + t * P:WIN + (t + 1) * P], src[rows], ACT.Copy)
                    last.then_inc(qkT_a.sem, 1)

                def exps(u, t):
                    if not live(u):
                        return
                    n = index(u)
                    act.wait_ge(sub_d.sem, sub_d.at(n, t))
                    S.activation(prob[:, t, :], prob[:, t, :], ACT.Exp, scale=QK_SCALE).then_inc(ex_a.sem, 1)

                def copy_pT(u, t):
                    if not live(u):
                        return
                    n = index(u)
                    act.wait_ge(ptp.sem, ptp.at(n, t))
                    if t > 0 or not (isinstance(n, int) and n < 1):
                        act.wait_ge(av_p.sem, av_p.before(n, t))
                    S.activation(pT[:, :, :].rearrange("p a q -> p (a q)"), ps[:, SO[t]:SO[t] + 2, :].rearrange("p a n -> p (a n)"),
                                 ACT.Copy).then_inc(pta.sem, 1)

                def copy_oT(u, t):
                    if not live(u):
                        return
                    n = index(u)
                    act.wait_ge(otp.sem, otp.at(n, t))
                    if t == 0 and not (isinstance(n, int) and n < 1):
                        act.wait_ge(wo_p.sem, wo_p.at(n - 1))
                    S.activation(oT[:, :, t * P:(t + 1) * P], ps[:, SO[t]:SO[t] + 2, :].rearrange("p s (a q) -> p (s a) q", a=4),
                                 ACT.Copy).then_inc(ota.sem, 1)

                def square_x(u):
                    if not live(u):
                        return
                    n = index(u)
                    act.wait_ge(xc_d.sem, xc_d.at(n))
                    S.activation(xq[:, :], xc[:, :], ACT.Square).then_inc(xq_a.sem, 1)

                def gelu(u, i):
                    if not live(u):
                        return
                    n, rows = index(u), PIECES[i][1]
                    act.wait_ge(w1_p.sem, w1_p.at(n, i))
                    if i > 0:
                        act.wait_ge(hid_d.sem, hid_d.at(n, i - 1))
                    S.activation(gate[0:rows, :], ps[0:rows, FB, T:2 * T], ACT.Gelu, bias=cur[0:rows, 0, 5 + i:6 + i]).then_inc(gelu_a.sem, 1)

                def step(before, u, after):
                    copy_qkT(u, 0, 1, 1)
                    copy_oT(before, 1)
                    copy_raw(after, 0, 0)
                    square(after, 0, 0)
                    copy_qkT(u, 1, 0, 0)
                    exps(u, 0)
                    copy_qkT(u, 1, 0, 1)
                    copy_raw(after, 0, 1)
                    copy_qkT(u, 1, 1, 0)
                    square_x(before)
                    square(after, 0, 1)
                    copy_v(after, 0)
                    copy_qkT(u, 1, 1, 1)
                    copy_raw(after, 1, 0)
                    square(after, 1, 0)
                    copy_qkT(after, 0, 0, 0)
                    copy_pT(u, 0)
                    exps(u, 1)
                    gelu(before, 0)
                    copy_raw(after, 1, 1)
                    copy_pT(u, 1)
                    gelu(before, 1)
                    copy_qkT(after, 0, 0, 1)
                    square(after, 1, 1)
                    copy_qkT(after, 0, 1, 0)
                    gelu(before, 2)
                    copy_oT(u, 0)
                    copy_v(after, 1)

                pipeline(act, step)

            @block.tensor
            def _(pe):
                M = nc.tensor
                pe.wait_ge(x0_ready.sem, B)
                pe.wait_ge(zeroed.sem, 1)
                pe.sem_inc(av_p.sem, av_p.start)

                def proj(u, t, kind):
                    if not live(u):
                        return
                    n, par = index(u), u[1] % 2
                    i = 3 * t + kind
                    if i == 0:
                        pe.wait_ge(xs_d.sem, xs_d.at(n))
                        pe.wait_ge(qkvw_in.sem, 16 * (n // B) + 16)
                    if kind > 0:
                        pe.wait_ge(raw_a.sem, raw_a.at(n, 2 * t + kind - 1))
                    elif t > 0 or not (isinstance(n, int) and n < 1):
                        pe.wait_ge(vn_a.sem, vn_a.before(n, t))
                    w = wqkv_s[:, kind * INNER:(kind + 1) * INNER]
                    for half in range(2):
                        last = M.matmul(ps[:, PJ + half, :], xs[:, par, t * P:(t + 1) * P], w[:, half * 512:(half + 1) * 512], start=True, stop=True)
                    last.then_inc(proj_p.sem, 1)

                def transpose_qk(u, t, kind, half):
                    if not live(u):
                        return
                    n = index(u)
                    i = 4 * t + 2 * kind + half
                    pe.wait_ge(rope_d.sem, rope_d.at(n, 2 * t + kind))
                    pe.wait_ge(qkT_a.sem, qkT_a.before(n, i))
                    for a in range(4):
                        c = 4 * half + a
                        last = M.transpose(ps[:, TP, a * P:(a + 1) * P], rot1[:, kind, c * P:(c + 1) * P], ident_s[:, :])
                    last.then_inc(qkT_p.sem, 1)

                def scores(u, t):
                    if not live(u):
                        return
                    n, par = index(u), u[1] % 2
                    pe.wait_ge(qkT_a.sem, qkT_a.at(n, 4 * t + 3))
                    if not (isinstance(n, int) and n < 1):
                        pe.wait_ge(ota.sem, ota.at(n - 1, t))
                    mask = wmask[:, 0 if t == 0 else 1, :, :].rearrange("p a k -> p (a k)")
                    for hp in range(2):
                        M.matmul(ps[:, SO[t] + hp, :], ident_b[:, :], mask, start=True, stop=False)
                    for a in range(PAIRS):
                        for k in range(4):
                            w = 4 * t + k
                            out_s = ps[32 * k:32 * k + 32, SO[t] + a // 4, (a % 4) * P:(a % 4 + 1) * P]
                            last = M.matmul(out_s, qT[:, par, a, 32 * w:32 * w + 32], kT[:, :, a, 32 * w:32 * w + 64],
                                            start=False, stop=a % 4 == 3)
                    last.then_inc(sc_p.sem, 1)

                def transpose_p(u, t):
                    if not live(u):
                        return
                    n = index(u)
                    pe.wait_ge(vk_in[t].sem, vk_in[t].at(n, vk_in[t].per - 1))
                    pe.wait_ge(ex_a.sem, ex_a.at(n, t))
                    for a in range(PAIRS):
                        last = M.transpose(ps[:, SO[t] + a // 4, (a % 4) * P:(a % 4 + 1) * P], prob[:, t, a * P:(a + 1) * P], ident_s[:, :])
                    last.then_inc(ptp.sem, 1)

                def values(u, t):
                    if not live(u):
                        return
                    n, par = index(u), u[1] % 2
                    pe.wait_ge(pta.sem, pta.at(n, t))
                    for a in range(PAIRS):
                        for k in range(4):
                            last = M.matmul(ps[32 * k:32 * k + 32, SO[t] + a // 4, (a % 4) * P:(a % 4 + 1) * P],
                                            pT[:, a, 32 * k:32 * k + 32], vk[:, 4 * t + k, a, :, :], start=True, stop=True)
                    last.then_inc(av_p.sem, 1)

                def transpose_o(u, t):
                    if not live(u):
                        return
                    n = index(u)
                    pe.wait_ge(on_d.sem, on_d.at(n, t))
                    for a in range(PAIRS):
                        last = M.transpose(ps[:, SO[t] + a // 4, (a % 4) * P:(a % 4 + 1) * P], on[:, a * P:(a + 1) * P], ident_s[:, :])
                    last.then_inc(otp.sem, 1)

                def feed_wo(u):
                    if not live(u):
                        return
                    n = index(u)
                    pe.wait_ge(ffw_in.sem, 48 * (n // B) + 48)
                    pe.wait_ge(ota.sem, ota.at(n, 1))
                    pe.wait_ge(fin_d.sem, fin_d.at(n))
                    for a in range(PAIRS):
                        last = M.matmul(ps[:, FB, 0:T], wo_s[:, a, :], oT[:, a, :], start=a == 0, stop=a == PAIRS - 1)
                    last.then_inc(wo_p.sem, 1)

                def feed_mean(u):
                    if not live(u):
                        return
                    n = index(u)
                    pe.wait_ge(xf_d.sem, xf_d.at(n))
                    M.matmul(ps[:, FB, 0:T], mean_w[:, :], xf[:, :], start=True, stop=True).then_inc(mean_p.sem, 1)

                def feed_var(u):
                    if not live(u):
                        return
                    n = index(u)
                    pe.wait_ge(xq_a.sem, xq_a.at(n))
                    for t in range(TT):
                        last = M.matmul(ps[:, FB, T + t:T + t + 1], xq[:, t * P:(t + 1) * P], mean_w[:, 0:1], start=True, stop=True)
                    last.then_inc(var_p.sem, 1)

                def feed_rstd(u):
                    if not live(u):
                        return
                    n = index(u)
                    pe.wait_ge(rx_d.sem, rx_d.at(n))
                    for t in range(TT):
                        last = M.transpose(ps[:, FB, t * P:(t + 1) * P], rwide[:, t, :], ident_s[:, :])
                    last.then_inc(rt_p.sem, 1)

                def feed_w1(u, i):
                    if not live(u):
                        return
                    n = index(u)
                    at, rows = PIECES[i]
                    if i == 0:
                        pe.wait_ge(xh_d.sem, xh_d.at(n))
                    else:
                        pe.wait_ge(hid_d.sem, hid_d.at(n, i - 1))
                    for g in range(2):
                        last = M.matmul(ps[0:rows, FB, g * T:(g + 1) * T], w1_s[:, g * DI + at:g * DI + at + rows], xg[:, :],
                                        start=True, stop=True)
                    last.then_inc(w1_p.sem, 1)

                def feed_w2(u):
                    if not live(u):
                        return
                    n = index(u)
                    pe.wait_ge(hid_d.sem, hid_d.at(n, 2))
                    for i, (_, rows) in enumerate(PIECES):
                        last = M.matmul(ps[:, FB, 0:T], w2_s[0:rows, i, :], hid[0:rows, i, :], start=i == 0, stop=i == 2)
                    last.then_inc(w2_p.sem, 1)

                def step(before, u, after):
                    scores(u, 0)
                    proj(after, 0, 0)
                    transpose_qk(u, 1, 0, 0)
                    feed_wo(before)
                    transpose_qk(u, 1, 0, 1)
                    proj(after, 0, 1)
                    transpose_qk(u, 1, 1, 0)
                    feed_mean(before)
                    transpose_p(u, 0)
                    proj(after, 0, 2)
                    feed_var(before)
                    transpose_qk(u, 1, 1, 1)
                    proj(after, 1, 0)
                    feed_rstd(before)
                    scores(u, 1)
                    transpose_qk(after, 0, 0, 0)
                    proj(after, 1, 1)
                    feed_w1(before, 0)
                    values(u, 0)
                    transpose_qk(after, 0, 0, 1)
                    transpose_p(u, 1)
                    feed_w1(before, 1)
                    proj(after, 1, 2)
                    transpose_qk(after, 0, 1, 0)
                    transpose_o(u, 0)
                    feed_w1(before, 2)
                    values(u, 1)
                    transpose_qk(after, 0, 1, 1)
                    feed_w2(before)
                    transpose_o(u, 1)

                pipeline(pe, step)

                with pe.Fori(0, B) as b:
                    pe.wait_ge(xl_d.sem, xl_d.at(b))
                    for t in range(TT):
                        last = M.transpose(ps[:, PJ, t * P:(t + 1) * P], xlast[:, t * P:(t + 1) * P], ident_s[:, :])
                    last.then_inc(xl_p.sem, 1)


def _constants():
    import numpy as np

    f = np.float32
    half = np.arange(0, D, 2, dtype=f)
    inv_freq = f(1.0) / f(10000.0) ** (half / f(D))
    pos = np.arange(T, dtype=f)
    freqs = pos[:, None] * inv_freq[None, :]
    freqs = np.concatenate([freqs, freqs], -1)
    base = (half + f(0.4 * D)) / f(1.4 * D)
    power = (pos - T // 2) / f(WIN // 2)
    scale = base[None, :] ** power[:, None]
    scale = np.concatenate([scale, scale], -1).astype(f)
    cos, sin = np.cos(freqs).astype(f), np.sin(freqs).astype(f)
    sign = np.concatenate([-np.ones(D // 2, f), np.ones(D // 2, f)])
    inv = (f(1.0) / scale).astype(f)
    rope = np.stack([cos * scale, sin * scale * sign, cos * inv, sin * inv * sign]).astype(f)
    rope = rope.reshape(4, TT, P, D).transpose(2, 0, 1, 3)

    i = np.arange(P)[:, None] % WIN
    j = np.arange(2 * WIN)[None, :]
    seen = (j >= i) & (j <= i + WIN)
    first = seen & ((np.arange(P)[:, None] >= WIN) | (j >= WIN))
    win_mask = np.where(np.stack([first, seen], 1), f(0), f(NEG)).astype(f)

    q = np.arange(P)[:, None]
    k = np.arange(P)[None, :]
    tri = np.where(k <= q, f(0), f(NEG)).astype(f)
    causal = np.concatenate([tri, np.zeros((P, P), f), tri], 1)

    def bf16_part(a):
        bits = np.ascontiguousarray(a, f).view(np.uint32) & np.uint32(0xFFFF0000)
        return bits.view(f)

    slopes = (f(2.0) ** (-f(8.0 / H0) * np.arange(1, H0 + 1, dtype=f))).astype(f)
    keys = np.concatenate([np.arange(P), np.arange(T)]).astype(f)
    bias = (slopes[:, None] * keys[None, :]).astype(f)
    parts = []
    for _ in range(3):
        part = bf16_part(bias)
        parts.append(part)
        bias = bias - part
    alibi = np.zeros((P, HG, KEYS), f)
    ones3 = np.zeros((P, HG, P), f)
    pick = np.zeros((P, H0), f)
    for h in range(H0):
        for n in range(3):
            alibi[32 * (h // HG) + n, h % HG] = parts[n][h]
            ones3[32 * (h // HG) + n, h // HG] = 1
        pick[h * D0:(h + 1) * D0, h] = f(1.0) / np.sqrt(f(D0))
    return {"rope": rope, "ident": np.eye(P, dtype=f), "win_mask": win_mask, "causal": causal,
            "alibi": alibi, "ones3": ones3, "head_pick": pick}


def kernel(**inputs):
    import numpy as np
    import concourse.bacc as bacc
    from concourse.bass_utils import run_bass_kernel_spmd

    a = {k: np.asarray(v) for k, v in inputs.items()}

    def rows(v, n=P):
        return np.ascontiguousarray(np.broadcast_to(v, (n,) + v.shape))

    b1 = np.zeros((L, 6, P), np.float32)
    w2 = np.zeros((L, 3, P, C), np.float32)
    for i, (at, n) in enumerate(PIECES):
        w2[:, i, :n] = a["L0_ffn_W2"][:, at:at + n]
        for g in range(2):
            b1[:, 3 * g + i, :n] = a["L0_ffn_b1"][:, g * DI + at:g * DI + at + n]
    arrays = {
        "x": a["L0_attn_x"],
        "w_attn": a["L0_attn_w_attn"],
        "b_attn_cols": a["L0_attn_b_attn"][:2 * C].reshape(2, C).T,
        "b_v_rows": rows(a["L0_attn_b_attn"][2 * C:]),
        "w_proj": a["L0_attn_w_proj"],
        "b_proj_rows": rows(a["L0_attn_b_proj"]),
        "wqkv": a["L0_ffn_Wqkv"],
        "q_scale_rows": rows(a["L0_ffn_q_scale"]),
        "k_scale_rows": rows(a["L0_ffn_k_scale"]),
        "wo": a["L0_ffn_Wo"].reshape(L, PAIRS, P, C).transpose(0, 2, 1, 3),
        "ln_cols": np.stack([a["L0_ffn_ln_g"].T, a["L0_ffn_ln_b"].T], 1),
        "w1": a["L0_ffn_W1"],
        "b1_cols": b1.transpose(2, 0, 1).reshape(P, L * 6),
        "w2": w2.transpose(0, 2, 1, 3),
        "b2_cols": a["L0_ffn_b2"].T,
        **_constants(),
    }
    nc = bacc.Bacc("TRN2", target_bir_lowering=False, num_devices=1)
    feeds, args = {}, {}
    for name, v in arrays.items():
        v = np.ascontiguousarray(v)
        feeds[name + "_dram"] = v
        args[name] = nc.dram_tensor(name + "_dram", v.shape, mybir.dt.from_np(v.dtype), kind="ExternalInput").ap()
    out = nc.dram_tensor("out_dram", (B, T, C), F32, kind="ExternalOutput").ap()
    build(nc, out=out, **args)
    r = run_bass_kernel_spmd(nc, [feeds], core_ids=[0])
    return r.results[0]["out_dram"]
```

```python
from contextlib import ExitStack

import concourse.bass as bass
from concourse import mybir

F32 = mybir.dt.float32
BF16 = mybir.dt.bfloat16
F32R = mybir.dt.float32r
ALU = mybir.AluOpType
ACT = mybir.ActivationFunctionType
AX_X = mybir.AxisListType.X

P = 128
C = 128
B = 8
T = 256
TT = T // P
LN_EPS = 1e-5
NEG = -1e30

H0 = 16
D0 = C // H0
HG = 4
KEYS = P + T

L = 6
H = 16
D = 64
PAIRS = H // 2
INNER = H * D
WIN = 32
NW = T // WIN
QK_SCALE = 8.0
DI = int(C * 4 * 2 / 3)
PIECES = [(0, 128), (128, 128), (256, DI - 256)]
UNITS = L * B
LOOP_FROM = 2
LOOP_STEPS = UNITS - 4


class Signal:

    def __init__(self, sem, per=1, start=0):
        self.sem, self.per, self.start = sem, per, start

    def at(self, u, i=0):
        return self.per * u + (i + 1 + self.start)

    def before(self, u, i=0):
        return self.per * u + (i + self.start)


def build(nc, x, w_attn, b_attn_cols, b_v_rows, w_proj, b_proj_rows, wqkv, q_scale_rows, k_scale_rows, wo,
          ln_cols, w1, b1_cols, w2, b2_cols, rope, ident, win_mask, causal, alibi, ones3, head_pick, out):
    with ExitStack() as ctx:
        def sb(name, shape, dt=F32):
            return ctx.enter_context(nc.sbuf_tensor(name, shape, dt))

        def signal(name, per=1, start=0):
            return Signal(ctx.enter_context(nc.semaphore(name)), per, start)

        ps = ctx.enter_context(nc.psum_tensor("ps", [P, 8, 512], F32))

        xT = sb("xT", [P, B * T])
        ident_s = sb("ident_s", [P, P])
        ident_b = sb("ident_b", [P, P], BF16)
        mean_w = sb("mean_w", [P, P])
        rope_l = sb("rope_l", [P, L * 4 * TT * D])
        ln_s = sb("ln_s", [P, 2, L])
        b1_s = sb("b1_s", [P, L * 6])
        b2_s = sb("b2_s", [P, L])
        cur = sb("cur", [P, 2, 9])
        minus_half = sb("minus_half", [P, H])
        wmask = sb("wmask", [P, 2, PAIRS, 2 * WIN], BF16)
        wqkv_s = sb("wqkv_s", [P, 3 * INNER])
        wqkv_hi = sb("wqkv_hi", [P, 3 * INNER], F32R)
        wqkv_lo = sb("wqkv_lo", [P, 3 * INNER], F32R)
        wo_s = sb("wo_s", [P, PAIRS, C])
        w1_s = sb("w1_s", [P, 2 * DI])
        w2_s = sb("w2_s", [P, 3, C])

        xs_hi = sb("xs_hi", [P, 2, T], F32R)
        xs_lo = sb("xs_lo", [P, 2, T], F32R)
        xf = sb("xf", [P, T])
        kT = sb("kT", [P, 2, PAIRS, WIN + T])
        vk = sb("vk", [P, NW, PAIRS, 2, D])

        consts_in = signal("consts_in")
        tables_in = signal("tables_in")
        xf_zeroed = signal("xf_zeroed")
        tables_ready = signal("tables_ready")
        zeroed = signal("zeroed")
        x_in = signal("x_in")
        qkvw_in = [signal(f"{kind}w_in", 16) for kind in "qkv"]
        w_hi = [signal(f"{kind}w_hi") for kind in "qkv"]
        w_split_g = [signal(f"{kind}w_split_g") for kind in "qkv"]
        spilled = signal("spilled", 16)
        wo_in = signal("wo_in", 16)
        w1_in = signal("w1_in", 16)
        w2_in = signal("w2_in", 16)
        setup_done = signal("setup_done")
        pool_setup = signal("pool_setup")
        proj_p = signal("proj_p", 6)
        x0_ready = signal("x0_ready")

        def in_register(eng, value):
            return value if isinstance(value, int) else eng.snap(value)

        def w_cols(kind):
            return slice(kind * INNER, (kind + 1) * INNER)

        def weights_hi(act, layer, kind):
            act.wait_ge(qkvw_in[kind].sem, 16 * layer + 16)
            act.wait_ge(proj_p.sem, proj_p.at(layer * B - 1, 3 + kind))
            nc.scalar.activation(wqkv_hi[:, w_cols(kind)], wqkv_s[:, w_cols(kind)], ACT.Copy).then_inc(w_hi[kind].sem, 1)

        def weights_lo(eng, ops, layer, kind):
            eng.wait_ge(w_hi[kind].sem, layer + 1)
            ops.tensor_tensor(wqkv_lo[:, w_cols(kind)], wqkv_s[:, w_cols(kind)], wqkv_hi[:, w_cols(kind)],
                              ALU.subtract).then_inc(w_split_g[kind].sem, 1)

        with ExitStack() as ctx0:
            def sb0(name, shape, dt=F32):
                return ctx0.enter_context(nc.sbuf_tensor(name, shape, dt))

            x1 = sb0("x1", [P, B * TT, C])
            rope_s = sb0("rope_s", [P, 4, TT, D])
            scale_s = sb0("scale_s", [P, 2, L, D])
            wmask_s = sb0("wmask_s", [P, 2, 2 * WIN])
            wa = sb0("wa", [P, 3 * C])
            wp = sb0("wp", [P, C])
            bqk = sb0("bqk", [P, 2])
            bqm = sb0("bqm", [P, H0])
            pick = sb0("pick", [P, H0])
            bv = sb0("bv", [P, C])
            bp = sb0("bp", [P, C])
            causal_s = sb0("causal_s", [P, P])
            causal_b = sb0("causal_b", [P, P], BF16)
            alibi_s = sb0("alibi_s", [P, HG, KEYS])
            alibi_b = sb0("alibi_b", [P, HG, KEYS], BF16)
            ones3_s = sb0("ones3_s", [P, HG, P])
            ones3_b = sb0("ones3_b", [P, HG, P], BF16)
            stats = sb0("stats", [P, TT, 6])
            mv = sb0("mv", [P, TT, 2])
            var0 = sb0("var0", [P, TT])
            rstd0 = sb0("rstd0", [P, TT])
            xn = sb0("xn", [P, TT, C])
            xnT = sb0("xnT", [P, T])
            kT0 = sb0("kT0", [P, T])
            qm = sb0("qm", [P, H0, T])
            vm = sb0("vm", [P, TT, HG, HG, HG, D0])
            nmax = sb0("nmax", [P, H0, TT])
            rsum = sb0("rsum", [P, TT, H0])
            rinv = sb0("rinv", [P, TT, H0])
            rexp = sb0("rexp", [P, TT, H0, D0])
            p0 = sb0("p0", [P, 2, KEYS])
            pT0 = sb0("pT0", [P, 2, KEYS])
            rT = sb0("rT", [P, T])
            oT0 = sb0("oT0", [P, T])
            ybuf = sb0("ybuf", [P, TT, C])

            const_loads = [
                (ident_s[:, :], ident), (wa[:, :], w_attn), (bqk[:, :], b_attn_cols), (pick[:, :], head_pick),
                (causal_s[:, :], causal), (ones3_s[:, :, :], ones3), (alibi_s[:, :, :], alibi), (bv[:, :], b_v_rows),
                (wp[:, :], w_proj), (bp[:, :], b_proj_rows),
            ]
            table_loads = [
                (rope_s[:, :, :, :], rope), (scale_s[:, 0, :, :], q_scale_rows), (scale_s[:, 1, :, :], k_scale_rows),
                (ln_s[:, :, :], ln_cols), (b1_s[:, :], b1_cols), (b2_s[:, :], b2_cols), (wmask_s[:, :, :], win_mask),
            ]

            stats_d = [signal(f"stats_d{n}") for n in range(2)]
            aggr_d = [signal(f"aggr_d{n}") for n in range(2)]
            var_d = [signal(f"var_d{n}") for n in range(2)]
            rstd_g = [signal(f"rstd_g{n}") for n in range(2)]
            xn_d = [signal(f"xn_d{n}") for n in range(2)]
            xnT_p = [signal(f"xnT_p{n}") for n in range(2)]
            xnT_a = signal("xnT_a")
            qk_p = signal("qk_p")
            k_a = signal("k_a")
            q_a = signal("q_a", H0)
            v_p = signal("v_p")
            v_d = signal("v_d")
            s_p = signal("s_p", H0)
            max_d = signal("max_d", H0)
            exp_a = signal("exp_a", H0)
            pT_p = signal("pT_p", H0)
            pT_d = signal("pT_d", H0)
            pv_p = signal("pv_p", H0)
            rinv_d = signal("rinv_d")
            rexp_d = signal("rexp_d")
            rT_p = signal("rT_p")
            rT_a = signal("rT_a")
            oT_d = signal("oT_d")
            y_p = signal("y_p")
            yb_d = signal("yb_d")
            x1_d = signal("x1_d")

            BANK_TV, BANK_S, BANK_PT, BANK_O, BANK_QK = 0, 1, 4, 6, 7
            COL_V = T
            SB = 3

            def sequences(eng, step):
                step(0, False, True)
                with eng.Fori(1, B - 1) as b:
                    step(b, True, True)
                step(B - 1, True, False)

            with nc.Block() as block:
                @block.sync
                def _(sp):
                    sp.dma_start(x1[:, :, :], x.rearrange("b (t p) c -> p (b t) c", p=P)).then_inc(x_in.sem, 16)
                    for dst, src in const_loads:
                        sp.dma_start(dst, src).then_inc(consts_in.sem, 16)
                    for dst, src in table_loads:
                        sp.dma_start(dst, src).then_inc(tables_in.sem, 16)
                    for kind in range(3):
                        cols = slice(kind * INNER, (kind + 1) * INNER)
                        sp.dma_start(wqkv_s[:, cols], wqkv[0, :, cols]).then_inc(qkvw_in[kind].sem, 16)
                    sp.dma_start(wo_s[:, :, :], wo[0, :, :, :]).then_inc(wo_in.sem, 16)
                    sp.dma_start(w1_s[:, :], w1[0, :, :]).then_inc(w1_in.sem, 16)
                    sp.dma_start(w2_s[:, :, :], w2[0, :, :, :]).then_inc(w2_in.sem, 16)
                    with sp.Fori(0, B) as b:
                        sp.wait_ge(x1_d.sem, x1_d.at(b))
                        sp.dma_start(out[bass.ds(b, 1), :, :].rearrange("o (t p) c -> p (o t) c", p=P),
                                     x1[:, bass.ds(b * TT, TT), :]).then_inc(spilled.sem, 16)

                @block.gpsimd
                def _(pool):
                    nc.gpsimd.memset(vm[:, :, :, :, :, :], 0.0)
                    nc.gpsimd.memset(minus_half[:, :], -0.5).then_inc(pool_setup.sem, 1)
                    pool.wait_ge(pool_setup.sem, 1)

                    def rstd(b, n):
                        pool.wait_ge(var_d[n].sem, var_d[n].at(b))
                        nc.gpsimd.tensor_tensor(rstd0[:, :], var0[:, :], minus_half[:, 0:TT], ALU.pow).then_inc(rstd_g[n].sem, 1)

                    def first_weights():
                        for kind in range(3):
                            pool.wait_ge(qkvw_in[kind].sem, 16)
                            nc.gpsimd.tensor_copy(wqkv_hi[:, w_cols(kind)], wqkv_s[:, w_cols(kind)]).then_inc(w_hi[kind].sem, 1)
                            weights_lo(pool, nc.gpsimd, 0, kind)

                    def step(b, ends, leads):
                        if ends:
                            rstd(b - 1, 1)
                        if leads:
                            rstd(b + 1, 0)
                        if not ends:
                            first_weights()

                    rstd(0, 0)
                    nc.gpsimd.memset(xf[:, :], 0.0).then_inc(xf_zeroed.sem, 1)
                    pool.wait_ge(xf_zeroed.sem, 1)
                    for v in (xs_hi, xs_lo):
                        nc.gpsimd.tensor_copy(v[:, :, 0], xf[:, 0:2])
                    nc.gpsimd.memset(kT[:, :, :, :], 0.0)
                    nc.gpsimd.memset(vk[:, :, :, :, :], 0.0).then_inc(zeroed.sem, 1)
                    pool.wait_ge(tables_in.sem, 16 * len(table_loads))
                    for m in range(2):
                        nc.gpsimd.tensor_copy(wmask[:, m, :, :], wmask_s[:, m, None, :].broadcast_to([P, PAIRS, 2 * WIN]))
                    for layer in range(L):
                        for k in range(4):
                            dst = rope_l[:, (layer * 4 + k) * TT * D:(layer * 4 + k + 1) * TT * D]
                            dst = dst.rearrange("p (t s e) -> p t s e", t=TT, s=2)
                            src = rope_s[:, k, :, :].rearrange("p t (s e) -> p t s e", s=2)
                            sc = scale_s[:, k // 2, layer, :].rearrange("p (s e) -> p s e", s=2)
                            for half in range(2):
                                other = half if k % 2 == 0 else 1 - half
                                last = nc.gpsimd.tensor_tensor(dst[:, :, half, :], src[:, :, half, :],
                                                       sc[:, other, None, :].broadcast_to([P, TT, D // 2]), ALU.mult)
                    last.then_inc(tables_ready.sem, 1)
                    sequences(pool, step)
                    rstd(B - 1, 1)

                @block.vector
                def _(dve):
                    V = nc.vector
                    def rows_of(b, t):
                        return x1[:, bass.ds(b * TT + t, 1), :].rearrange("p o c -> p (o c)")

                    def moments(b, n):
                        for t in range(TT):
                            last = V.bn_stats(stats[:, t, :], rows_of(b, t))
                        last.then_inc(stats_d[n].sem, 1)
                        dve.wait_ge(stats_d[n].sem, stats_d[n].at(b))
                        V.memset(var0[:, :], LN_EPS)
                        for t in range(TT):
                            last = V.bn_aggr(mv[:, t, :], stats[:, t, :])
                        last.then_inc(aggr_d[n].sem, 1)
                        value = in_register(dve, aggr_d[n].at(b))
                        dve.wait_ge(pool_setup.sem, 1)
                        dve.wait_ge(aggr_d[n].sem, value)
                        V.tensor_tensor(var0[:, :], mv[:, :, 1], var0[:, :], ALU.add).then_inc(var_d[n].sem, 1)

                    def layernorm(b, n):
                        dve.wait_ge(rstd_g[n].sem, rstd_g[n].at(b))
                        for t in range(TT):
                            last = V.tensor_scalar(xn[:, t, :], rows_of(b, t), mv[:, t, 0:1], rstd0[:, t:t + 1], ALU.subtract, ALU.mult)
                        last.then_inc(xn_d[n].sem, 1)

                    def place_v(b):
                        dve.wait_ge(v_p.sem, v_p.at(b))
                        for j in range(HG):
                            for t in range(TT):
                                src = ps[:, BANK_TV, COL_V + t * C:COL_V + (t + 1) * C].rearrange("p (r j d) -> p r j d", r=HG, j=HG)
                                bias = bv[:, :].rearrange("p (r j d) -> p r j d", r=HG, j=HG)
                                last = V.tensor_tensor(vm[:, t, j, :, j, :], src[:, :, j, :], bias[:, :, j, :], ALU.add)
                        last.then_inc(v_d.sem, 1)

                    def row_max(b, h):
                        dve.wait_ge(s_p.sem, s_p.at(b, h))
                        s = ps[:, BANK_S + h % SB, :]
                        V.tensor_reduce(nmax[:, h, 0:1], s[:, 0:P], AX_X, ALU.max, negate=True)
                        V.tensor_reduce(nmax[:, h, 1:2], s[:, P:KEYS], AX_X, ALU.max, negate=True).then_inc(max_d.sem, 1)

                    def normalise_o(b):
                        dve.wait_ge(rT_a.sem, rT_a.at(b))
                        dve.wait_ge(pv_p.sem, pv_p.at(b, H0 - 1))
                        V.tensor_tensor(oT0[:, :], ps[:, BANK_O, 0:T], rT[:, :], ALU.mult).then_inc(oT_d.sem, 1)

                    def add_y(b):
                        dve.wait_ge(y_p.sem, y_p.at(b))
                        V.tensor_tensor(ybuf[:, :, :], ps[:, BANK_TV, 0:T].rearrange("p (t c) -> p t c", t=TT),
                                        bp[:, None, :].broadcast_to([P, TT, C]), ALU.add).then_inc(yb_d.sem, 1)
                        dve.wait_ge(yb_d.sem, yb_d.at(b))
                        xb = x1[:, bass.ds(b * TT, TT), :]
                        V.tensor_tensor(xb, ybuf[:, :, :], xb, ALU.add).then_inc(x1_d.sem, 1)

                    def moments_x1(b):
                        value = in_register(dve, x1_d.at(b))
                        dve.wait_ge(setup_done.sem, 1)
                        dve.wait_ge(x1_d.sem, value)
                        moments(b, 1)

                    def evac_pT(b, h):
                        dve.wait_ge(pT_p.sem, pT_p.at(b, h))
                        if h >= 2:
                            dve.wait_ge(pv_p.sem, pv_p.at(b, h - 2))
                        V.tensor_copy(pT0[:, h % 2, :], ps[:, BANK_PT + h % 2, 0:KEYS]).then_inc(pT_d.sem, 1)

                    def step(b, ends, leads):
                        row_max(b, 0)
                        if ends:
                            normalise_o(b - 1)
                        row_max(b, 1)
                        place_v(b)
                        if ends:
                            add_y(b - 1)
                        for h in range(2, H0):
                            row_max(b, h)
                            evac_pT(b, h - 2)
                            if ends and h == 4:
                                moments_x1(b - 1)
                            if ends and h == 6:
                                layernorm(b - 1, 1)
                            if leads and h == 9:
                                moments(b + 1, 0)
                            if leads and h == 11:
                                if ends:
                                    dve.wait_ge(xnT_p[1].sem, xnT_p[1].at(b - 1))
                                layernorm(b + 1, 0)
                        evac_pT(b, H0 - 2)
                        evac_pT(b, H0 - 1)
                        V.reciprocal(rinv[:, :, :], rsum[:, :, :]).then_inc(rinv_d.sem, 1)
                        dve.wait_ge(rinv_d.sem, rinv_d.at(b))
                        V.tensor_copy(rexp[:, :, :, :], rinv[:, :, :, None].broadcast_to([P, TT, H0, D0])).then_inc(rexp_d.sem, 1)

                    V.memset(mean_w[:, :], 1.0 / C)
                    dve.wait_ge(x_in.sem, 16)
                    dve.wait_ge(pool_setup.sem, 1)
                    moments(0, 0)
                    layernorm(0, 0)
                    dve.wait_ge(consts_in.sem, 16 * len(const_loads))
                    V.tensor_copy(ident_b[:, :], ident_s[:, :])
                    V.tensor_copy(causal_b[:, :], causal_s[:, :])
                    V.tensor_copy(alibi_b[:, :, :], alibi_s[:, :, :])
                    V.tensor_copy(ones3_b[:, :, :], ones3_s[:, :, :])
                    V.tensor_scalar(bqm[:, :], pick[:, :], bqk[:, 0:1], None, ALU.mult).then_inc(setup_done.sem, 1)
                    sequences(dve, step)
                    normalise_o(B - 1)
                    add_y(B - 1)
                    moments_x1(B - 1)
                    layernorm(B - 1, 1)

                @block.scalar
                def _(act):
                    S = nc.scalar
                    act.wait_ge(setup_done.sem, 1)

                    def head_q(h):
                        S.activation(qm[:, h, :], ps[:, BANK_QK, 0:T], ACT.Identity,
                                     bias=bqm[:, h:h + 1], scale=pick[:, h:h + 1]).then_inc(q_a.sem, 1)

                    def copy_xnT(b):
                        act.wait_ge(xnT_p[0].sem, xnT_p[0].at(b))
                        S.activation(xnT[:, :], ps[:, BANK_TV, 0:T], ACT.Copy).then_inc(xnT_a.sem, 1)

                    def copy_xT(b):
                        act.wait_ge(xnT_p[1].sem, xnT_p[1].at(b))
                        S.activation(xT[:, bass.ds(b * T, T)], ps[:, BANK_TV, 0:T], ACT.Copy).then_inc(x0_ready.sem, 1)

                    def copy_rT(b):
                        act.wait_ge(rT_p.sem, rT_p.at(b))
                        S.activation(rT[:, :], ps[:, BANK_TV, COL_V:COL_V + T], ACT.Copy).then_inc(rT_a.sem, 1)

                    def step(b, ends, leads):
                        act.wait_ge(qk_p.sem, qk_p.at(b))
                        S.activation(kT0[:, :], ps[:, BANK_QK, T:2 * T], ACT.Identity, bias=bqk[:, 1:2]).then_inc(k_a.sem, 1)
                        for h in range(2):
                            head_q(h)
                        if ends:
                            copy_rT(b - 1)
                        for h in range(H0):
                            act.wait_ge(max_d.sem, max_d.at(b, h))
                            if h >= 2:
                                act.wait_ge(pT_p.sem, pT_p.at(b, h - 2))
                            s = ps[:, BANK_S + h % SB, :]
                            S.activation(p0[:, h % 2, 0:P], s[:, 0:P], ACT.Exp, bias=nmax[:, h, 0:1],
                                         accum_out=rsum[:, 0, h:h + 1])
                            S.activation(p0[:, h % 2, P:KEYS], s[:, P:KEYS], ACT.Exp, bias=nmax[:, h, 1:2],
                                         accum_out=rsum[:, 1, h:h + 1]).then_inc(exp_a.sem, 1)
                            if h + 2 < H0:
                                head_q(h + 2)
                            if ends and h == 8:
                                copy_xT(b - 1)
                            if leads and h == 13:
                                copy_xnT(b + 1)

                    copy_xnT(0)
                    sequences(act, step)
                    copy_rT(B - 1)
                    copy_xT(B - 1)

                @block.tensor
                def _(pe):
                    M = nc.tensor
                    pe.wait_ge(setup_done.sem, 1)

                    def scores(b, h):
                        r, j = h // HG, h % HG
                        s = ps[:, BANK_S + h % SB, :]
                        pe.wait_ge(q_a.sem, q_a.at(b, h))
                        if h >= SB:
                            pe.wait_ge(exp_a.sem, exp_a.at(b, h - SB))
                        M.matmul(s[:, 0:KEYS], ones3_b[:, r, :], alibi_b[:, j, :], start=True, stop=False)
                        for c in (0, KEYS - P):
                            M.matmul(s[:, c:c + P], ident_b[:, :], causal_b[:, :], start=False, stop=False)
                        M.matmul(s[:, 0:P], qm[:, h, 0:P], kT0[:, 0:P], start=False, stop=False)
                        M.matmul(s[:, P:KEYS], qm[:, h, P:T], kT0[:, :], start=False, stop=True).then_inc(s_p.sem, 1)

                    def transpose_p(b, h):
                        pe.wait_ge(exp_a.sem, exp_a.at(b, h))
                        if h >= 2:
                            pe.wait_ge(pT_d.sem, pT_d.at(b, h - 2))
                        for c in range(KEYS // P):
                            last = M.transpose(ps[:, BANK_PT + h % 2, c * P:(c + 1) * P], p0[:, h % 2, c * P:(c + 1) * P], ident_s[:, :])
                        last.then_inc(pT_p.sem, 1)

                    def values(b, h):
                        r, j = h // HG, h % HG
                        o = ps[32 * r:32 * r + 32, BANK_O, :]
                        pe.wait_ge(pT_d.sem, pT_d.at(b, h))
                        cols = [vm[:, t, j, r, :, :].rearrange("p j d -> p (j d)") for t in range(TT)]
                        M.matmul(o[:, 0:T], cols[0], pT0[:, h % 2, 0:T], start=j == 0, stop=False)
                        M.matmul(o[:, P:T], cols[1], pT0[:, h % 2, T:KEYS], start=False, stop=j == HG - 1).then_inc(pv_p.sem, 1)

                    def transpose_xn(b, n):
                        pe.wait_ge(xn_d[n].sem, xn_d[n].at(b))
                        for t in range(TT):
                            last = M.transpose(ps[:, BANK_TV, t * P:(t + 1) * P], xn[:, t, :], ident_s[:, :])
                        last.then_inc(xnT_p[n].sem, 1)

                    def transpose_r(b):
                        pe.wait_ge(rexp_d.sem, rexp_d.at(b))
                        for t in range(TT):
                            last = M.transpose(ps[:, BANK_TV, COL_V + t * P:COL_V + (t + 1) * P], rexp[:, t, :, :].rearrange("p h d -> p (h d)"), ident_s[:, :])
                        last.then_inc(rT_p.sem, 1)

                    def project_y(b):
                        pe.wait_ge(oT_d.sem, oT_d.at(b))
                        for t in range(TT):
                            last = M.matmul(ps[:, BANK_TV, t * C:(t + 1) * C], oT0[:, t * P:(t + 1) * P], wp[:, :], start=True, stop=True)
                        last.then_inc(y_p.sem, 1)

                    def step(b, ends, leads):
                        pe.wait_ge(xnT_a.sem, xnT_a.at(b))
                        for k in range(2):
                            last = M.matmul(ps[:, BANK_QK, k * T:(k + 1) * T], wa[:, k * C:(k + 1) * C], xnT[:, :], start=True, stop=True)
                        last.then_inc(qk_p.sem, 1)
                        if ends:
                            transpose_r(b - 1)
                        pe.wait_ge(k_a.sem, k_a.at(b))
                        scores(b, 0)
                        scores(b, 1)
                        if ends:
                            pe.wait_ge(rT_a.sem, rT_a.at(b - 1))
                        for t in range(TT):
                            last = M.matmul(ps[:, BANK_TV, COL_V + t * C:COL_V + (t + 1) * C], xnT[:, t * P:(t + 1) * P], wa[:, 2 * C:3 * C], start=True, stop=True)
                        last.then_inc(v_p.sem, 1)
                        scores(b, 2)
                        pe.wait_ge(v_d.sem, v_d.at(b))
                        if ends:
                            project_y(b - 1)
                        transpose_p(b, 0)
                        for h in range(3, H0 + 3):
                            if h < H0:
                                scores(b, h)
                            if h < H0 + 2:
                                transpose_p(b, h - 2)
                            values(b, h - 3)
                            if ends and h == 8:
                                transpose_xn(b - 1, 1)
                            if leads and h == 13:
                                if ends:
                                    pe.wait_ge(x0_ready.sem, x0_ready.at(b - 1))
                                transpose_xn(b + 1, 0)

                    transpose_xn(0, 0)
                    sequences(pe, step)
                    transpose_r(B - 1)
                    project_y(B - 1)
                    transpose_xn(B - 1, 1)
                    pe.wait_ge(x0_ready.sem, B)

        raw = sb("raw", [P, 2, INNER])
        x1_again = raw[:, :, :].rearrange("p k (c n) -> p (k c) n", n=C)
        sq = sb("sq", [P, INNER])
        rot1 = sb("rot1", [P, 2, INNER])
        rot2 = sb("rot2", [P, 2, INNER])
        ssum = sb("ssum", [P, 2, H])
        rnorm = sb("rnorm", [P, 2, H])
        qT = sb("qT", [P, 2, PAIRS, T])
        vn = sb("vn", [P, TT, INNER])
        smax = sb("smax", [P, 2, H])
        prob = sb("prob", [P, 2, H * 2 * WIN])
        lsum = sb("lsum", [P, 2, H])
        linv = sb("linv", [P, 2, H])
        pT = sb("pT", [P, PAIRS, P])
        on = sb("on", [P, INNER])
        oT = sb("oT", [P, PAIRS, T])
        xc = sb("xc", [P, T])
        xq = sb("xq", [P, T])
        vtok = sb("vtok", [P, TT])
        rtok = sb("rtok", [P, TT])
        rwide = sb("rwide", [P, TT, P])
        xg = sb("xg", [P, T])
        gate = sb("gate", [P, T])
        hid = sb("hid", [P, 3, T])

        PJ, SO, TP, FB = 0, (2, 4), 6, 7

        xs_hi_d = signal("xs_hi_d")
        xs_d = signal("xs_d")
        raw_a = signal("raw_a", 4)
        sq_a = signal("sq_a", 4)
        ss_d = signal("ss_d", 4)
        cl_d = signal("cl_d", 4)
        rn_g = signal("rn_g", 4)
        nrm = [[signal(f"nrm{t}{kind}") for kind in range(2)] for t in range(TT)]
        cos_d = signal("cos_d", 4)
        sin_g = signal("sin_g", 4)
        rope_d = signal("rope_d", 4)
        qkT_p = signal("qkT_p", 8)
        qkT_a = signal("qkT_a", 8)
        vn_a = signal("vn_a", 2)
        VK_DMAS = (14, 16)
        vk_in = [signal(f"vk_in{t}", 16 * VK_DMAS[t]) for t in range(TT)]
        sc_p = signal("sc_p", 2)
        mx_d = signal("mx_d", 2)
        sub_d = signal("sub_d", 2)
        ex_a = signal("ex_a", 2)
        ls_d = signal("ls_d", 2)
        li_d = signal("li_d", 2)
        ptp = signal("ptp", 2)
        pta = signal("pta", 2)
        av_p = signal("av_p", 2, start=2)
        on_d = signal("on_d", 2)
        otp = signal("otp", 2)
        ota = signal("ota", 2)
        wo_p = signal("wo_p")
        x2_d = signal("x2_d")
        xf_d = signal("xf_d")
        cur_d = signal("cur_d")
        mean_p = signal("mean_p")
        xc_d = signal("xc_d")
        xq_a = signal("xq_a")
        var_p = signal("var_p")
        vr_d = signal("vr_d")
        rr_g = signal("rr_g")
        rx_d = signal("rx_d")
        rt_p = signal("rt_p")
        xg_d = signal("xg_d")
        xh_d = signal("xh_d")
        w1_p = signal("w1_p", 3)
        gelu_a = signal("gelu_a", 3)
        hid_d = signal("hid_d", 3)
        w2_p = signal("w2_p")
        fin_d = signal("fin_d")
        xl_p = signal("xl_p")
        x1_in = signal("x1_in")
        res_d = signal("res_d")
        out_done = signal("out_done", 16)

        def index(u):
            return u[0] * 2 + u[1]

        def live(u):
            n = index(u)
            return not isinstance(n, int) or 0 <= n < UNITS

        def pipeline(eng, step):
            for u in range(-1, LOOP_FROM):
                step((0, u - 1), (0, u), (0, u + 1))
            with eng.Fori(0, LOOP_STEPS // 2) as m:
                for u in range(LOOP_FROM, LOOP_FROM + 2):
                    step((m, u - 1), (m, u), (m, u + 1))
            for u in range(LOOP_FROM + LOOP_STEPS, UNITS + 1):
                step((0, u - 1), (0, u), (0, u + 1))

        def pipeline_by_layer(eng, step):
            for u in range(-1, LOOP_FROM):
                step((0, u - 1), (0, u), (0, u + 1))
            with eng.Fori(0, L - 1) as layer:
                with eng.Fori(0, (B - 4) // 2) as i:
                    m = layer * (B // 2) + i
                    for u in range(LOOP_FROM, LOOP_FROM + 2):
                        step((m, u - 1), (m, u), (m, u + 1))
                m = layer * (B // 2)
                for u in range(B - 2, B + LOOP_FROM):
                    step((m, u - 1), (m, u), (m, u + 1), layer + 1 if u == B - 2 else None)
            with eng.Fori(0, (B - 4) // 2) as m:
                for u in range(UNITS - B + LOOP_FROM, UNITS - B + LOOP_FROM + 2):
                    step((m, u - 1), (m, u), (m, u + 1))
            for u in range(LOOP_FROM + LOOP_STEPS, UNITS + 1):
                step((0, u - 1), (0, u), (0, u + 1))

        with nc.Block() as block:
            @block.sync
            def _(sp):
                def copy_v(n, t):
                    value = in_register(sp, vn_a.at(n, t))
                    sp.wait_ge(setup_done.sem, 1)
                    sp.wait_ge(av_p.sem, value)
                    sp.wait_ge(vn_a.sem, value)
                    for w in range(4 * t, 4 * t + 4):
                        for back in (1, 0):
                            if w - back < 0:
                                continue
                            tile, k = (w - back) // 4, (w - back) % 4
                            src = vn[32 * k:32 * k + 32, tile, :].rearrange("p (a s e) -> p a s e", a=PAIRS, s=2)
                            for hp in range(2):
                                lo = 64 * hp + 32 * (1 - back)
                                sp.dma_start(vk[lo:lo + 32, w, :, hp, :], src[:, :, hp, :]).then_inc(vk_in[t].sem, 16)

                def load_qkv(layer, kind):
                    split = in_register(sp, w_split_g[kind].at(layer - 1))
                    sp.wait_ge(setup_done.sem, 1)
                    sp.wait_ge(w_split_g[kind].sem, split)
                    src = wqkv[bass.ds(layer, 1), :, kind * INNER:(kind + 1) * INNER]
                    sp.dma_start(wqkv_s[:, kind * INNER:(kind + 1) * INNER], src.rearrange("o p n -> p (o n)")).then_inc(qkvw_in[kind].sem, 16)

                def load_wo(layer):
                    last = in_register(sp, wo_p.at(layer * B - 1))
                    sp.wait_ge(setup_done.sem, 1)
                    sp.wait_ge(wo_p.sem, last)
                    sp.dma_start(wo_s[:, :, :], wo[bass.ds(layer, 1), :, :, :].rearrange("o p k n -> p (o k) n")).then_inc(wo_in.sem, 16)

                def load_w1(layer):
                    last = in_register(sp, w1_p.at(layer * B - 1, 2))
                    sp.wait_ge(setup_done.sem, 1)
                    sp.wait_ge(w1_p.sem, last)
                    sp.dma_start(w1_s[:, :], w1[bass.ds(layer, 1), :, :].rearrange("o p n -> p (o n)")).then_inc(w1_in.sem, 16)

                def load_w2(layer):
                    last = in_register(sp, w2_p.at(layer * B - 1))
                    sp.wait_ge(setup_done.sem, 1)
                    sp.wait_ge(w2_p.sem, last)
                    sp.dma_start(w2_s[:, :, :], w2[bass.ds(layer, 1), :, :, :].rearrange("o p k n -> p (o k) n")).then_inc(w2_in.sem, 16)

                sp.wait_ge(zeroed.sem, 1)
                for n in range(2):
                    for t in range(TT):
                        copy_v(n, t)
                with sp.Fori(0, L - 1) as layer:
                    for kind in range(3):
                        load_qkv(layer + 1, kind)
                    with sp.Fori(2, B + 1) as i:
                        for t in range(TT):
                            copy_v(layer * B + i, t)
                    load_wo(layer + 1)
                    copy_v(layer * B + (B + 1), 0)
                    load_w1(layer + 1)
                    copy_v(layer * B + (B + 1), 1)
                    load_w2(layer + 1)
                with sp.Fori(2, B) as i:
                    for t in range(TT):
                        copy_v(i + (L - 1) * B, t)
                sp.wait_ge(cos_d.sem, cos_d.at(UNITS - 1, 3))
                sp.wait_ge(sin_g.sem, sin_g.at(UNITS - 1, 3))
                sp.wait_ge(spilled.sem, 16 * B)
                sp.dma_start(x1_again, out.rearrange("b (t p) c -> p (b t) c", p=P)).then_inc(x1_in.sem, 16)
                sp.wait_ge(x1_in.sem, 16)
                for b in range(B):
                    sp.wait_ge(res_d.sem, res_d.at(b))
                    sp.dma_start(out[b, :, :].rearrange("(t p) c -> p t c", p=P), x1_again[:, b * TT:(b + 1) * TT, :]).then_inc(out_done.sem, 16)
                sp.wait_ge(out_done.sem, 16 * B)

            @block.gpsimd
            def _(pool):
                G = nc.gpsimd
                pool.wait_ge(x0_ready.sem, B)
                pool.wait_ge(spilled.sem, 16 * B)
                pool.wait_ge(tables_ready.sem, 1)

                def norms(u, t, kind):
                    if not live(u):
                        return
                    n, i = index(u), 2 * t + kind
                    pool.wait_ge(cl_d.sem, cl_d.at(n, i))
                    G.tensor_tensor(rnorm[:, kind, :], ssum[:, kind, :], minus_half[:, :], ALU.pow).then_inc(rn_g.sem, 1)

                def feed_rstd(u):
                    if not live(u):
                        return
                    n = index(u)
                    pool.wait_ge(vr_d.sem, vr_d.at(n))
                    G.tensor_tensor(rtok[:, :], vtok[:, :], minus_half[:, 0:TT], ALU.pow).then_inc(rr_g.sem, 1)

                def normalise(u, t, kind):
                    if not live(u):
                        return
                    n, i = index(u), 2 * t + kind
                    pool.wait_ge(rn_g.sem, rn_g.at(n, i))
                    v = raw[:, kind, :].rearrange("p (h e) -> p h e", h=H)
                    G.tensor_tensor(v, v, rnorm[:, kind, :, None].broadcast_to([P, H, D]), ALU.mult).then_inc(nrm[t][kind].sem, 1)

                def sin_term(u, t, kind):
                    if not live(u):
                        return
                    n = index(u)
                    i = 2 * t + kind
                    pool.wait_ge(nrm[t][kind].sem, nrm[t][kind].at(n))
                    if t > 0 or not (isinstance(n, int) and n < 1):
                        pool.wait_ge(rope_d.sem, rope_d.before(n, i - 1))
                    base = (n // B) * (4 * TT * D) + (2 * kind + 1) * TT * D + t * D
                    tab = rope_l[:, bass.ds(base, D)].rearrange("p (s e) -> p s e", s=2)
                    src = raw[:, kind, :].rearrange("p (h s e) -> p h s e", h=H, s=2)
                    dst = rot2[:, kind, :].rearrange("p (h s e) -> p h s e", h=H, s=2)
                    for half in range(2):
                        last = G.tensor_tensor(dst[:, :, half, :], src[:, :, 1 - half, :],
                                               tab[:, half, None, :].broadcast_to([P, H, D // 2]), ALU.mult)
                    last.then_inc(sin_g.sem, 1)

                def step(before, u, after, renew=None):
                    normalise(u, 1, 1)
                    sin_term(u, 1, 1)
                    norms(after, 0, 0)
                    normalise(after, 0, 0)
                    feed_rstd(before)
                    sin_term(after, 0, 0)
                    norms(after, 0, 1)
                    normalise(after, 0, 1)
                    sin_term(after, 0, 1)
                    norms(after, 1, 0)
                    if renew is not None:
                        weights_lo(pool, nc.gpsimd, renew, 0)
                    normalise(after, 1, 0)
                    sin_term(after, 1, 0)
                    norms(after, 1, 1)

                pipeline_by_layer(pool, step)

            @block.vector
            def _(dve):
                V = nc.vector
                dve.wait_ge(x0_ready.sem, B)
                dve.wait_ge(spilled.sem, 16 * B)
                dve.wait_ge(zeroed.sem, 1)
                dve.wait_ge(tables_ready.sem, 1)
                dve.sem_inc(fin_d.sem, 1)

                def seq(u):
                    return bass.ds((index(u) % B) * T, T)

                def shift_in(u):
                    if not live(u):
                        return
                    n, par = index(u), u[1] % 2
                    if not (isinstance(n, int) and n < 2):
                        dve.wait_ge(fin_d.sem, n - 1)
                        value = in_register(dve, proj_p.before(n - 1, 0))
                        dve.wait_ge(setup_done.sem, 1)
                        dve.wait_ge(proj_p.sem, value)
                    b = index(u) % B
                    V.tensor_copy(xs_hi[0:64, par, :], xT[0:64, bass.ds(b * T, T)])
                    V.tensor_copy(xs_hi[64:P, par, 1:T], xT[64:P, bass.ds(b * T, T - 1)]).then_inc(xs_hi_d.sem, 1)
                    dve.wait_ge(xs_hi_d.sem, xs_hi_d.at(n))
                    V.tensor_tensor(xs_lo[0:64, par, :], xT[0:64, bass.ds(b * T, T)], xs_hi[0:64, par, :], ALU.subtract)
                    V.tensor_tensor(xs_lo[64:P, par, 1:T], xT[64:P, bass.ds(b * T, T - 1)], xs_hi[64:P, par, 1:T],
                                    ALU.subtract).then_inc(xs_d.sem, 1)

                def sums(u, t, kind):
                    if not live(u):
                        return
                    n, i = index(u), 2 * t + kind
                    dve.wait_ge(sq_a.sem, sq_a.at(n, i))
                    V.tensor_reduce(ssum[:, kind, :], sq[:, :].rearrange("p (h e) -> p h e", h=H), AX_X, ALU.add).then_inc(ss_d.sem, 1)
                    dve.wait_ge(ss_d.sem, ss_d.at(n, i))
                    V.tensor_scalar(ssum[:, kind, :], ssum[:, kind, :], 1e-24, None, ALU.max).then_inc(cl_d.sem, 1)

                def cos_term(u, t, kind):
                    if not live(u):
                        return
                    n, i = index(u), 2 * t + kind
                    dve.wait_ge(nrm[t][kind].sem, nrm[t][kind].at(n))
                    if t > 0 or not (isinstance(n, int) and n < 1):
                        dve.wait_ge(qkT_p.sem, qkT_p.before(n, 4 * t + 2 * kind - 2))
                    base = (n // B) * (4 * TT * D) + 2 * kind * TT * D + t * D
                    tab = rope_l[:, bass.ds(base, D)]
                    V.tensor_tensor(rot1[:, kind, :].rearrange("p (h e) -> p h e", h=H),
                                    raw[:, kind, :].rearrange("p (h e) -> p h e", h=H),
                                    tab[:, None, :].broadcast_to([P, H, D]), ALU.mult).then_inc(cos_d.sem, 1)

                def rotate(u, t, kind):
                    if not live(u):
                        return
                    n, i = index(u), 2 * t + kind
                    dve.wait_ge(cos_d.sem, cos_d.at(n, i))
                    dve.wait_ge(sin_g.sem, sin_g.at(n, i))
                    V.tensor_tensor(rot1[:, kind, :], rot1[:, kind, :], rot2[:, kind, :], ALU.add).then_inc(rope_d.sem, 1)

                def tile_scores(t):
                    return ps[:, SO[t]:SO[t] + 2, :].rearrange("p b (h k) -> p (b h) k", k=64)

                def soft_max(u, t):
                    if not live(u):
                        return
                    n = index(u)
                    dve.wait_ge(sc_p.sem, sc_p.at(n, t))
                    V.tensor_reduce(smax[:, t, :], tile_scores(t), AX_X, ALU.max).then_inc(mx_d.sem, 1)
                    dve.wait_ge(mx_d.sem, mx_d.at(n, t))
                    if not (isinstance(n, int) and n < 1):
                        dve.wait_ge(ptp.sem, ptp.at(n - 1, t))
                    V.tensor_tensor(prob[:, t, :].rearrange("p (h k) -> p h k", h=H), tile_scores(t),
                                    smax[:, t, :, None].broadcast_to([P, H, 2 * WIN]), ALU.subtract).then_inc(sub_d.sem, 1)

                def soft_sum(u, t):
                    if not live(u):
                        return
                    n = index(u)
                    dve.wait_ge(ex_a.sem, ex_a.at(n, t))
                    V.tensor_reduce(lsum[:, t, :], prob[:, t, :].rearrange("p (h k) -> p h k", h=H), AX_X, ALU.add).then_inc(ls_d.sem, 1)
                    dve.wait_ge(ls_d.sem, ls_d.at(n, t))
                    V.reciprocal(linv[:, t, :], lsum[:, t, :]).then_inc(li_d.sem, 1)

                def normalise_o(u, t):
                    if not live(u):
                        return
                    n = index(u)
                    dve.wait_ge(li_d.sem, li_d.at(n, t))
                    dve.wait_ge(av_p.sem, av_p.at(n, t))
                    if t > 0 or not (isinstance(n, int) and n < 1):
                        dve.wait_ge(otp.sem, otp.before(n, t))
                    V.tensor_tensor(on[:, :].rearrange("p (h e) -> p h e", h=H), tile_scores(t),
                                    linv[:, t, :, None].broadcast_to([P, H, D]), ALU.mult).then_inc(on_d.sem, 1)

                def feed_1(u):
                    if not live(u):
                        return
                    n = index(u)
                    layer = n // B
                    dve.wait_ge(wo_p.sem, wo_p.at(n))
                    V.tensor_tensor(xT[:, seq(u)], ps[:, FB, 0:T], xT[:, seq(u)], ALU.add).then_inc(x2_d.sem, 1)
                    value = in_register(dve, x2_d.at(n))
                    dve.wait_ge(setup_done.sem, 1)
                    dve.wait_ge(x2_d.sem, value)
                    b = n % B
                    V.tensor_copy(xf[0:64, :], xT[0:64, bass.ds(b * T, T)])
                    V.tensor_copy(xf[64:P, 1:T], xT[64:P, bass.ds(b * T, T - 1)]).then_inc(xf_d.sem, 1)
                    V.tensor_copy(cur[:, 0, 0:2], ln_s[:, :, bass.ds(layer, 1)].rearrange("p a o -> p (a o)"))
                    V.tensor_copy(cur[:, 0, 2:8], b1_s[:, bass.ds(layer * 6, 6)])
                    V.tensor_copy(cur[:, 0, 8:9], b2_s[:, bass.ds(layer, 1)]).then_inc(cur_d.sem, 1)

                def feed_2(u):
                    if not live(u):
                        return
                    n = index(u)
                    dve.wait_ge(mean_p.sem, mean_p.at(n))
                    V.tensor_tensor(xc[:, :], xf[:, :], ps[:, FB, 0:T], ALU.subtract).then_inc(xc_d.sem, 1)

                def feed_3(u):
                    if not live(u):
                        return
                    n = index(u)
                    dve.wait_ge(var_p.sem, var_p.at(n))
                    V.tensor_scalar(vtok[:, :], ps[:, FB, T:T + TT], LN_EPS, None, ALU.add).then_inc(vr_d.sem, 1)

                def feed_spread(u):
                    if not live(u):
                        return
                    n = index(u)
                    dve.wait_ge(rr_g.sem, rr_g.at(n))
                    V.tensor_copy(rwide[:, :, :], rtok[:, :, None].broadcast_to([P, TT, P])).then_inc(rx_d.sem, 1)

                def feed_norm(u):
                    if not live(u):
                        return
                    n = index(u)
                    dve.wait_ge(rt_p.sem, rt_p.at(n))
                    V.tensor_tensor(xg[:, :], xc[:, :], ps[:, FB, 0:T], ALU.mult).then_inc(xg_d.sem, 1)
                    dve.wait_ge(xg_d.sem, xg_d.at(n))
                    V.tensor_scalar(xg[:, :], xg[:, :], cur[:, 0, 0:1], cur[:, 0, 1:2], ALU.mult, ALU.add).then_inc(xh_d.sem, 1)

                def feed_hidden(u, i):
                    if not live(u):
                        return
                    n, rows = index(u), PIECES[i][1]
                    dve.wait_ge(gelu_a.sem, gelu_a.at(n, i))
                    V.scalar_tensor_tensor(hid[0:rows, i, :], ps[0:rows, FB, 0:T], cur[0:rows, 0, 2 + i:3 + i],
                                           gate[0:rows, :], ALU.add, ALU.mult).then_inc(hid_d.sem, 1)

                def feed_4(u):
                    if not live(u):
                        return
                    n = index(u)
                    dve.wait_ge(w2_p.sem, w2_p.at(n))
                    V.scalar_tensor_tensor(xT[:, seq(u)], ps[:, FB, 0:T], cur[:, 0, 8:9], xT[:, seq(u)],
                                           ALU.add, ALU.add).then_inc(fin_d.sem, 1)

                def step(before, u, after, renew=None):
                    shift_in(after)
                    rotate(u, 1, 0)
                    soft_max(u, 0)
                    cos_term(u, 1, 1)
                    rotate(u, 1, 1)
                    sums(after, 0, 0)
                    feed_1(before)
                    feed_2(before)
                    soft_sum(u, 0)
                    feed_3(before)
                    sums(after, 0, 1)
                    feed_spread(before)
                    cos_term(after, 0, 0)
                    feed_norm(before)
                    soft_max(u, 1)
                    rotate(after, 0, 0)
                    normalise_o(u, 0)
                    sums(after, 1, 0)
                    feed_hidden(before, 0)
                    cos_term(after, 0, 1)
                    rotate(after, 0, 1)
                    feed_hidden(before, 1)
                    soft_sum(u, 1)
                    normalise_o(u, 1)
                    feed_hidden(before, 2)
                    sums(after, 1, 1)
                    if renew is not None:
                        weights_lo(dve, V, renew, 1)
                    cos_term(after, 1, 0)
                    feed_4(before)
                    if renew is not None:
                        weights_lo(dve, V, renew, 2)

                pipeline_by_layer(dve, step)

                dve.wait_ge(x1_in.sem, 16)
                for b in range(B):
                    dve.wait_ge(xl_p.sem, xl_p.at(b))
                    xb = x1_again[:, b * TT:(b + 1) * TT, :]
                    V.tensor_tensor(xb, ps[:, PJ + b % 2, 0:T].rearrange("p (t c) -> p t c", t=TT), xb, ALU.add).then_inc(res_d.sem, 1)

            @block.scalar
            def _(act):
                S = nc.scalar
                act.wait_ge(x0_ready.sem, B)
                act.wait_ge(spilled.sem, 16 * B)
                act.wait_ge(zeroed.sem, 1)

                def copy_raw(u, t, kind):
                    if not live(u):
                        return
                    n, i = index(u), 2 * t + kind
                    act.wait_ge(proj_p.sem, proj_p.at(n, 3 * t + kind))
                    if t > 0 or not (isinstance(n, int) and n < 1):
                        act.wait_ge(cos_d.sem, cos_d.before(n, i - 1))
                        act.wait_ge(sin_g.sem, sin_g.before(n, i - 1))
                    S.activation(raw[:, kind, :], ps[:, PJ:PJ + 2, :].rearrange("p a n -> p (a n)"), ACT.Copy).then_inc(raw_a.sem, 1)

                def square(u, t, kind):
                    if not live(u):
                        return
                    n, i = index(u), 2 * t + kind
                    act.wait_ge(raw_a.sem, raw_a.at(n, i))
                    if i > 0 or not (isinstance(n, int) and n < 1):
                        act.wait_ge(ss_d.sem, ss_d.before(n, i))
                    S.activation(sq[:, :], raw[:, kind, :], ACT.Square).then_inc(sq_a.sem, 1)

                def copy_v(u, t):
                    if not live(u):
                        return
                    n, par = index(u), u[1] % 2
                    act.wait_ge(proj_p.sem, proj_p.at(n, 3 * t + 2))
                    if not (isinstance(n, int) and n < 1):
                        act.wait_ge(vk_in[1].sem, vk_in[1].at(n - 1, vk_in[1].per - 1))
                    S.activation(vn[:, t, :], ps[:, PJ:PJ + 2, :].rearrange("p a n -> p (a n)"), ACT.Copy).then_inc(vn_a.sem, 1)

                def copy_qkT(u, t, kind, half):
                    if not live(u):
                        return
                    n, par = index(u), u[1] % 2
                    i = 4 * t + 2 * kind + half
                    act.wait_ge(qkT_p.sem, qkT_p.at(n, i))
                    src = ps[:, TP, :].rearrange("p (a n) -> p a n", a=4)
                    pairs = slice(4 * half, 4 * half + 4)
                    if kind == 0:
                        last = S.activation(qT[:, par, pairs, t * P:(t + 1) * P], src, ACT.Copy)
                    else:
                        if not (isinstance(n, int) and n < 1):
                            act.wait_ge(sc_p.sem, sc_p.at(n - 1, 1))
                        for hp in range(2):
                            rows = slice(64 * hp, 64 * hp + 64)
                            last = S.activation(kT[rows, hp, pairs, WIN + t * P:WIN + (t + 1) * P], src[rows], ACT.Copy)
                    last.then_inc(qkT_a.sem, 1)

                def exps(u, t):
                    if not live(u):
                        return
                    n = index(u)
                    act.wait_ge(sub_d.sem, sub_d.at(n, t))
                    S.activation(prob[:, t, :], prob[:, t, :], ACT.Exp, scale=QK_SCALE).then_inc(ex_a.sem, 1)

                def copy_pT(u, t):
                    if not live(u):
                        return
                    n = index(u)
                    act.wait_ge(ptp.sem, ptp.at(n, t))
                    if t > 0 or not (isinstance(n, int) and n < 1):
                        act.wait_ge(av_p.sem, av_p.before(n, t))
                    S.activation(pT[:, :, :].rearrange("p a q -> p (a q)"), ps[:, SO[t]:SO[t] + 2, :].rearrange("p a n -> p (a n)"),
                                 ACT.Copy).then_inc(pta.sem, 1)

                def copy_oT(u, t):
                    if not live(u):
                        return
                    n = index(u)
                    act.wait_ge(otp.sem, otp.at(n, t))
                    if t == 0 and not (isinstance(n, int) and n < 1):
                        act.wait_ge(wo_p.sem, wo_p.at(n - 1))
                    S.activation(oT[:, :, t * P:(t + 1) * P], ps[:, SO[t]:SO[t] + 2, :].rearrange("p s (a q) -> p (s a) q", a=4),
                                 ACT.Copy).then_inc(ota.sem, 1)

                def square_x(u):
                    if not live(u):
                        return
                    n = index(u)
                    act.wait_ge(xc_d.sem, xc_d.at(n))
                    S.activation(xq[:, :], xc[:, :], ACT.Square).then_inc(xq_a.sem, 1)

                def gelu(u, i):
                    if not live(u):
                        return
                    n, rows = index(u), PIECES[i][1]
                    act.wait_ge(w1_p.sem, w1_p.at(n, i))
                    if i > 0:
                        act.wait_ge(hid_d.sem, hid_d.at(n, i - 1))
                    S.activation(gate[0:rows, :], ps[0:rows, FB, T:2 * T], ACT.Gelu, bias=cur[0:rows, 0, 5 + i:6 + i]).then_inc(gelu_a.sem, 1)

                def step(before, u, after, renew=None):
                    copy_qkT(u, 1, 0, 0)
                    copy_oT(before, 1)
                    copy_raw(after, 0, 0)
                    copy_qkT(u, 1, 0, 1)
                    square(after, 0, 0)
                    exps(u, 0)
                    copy_qkT(u, 1, 1, 0)
                    copy_raw(after, 0, 1)
                    copy_qkT(u, 1, 1, 1)
                    square_x(before)
                    square(after, 0, 1)
                    copy_v(after, 0)
                    copy_pT(u, 0)
                    copy_raw(after, 1, 0)
                    if renew is not None:
                        weights_hi(act, renew, 0)
                    square(after, 1, 0)
                    exps(u, 1)
                    gelu(before, 0)
                    copy_qkT(after, 0, 0, 0)
                    copy_pT(u, 1)
                    copy_qkT(after, 0, 0, 1)
                    gelu(before, 1)
                    copy_raw(after, 1, 1)
                    if renew is not None:
                        weights_hi(act, renew, 1)
                    square(after, 1, 1)
                    gelu(before, 2)
                    copy_qkT(after, 0, 1, 0)
                    copy_oT(u, 0)
                    copy_qkT(after, 0, 1, 1)
                    copy_v(after, 1)
                    if renew is not None:
                        weights_hi(act, renew, 2)

                pipeline_by_layer(act, step)

            @block.tensor
            def _(pe):
                M = nc.tensor
                pe.wait_ge(x0_ready.sem, B)
                pe.wait_ge(zeroed.sem, 1)
                pe.wait_ge(tables_ready.sem, 1)
                pe.sem_inc(av_p.sem, av_p.start)

                def proj(u, t, kind):
                    if not live(u):
                        return
                    n, par = index(u), u[1] % 2
                    i = 3 * t + kind
                    if i == 0:
                        pe.wait_ge(xs_d.sem, xs_d.at(n))
                    if t == 0:
                        pe.wait_ge(w_split_g[kind].sem, n // B + 1)
                    if kind > 0:
                        pe.wait_ge(raw_a.sem, raw_a.at(n, 2 * t + kind - 1))
                    elif t > 0 or not (isinstance(n, int) and n < 1):
                        pe.wait_ge(vn_a.sem, vn_a.before(n, t))
                    x_hi, x_lo = (v[:, par, t * P:(t + 1) * P] for v in (xs_hi, xs_lo))
                    for half in range(2):
                        cols = slice(kind * INNER + half * 512, kind * INNER + (half + 1) * 512)
                        M.matmul(ps[:, PJ + half, :], x_hi, wqkv_hi[:, cols], start=True, stop=False)
                        M.matmul(ps[:, PJ + half, :], x_hi, wqkv_lo[:, cols], start=False, stop=False)
                        last = M.matmul(ps[:, PJ + half, :], x_lo, wqkv_hi[:, cols], start=False, stop=True)
                    last.then_inc(proj_p.sem, 1)

                def transpose_qk(u, t, kind, half):
                    if not live(u):
                        return
                    n = index(u)
                    i = 4 * t + 2 * kind + half
                    pe.wait_ge(rope_d.sem, rope_d.at(n, 2 * t + kind))
                    pe.wait_ge(qkT_a.sem, qkT_a.before(n, i))
                    for a in range(4):
                        c = 4 * half + a
                        last = M.transpose(ps[:, TP, a * P:(a + 1) * P], rot1[:, kind, c * P:(c + 1) * P], ident_s[:, :])
                    last.then_inc(qkT_p.sem, 1)

                def scores(u, t):
                    if not live(u):
                        return
                    n, par = index(u), u[1] % 2
                    pe.wait_ge(qkT_a.sem, qkT_a.at(n, 4 * t + 3))
                    if not (isinstance(n, int) and n < 1):
                        pe.wait_ge(ota.sem, ota.at(n - 1, t))
                    mask = wmask[:, 0 if t == 0 else 1, :, :].rearrange("p a k -> p (a k)")
                    for hp in range(2):
                        M.matmul(ps[:, SO[t] + hp, :], ident_b[:, :], mask, start=True, stop=False)
                    for a in range(PAIRS):
                        for k in range(4):
                            w = 4 * t + k
                            out_s = ps[32 * k:32 * k + 32, SO[t] + a // 4, (a % 4) * P:(a % 4 + 1) * P]
                            last = M.matmul(out_s, qT[:, par, a, 32 * w:32 * w + 32], kT[:, :, a, 32 * w:32 * w + 64],
                                            start=False, stop=a % 4 == 3)
                    last.then_inc(sc_p.sem, 1)

                def transpose_p(u, t):
                    if not live(u):
                        return
                    n = index(u)
                    pe.wait_ge(vk_in[t].sem, vk_in[t].at(n, vk_in[t].per - 1))
                    pe.wait_ge(ex_a.sem, ex_a.at(n, t))
                    for a in range(PAIRS):
                        last = M.transpose(ps[:, SO[t] + a // 4, (a % 4) * P:(a % 4 + 1) * P], prob[:, t, a * P:(a + 1) * P], ident_s[:, :])
                    last.then_inc(ptp.sem, 1)

                def values(u, t):
                    if not live(u):
                        return
                    n, par = index(u), u[1] % 2
                    pe.wait_ge(pta.sem, pta.at(n, t))
                    for a in range(PAIRS):
                        for k in range(4):
                            last = M.matmul(ps[32 * k:32 * k + 32, SO[t] + a // 4, (a % 4) * P:(a % 4 + 1) * P],
                                            pT[:, a, 32 * k:32 * k + 32], vk[:, 4 * t + k, a, :, :], start=True, stop=True)
                    last.then_inc(av_p.sem, 1)

                def transpose_o(u, t):
                    if not live(u):
                        return
                    n = index(u)
                    pe.wait_ge(on_d.sem, on_d.at(n, t))
                    for a in range(PAIRS):
                        last = M.transpose(ps[:, SO[t] + a // 4, (a % 4) * P:(a % 4 + 1) * P], on[:, a * P:(a + 1) * P], ident_s[:, :])
                    last.then_inc(otp.sem, 1)

                def feed_wo(u):
                    if not live(u):
                        return
                    n = index(u)
                    pe.wait_ge(wo_in.sem, 16 * (n // B) + 16)
                    pe.wait_ge(ota.sem, ota.at(n, 1))
                    pe.wait_ge(fin_d.sem, fin_d.at(n))
                    for a in range(PAIRS):
                        last = M.matmul(ps[:, FB, 0:T], wo_s[:, a, :], oT[:, a, :], start=a == 0, stop=a == PAIRS - 1)
                    last.then_inc(wo_p.sem, 1)

                def feed_mean(u):
                    if not live(u):
                        return
                    n = index(u)
                    pe.wait_ge(xf_d.sem, xf_d.at(n))
                    M.matmul(ps[:, FB, 0:T], mean_w[:, :], xf[:, :], start=True, stop=True).then_inc(mean_p.sem, 1)

                def feed_var(u):
                    if not live(u):
                        return
                    n = index(u)
                    pe.wait_ge(xq_a.sem, xq_a.at(n))
                    for t in range(TT):
                        last = M.matmul(ps[:, FB, T + t:T + t + 1], xq[:, t * P:(t + 1) * P], mean_w[:, 0:1], start=True, stop=True)
                    last.then_inc(var_p.sem, 1)

                def feed_rstd(u):
                    if not live(u):
                        return
                    n = index(u)
                    pe.wait_ge(rx_d.sem, rx_d.at(n))
                    for t in range(TT):
                        last = M.transpose(ps[:, FB, t * P:(t + 1) * P], rwide[:, t, :], ident_s[:, :])
                    last.then_inc(rt_p.sem, 1)

                def feed_w1(u, i):
                    if not live(u):
                        return
                    n = index(u)
                    at, rows = PIECES[i]
                    if i == 0:
                        pe.wait_ge(w1_in.sem, 16 * (n // B) + 16)
                        pe.wait_ge(xh_d.sem, xh_d.at(n))
                    else:
                        pe.wait_ge(hid_d.sem, hid_d.at(n, i - 1))
                    for g in range(2):
                        last = M.matmul(ps[0:rows, FB, g * T:(g + 1) * T], w1_s[:, g * DI + at:g * DI + at + rows], xg[:, :],
                                        start=True, stop=True)
                    last.then_inc(w1_p.sem, 1)

                def feed_w2(u):
                    if not live(u):
                        return
                    n = index(u)
                    pe.wait_ge(w2_in.sem, 16 * (n // B) + 16)
                    pe.wait_ge(hid_d.sem, hid_d.at(n, 2))
                    for i, (_, rows) in enumerate(PIECES):
                        last = M.matmul(ps[:, FB, 0:T], w2_s[0:rows, i, :], hid[0:rows, i, :], start=i == 0, stop=i == 2)
                    last.then_inc(w2_p.sem, 1)

                def step(before, u, after):
                    transpose_o(before, 1)
                    transpose_qk(u, 1, 0, 0)
                    proj(after, 0, 0)
                    transpose_qk(u, 1, 0, 1)
                    feed_wo(before)
                    transpose_qk(u, 1, 1, 0)
                    proj(after, 0, 1)
                    transpose_p(u, 0)
                    transpose_qk(u, 1, 1, 1)
                    feed_mean(before)
                    proj(after, 0, 2)
                    feed_var(before)
                    scores(u, 1)
                    feed_rstd(before)
                    proj(after, 1, 0)
                    values(u, 0)
                    feed_w1(before, 0)
                    proj(after, 1, 1)
                    transpose_qk(after, 0, 0, 0)
                    transpose_o(u, 0)
                    transpose_p(u, 1)
                    transpose_qk(after, 0, 0, 1)
                    feed_w1(before, 1)
                    values(u, 1)
                    feed_w1(before, 2)
                    transpose_qk(after, 0, 1, 0)
                    proj(after, 1, 2)
                    transpose_qk(after, 0, 1, 1)
                    feed_w2(before)
                    scores(after, 0)

                pipeline(pe, step)

                for b in range(B):
                    pe.wait_ge(fin_d.sem, fin_d.at(UNITS - B + b) + 1)
                    if b >= 2:
                        pe.wait_ge(res_d.sem, res_d.at(b - 2))
                    for t in range(TT):
                        last = M.transpose(ps[:, PJ + b % 2, t * P:(t + 1) * P], xT[:, b * T + t * P:b * T + (t + 1) * P], ident_s[:, :])
                    last.then_inc(xl_p.sem, 1)


def _constants():
    import numpy as np

    f = np.float32
    half = np.arange(0, D, 2, dtype=f)
    inv_freq = f(1.0) / f(10000.0) ** (half / f(D))
    pos = np.arange(T, dtype=f)
    freqs = pos[:, None] * inv_freq[None, :]
    freqs = np.concatenate([freqs, freqs], -1)
    base = (half + f(0.4 * D)) / f(1.4 * D)
    power = (pos - T // 2) / f(WIN // 2)
    scale = base[None, :] ** power[:, None]
    scale = np.concatenate([scale, scale], -1).astype(f)
    cos, sin = np.cos(freqs).astype(f), np.sin(freqs).astype(f)
    sign = np.concatenate([-np.ones(D // 2, f), np.ones(D // 2, f)])
    inv = (f(1.0) / scale).astype(f)
    rope = np.stack([cos * scale, sin * scale * sign, cos * inv, sin * inv * sign]).astype(f)
    rope = rope.reshape(4, TT, P, D).transpose(2, 0, 1, 3)

    i = np.arange(P)[:, None] % WIN
    j = np.arange(2 * WIN)[None, :]
    seen = (j >= i) & (j <= i + WIN)
    first = seen & ((np.arange(P)[:, None] >= WIN) | (j >= WIN))
    win_mask = np.where(np.stack([first, seen], 1), f(0), f(NEG)).astype(f)

    q = np.arange(P)[:, None]
    k = np.arange(P)[None, :]
    causal = np.where(k <= q, f(0), f(NEG)).astype(f)

    def bf16_part(a):
        bits = np.ascontiguousarray(a, f).view(np.uint32) & np.uint32(0xFFFF0000)
        return bits.view(f)

    slopes = (f(2.0) ** (-f(8.0 / H0) * np.arange(1, H0 + 1, dtype=f))).astype(f)
    keys = np.concatenate([np.arange(P), np.arange(T)]).astype(f)
    bias = (slopes[:, None] * keys[None, :]).astype(f)
    parts = []
    for _ in range(3):
        part = bf16_part(bias)
        parts.append(part)
        bias = bias - part
    alibi = np.zeros((P, HG, KEYS), f)
    ones3 = np.zeros((P, HG, P), f)
    pick = np.zeros((P, H0), f)
    for h in range(H0):
        for n in range(3):
            alibi[32 * (h // HG) + n, h % HG] = parts[n][h]
            ones3[32 * (h // HG) + n, h // HG] = 1
        pick[h * D0:(h + 1) * D0, h] = f(1.0) / np.sqrt(f(D0))
    return {"rope": rope, "ident": np.eye(P, dtype=f), "win_mask": win_mask, "causal": causal,
            "alibi": alibi, "ones3": ones3, "head_pick": pick}


def kernel(**inputs):
    import numpy as np
    import concourse.bacc as bacc
    from concourse.bass_utils import run_bass_kernel_spmd

    a = {k: np.asarray(v) for k, v in inputs.items()}

    def rows(v, n=P):
        return np.ascontiguousarray(np.broadcast_to(v, (n,) + v.shape))

    b1 = np.zeros((L, 6, P), np.float32)
    w2 = np.zeros((L, 3, P, C), np.float32)
    for i, (at, n) in enumerate(PIECES):
        w2[:, i, :n] = a["L0_ffn_W2"][:, at:at + n]
        for g in range(2):
            b1[:, 3 * g + i, :n] = a["L0_ffn_b1"][:, g * DI + at:g * DI + at + n]
    arrays = {
        "x": a["L0_attn_x"],
        "w_attn": a["L0_attn_w_attn"],
        "b_attn_cols": a["L0_attn_b_attn"][:2 * C].reshape(2, C).T,
        "b_v_rows": rows(a["L0_attn_b_attn"][2 * C:]),
        "w_proj": a["L0_attn_w_proj"],
        "b_proj_rows": rows(a["L0_attn_b_proj"]),
        "wqkv": a["L0_ffn_Wqkv"],
        "q_scale_rows": rows(a["L0_ffn_q_scale"]),
        "k_scale_rows": rows(a["L0_ffn_k_scale"]),
        "wo": a["L0_ffn_Wo"].reshape(L, PAIRS, P, C).transpose(0, 2, 1, 3),
        "ln_cols": np.stack([a["L0_ffn_ln_g"].T, a["L0_ffn_ln_b"].T], 1),
        "w1": a["L0_ffn_W1"],
        "b1_cols": b1.transpose(2, 0, 1).reshape(P, L * 6),
        "w2": w2.transpose(0, 2, 1, 3),
        "b2_cols": a["L0_ffn_b2"].T,
        **_constants(),
    }
    nc = bacc.Bacc("TRN2", target_bir_lowering=False, num_devices=1)
    feeds, args = {}, {}
    for name, v in arrays.items():
        v = np.ascontiguousarray(v)
        feeds[name + "_dram"] = v
        args[name] = nc.dram_tensor(name + "_dram", v.shape, mybir.dt.from_np(v.dtype), kind="ExternalInput").ap()
    out = nc.dram_tensor("out_dram", (B, T, C), F32, kind="ExternalOutput").ap()
    build(nc, out=out, **args)
    r = run_bass_kernel_spmd(nc, [feeds], core_ids=[0])
    return r.results[0]["out_dram"]
```
